# Optimizing a Trainium2 kernel written in Bass

```python
import numpy as np
import jax
import jax.numpy as jnp

def _softmax(x, axis=-1):
    return jax.nn.softmax(x, axis=axis)

def _gelu(x):
    return jax.nn.gelu(x, approximate=True)

def _silu(x):
    return jax.nn.silu(x)

def _sigmoid(x):
    return jax.nn.sigmoid(x)

def _layernorm(x, axis=-1, eps=1e-05):
    m = jnp.mean(x, axis=axis, keepdims=True)
    v = jnp.var(x, axis=axis, keepdims=True)
    return (x - m) / jnp.sqrt(v + eps)

def _scatter_add(tgt, idx, src, axis=0):
    return tgt.at[idx].add(src)

def _segment_sum(src, seg, n):
    return jax.ops.segment_sum(src, seg, n)
kernel_name = 'mk_xattn_ffn_d4_seqx_r8_367e93'

def setup_inputs(seed: int=0):
    np.random.seed(seed)
    _w = jnp.asarray

    def _rec_inputs():
        import jax
        import jax.numpy as jnp
        _rk = jax.random.key(seed)
        x = -0.0002928 + 1 * jax.random.normal(jax.random.fold_in(_rk, 1), (4, 512, 128), jnp.float32)
        _lenS = 512 - jax.random.randint(jax.random.fold_in(_rk, 7), (4,), 0, max(1, 512 // 4) + 1, jnp.int32)
        _lenS2 = 77 - jax.random.randint(jax.random.fold_in(_rk, 8), (4,), 0, max(1, 77 // 4) + 1, jnp.int32)
        _ctx_1024P = jax.random.normal(jax.random.fold_in(_rk, 11), (4, 16, 128), jnp.float32)
        _ctx_1024c = jax.random.dirichlet(jax.random.fold_in(_rk, 511), 0.3 * jnp.ones((16,), jnp.float32), (4, 77))
        _ctx_1024t = jnp.einsum('bsk,bkd->bsd', _ctx_1024c, _ctx_1024P)
        _ctx_1024t = _ctx_1024t * jax.lax.rsqrt(jnp.mean(jnp.square(_ctx_1024t)) + 1e-12) * 0.953939
        ctx_1024 = -1.39393e-06 + 0.999914 * (_ctx_1024t + 0.3 * jax.random.normal(jax.random.fold_in(_rk, 611), (4, 77, 128), jnp.float32))
        _validS = jnp.arange(512)[None, :] < _lenS[:, None]
        _validS2 = jnp.arange(77)[None, :] < _lenS2[:, None]
        _causal = jnp.tril(jnp.ones((512, 512), dtype=bool))
        mask_BxS2_bf1 = jnp.ones((4, 77), dtype=bool)
        mask_Bx1xSxS2_fk1 = jnp.where(jnp.broadcast_to(_validS2[:, None, None, :], (4, 1, 512, 77)), 1.0, 0.0).astype(jnp.float32)
        mask_BxS2_bk0 = jnp.logical_not(jnp.broadcast_to(_validS2[:, :], (4, 77)))
        return (x, ctx_1024, mask_BxS2_bf1, mask_Bx1xSxS2_fk1, mask_BxS2_bk0)
    x, ctx_1024, mask_BxS2_bf1, mask_Bx1xSxS2_fk1, mask_BxS2_bk0 = _rec_inputs()

    def _L0_xattn_setup():
        import jax, jax.numpy as jnp
        import numpy as np
        import math
        B, T, S, C, H = (2, 256, 256, 128, 16)
        D = C // H

        def _proj_heads(x, W, b):
            y = x @ W.T + b
            Bv, L, _ = y.shape
            return y.reshape(Bv, L, H, D).transpose(0, 2, 1, 3)
        key = jax.random.key(seed)
        ks = jax.random.split(key, 12)
        s = 1.0 / math.sqrt(C)
        inp = {'query': jax.random.normal(ks[0], (B, T, C), jnp.float32), 'key': jax.random.normal(ks[1], (B, S, C), jnp.float32), 'value': jax.random.normal(ks[2], (B, S, C), jnp.float32), 'Wq': jax.random.normal(ks[3], (C, C), jnp.float32) * s, 'bq': jax.random.normal(ks[4], (C,), jnp.float32) * s, 'Wk': jax.random.normal(ks[5], (C, C), jnp.float32) * s, 'bk': jax.random.normal(ks[6], (C,), jnp.float32) * s, 'Wv': jax.random.normal(ks[7], (C, C), jnp.float32) * s, 'bv': jax.random.normal(ks[8], (C,), jnp.float32) * s, 'Wo': jax.random.normal(ks[9], (C, C), jnp.float32) * s, 'bo': jax.random.normal(ks[10], (C,), jnp.float32) * s, 'query_chunk_size': 128}
        return inp
    _L0_xattn_all = _L0_xattn_setup()
    _L0_xattn_in = {k: v for k, v in _L0_xattn_all.items() if k in ('Wq', 'bq', 'Wk', 'bk', 'Wv', 'bv', 'Wo', 'bo')}
    del _L0_xattn_all

    def _L0_ffn_setup():
        import jax, jax.numpy as jnp
        import numpy as np
        E, K, D, F = (8, 2, 128, 512)
        EPS = 1e-06
        B, S = (2, 128)
        key = jax.random.key(seed)
        ks = jax.random.split(key, 6)
        s_in = 1.0 / np.sqrt(D)
        s_mid = 1.0 / np.sqrt(F)
        return {'x': jax.random.normal(ks[0], (B, S, D), dtype=jnp.float32), 'Wg': jax.random.normal(ks[1], (D, E), dtype=jnp.float32) * s_in, 'gamma': jnp.ones((E, D), dtype=jnp.float32), 'beta': jnp.zeros((E, D), dtype=jnp.float32), 'W1': jax.random.normal(ks[2], (E, D, F), dtype=jnp.float32) * s_in, 'b1': jnp.zeros((E, F), dtype=jnp.float32), 'W2': jax.random.normal(ks[3], (E, F, D), dtype=jnp.float32) * s_mid, 'b2': jnp.zeros((E, D), dtype=jnp.float32)}
    _L0_ffn_all = _L0_ffn_setup()
    _L0_ffn_in = {k: v for k, v in _L0_ffn_all.items() if k in ('Wg', 'gamma', 'beta', 'W1', 'b1', 'W2', 'b2')}
    del _L0_ffn_all

    def _L1_xattn_setup():
        import jax, jax.numpy as jnp
        import numpy as np
        DIM = 128
        DIM_LATENT = 128
        DIM_HEAD = 64
        HEADS = 16
        INNER = HEADS * DIM_HEAD

        def layernorm(x, g, b, eps=1e-05):
            m = jnp.mean(x, axis=-1, keepdims=True)
            v = jnp.mean((x - m) ** 2, axis=-1, keepdims=True)
            return (x - m) / jnp.sqrt(v + eps) * g + b

        def rmsnorm(x, gamma, eps=1e-08):
            n = jnp.linalg.norm(x, axis=-1, keepdims=True) * x.shape[-1] ** (-0.5)
            return x / jnp.maximum(n, eps) * gamma
        key = jax.random.key(seed)
        ks = jax.random.split(key, 8)
        b, n, m = (4, 512, 64)
        x = jax.random.normal(ks[0], (b, n, DIM), dtype=jnp.float32)
        latents = jax.random.normal(ks[1], (b, m, DIM_LATENT), dtype=jnp.float32)
        mask = jnp.ones((b, n), dtype=bool)
        s = 0.02
        return {'x': x, 'latents': latents, 'mask': mask, 'ln_x_g': jnp.ones((DIM,), jnp.float32), 'ln_x_b': jnp.zeros((DIM,), jnp.float32), 'ln_l_g': jnp.ones((DIM_LATENT,), jnp.float32), 'ln_l_b': jnp.zeros((DIM_LATENT,), jnp.float32), 'qn_g': jnp.ones((DIM_HEAD,), jnp.float32), 'kn_g': jnp.ones((DIM_HEAD,), jnp.float32), 'Wq': jax.random.normal(ks[2], (DIM_LATENT, INNER), jnp.float32) * s, 'Wkv': jax.random.normal(ks[3], (DIM, 2 * INNER), jnp.float32) * s, 'Wout': jax.random.normal(ks[4], (INNER, DIM_LATENT), jnp.float32) * s, 'bout': jnp.zeros((DIM_LATENT,), jnp.float32)}
    _L1_xattn_all = _L1_xattn_setup()
    _L1_xattn_in = {k: v for k, v in _L1_xattn_all.items() if k in ('ln_x_g', 'ln_x_b', 'ln_l_g', 'ln_l_b', 'qn_g', 'kn_g', 'Wq', 'Wkv', 'Wout', 'bout')}
    del _L1_xattn_all

    def _L1_ffn_setup():
        import jax, jax.numpy as jnp
        import numpy as np
        B, S, H, E, I, MAX_K, A_HID = (2, 256, 128, 8, 336, 6, 50)
        key = jax.random.key(seed)
        ks = jax.random.split(key, 10)
        sc = 0.02
        return {'hidden_states': jax.random.normal(ks[0], (B, S, H), dtype=jnp.float32), 'router_w': jax.random.normal(ks[1], (E, H), dtype=jnp.float32) * sc, 'actor_w1': jax.random.normal(ks[2], (A_HID, H), dtype=jnp.float32) * sc, 'actor_b1': jnp.zeros((A_HID,), dtype=jnp.float32), 'actor_w2': jax.random.normal(ks[3], (MAX_K, A_HID), dtype=jnp.float32) * sc, 'actor_b2': jnp.zeros((MAX_K,), dtype=jnp.float32), 'gate_w': jax.random.normal(ks[4], (E, I, H), dtype=jnp.float32) * sc, 'up_w': jax.random.normal(ks[5], (E, I, H), dtype=jnp.float32) * sc, 'down_w': jax.random.normal(ks[6], (E, H, I), dtype=jnp.float32) * sc}
    _L1_ffn_all = _L1_ffn_setup()
    _L1_ffn_in = {k: v for k, v in _L1_ffn_all.items() if k in ('router_w', 'actor_w1', 'actor_b1', 'actor_w2', 'actor_b2', 'gate_w', 'up_w', 'down_w')}
    del _L1_ffn_all

    def _L2_xattn_setup():
        import jax, jax.numpy as jnp
        import numpy as np
        D_MODEL = 128
        NUM_HEADS = 16
        DEPTH = D_MODEL // NUM_HEADS
        B, S = (2, 256)

        def _split_heads(x):
            b, s, _ = x.shape
            return x.reshape(b, s, NUM_HEADS, DEPTH).transpose(0, 2, 1, 3)
        key = jax.random.key(seed)
        ks = jax.random.split(key, 13)
        scale = 1.0 / np.sqrt(D_MODEL)
        inp = {'v': jax.random.normal(ks[0], (B, S, D_MODEL), jnp.float32), 'k': jax.random.normal(ks[1], (B, S, D_MODEL), jnp.float32), 'q': jax.random.normal(ks[2], (B, S, D_MODEL), jnp.float32), 'mask': jax.random.randint(ks[3], (B, 1, S, S), 0, 2).astype(jnp.float32), 'wq': jax.random.normal(ks[4], (D_MODEL, D_MODEL), jnp.float32) * scale, 'bq': jnp.zeros((D_MODEL,), jnp.float32), 'wk': jax.random.normal(ks[5], (D_MODEL, D_MODEL), jnp.float32) * scale, 'bk': jnp.zeros((D_MODEL,), jnp.float32), 'wv': jax.random.normal(ks[6], (D_MODEL, D_MODEL), jnp.float32) * scale, 'bv': jnp.zeros((D_MODEL,), jnp.float32), 'wo': jax.random.normal(ks[7], (D_MODEL, D_MODEL), jnp.float32) * scale, 'bo': jnp.zeros((D_MODEL,), jnp.float32)}
        return inp
    _L2_xattn_all = _L2_xattn_setup()
    _L2_xattn_in = {k: v for k, v in _L2_xattn_all.items() if k in ('wq', 'bq', 'wk', 'bk', 'wv', 'bv', 'wo', 'bo')}
    del _L2_xattn_all

    def _L2_ffn_setup():
        import jax, jax.numpy as jnp
        import numpy as np
        K = 3
        TAU = 1.0
        EPS = 1e-08

        def _route_dense(z, k, tau):
            topi = jax.lax.top_k(z, k)[1]
            topv = jnp.take_along_axis(z, topi, axis=1)
            w = jax.nn.softmax(topv / (tau + EPS), axis=1)
            N, L = z.shape
            dw = jnp.zeros((N, L), z.dtype)
            dw = dw.at[jnp.arange(N)[:, None], topi].add(w)
            return dw

        def _apply_mixture(x, dw, W):
            y = jnp.zeros((x.shape[0], W.shape[1]), x.dtype)
            for e in range(W.shape[0]):
                y = y + x @ W[e].T * dw[:, e:e + 1]
            return y
        key = jax.random.key(seed)
        ks = jax.random.split(key, 8)
        B, T, D_in, H, D_out, L, d_addr = (4, 256, 128, 512, 128, 12, 64)

        def unitize(U):
            U = U - U.mean(axis=1, keepdims=True)
            return U / (jnp.linalg.norm(U, axis=1, keepdims=True) + EPS)
        x = jax.random.normal(ks[0], (B, T, D_in), jnp.float32)
        P_w = jax.random.normal(ks[1], (d_addr, D_in), jnp.float32) / np.sqrt(D_in)
        U1 = unitize(jax.random.normal(ks[2], (L, d_addr), jnp.float32))
        U2 = unitize(jax.random.normal(ks[3], (L, d_addr), jnp.float32))
        U3 = unitize(jax.random.normal(ks[4], (L, d_addr), jnp.float32))
        W1 = jax.random.normal(ks[5], (L, H, D_in), jnp.float32)
        W1 = W1 / jnp.linalg.norm(W1.reshape(L, -1), axis=1)[:, None, None]
        W2 = jax.random.normal(ks[6], (L, D_out, H), jnp.float32)
        W2 = W2 / jnp.linalg.norm(W2.reshape(L, -1), axis=1)[:, None, None]
        b2 = jax.random.normal(ks[7], (L, D_out), jnp.float32)
        b2 = b2 / jnp.linalg.norm(b2, axis=1, keepdims=True)
        return {'x': x, 'P_w': P_w, 'U1': U1, 'U2': U2, 'U3': U3, 'W1': W1, 'W2': W2, 'b2': b2}
    _L2_ffn_all = _L2_ffn_setup()
    _L2_ffn_in = {k: v for k, v in _L2_ffn_all.items() if k in ('P_w', 'U1', 'U2', 'U3', 'W1', 'W2', 'b2')}
    del _L2_ffn_all

    def _L3_xattn_setup():
        import jax, jax.numpy as jnp
        import numpy as np
        DIM = 128
        DIM_MEDIA = 128
        DIM_HEAD = 64
        HEADS = 8
        INNER = DIM_HEAD * HEADS
        B, N_TOK, N_LAT = (4, 512, 128)
        LN_EPS = 1e-05
        key = jax.random.key(seed)
        ks = jax.random.split(key, 6)
        x = jax.random.normal(ks[0], (B, N_TOK, DIM), dtype=jnp.float32)
        media = jax.random.normal(ks[1], (B, N_LAT, DIM_MEDIA), dtype=jnp.float32)
        media_mask = jax.random.randint(ks[2], (B, N_LAT), 0, 2).astype(bool)
        media_mask = media_mask.at[:, 0].set(True)
        ln_gamma = jnp.ones((DIM,), jnp.float32)
        ln_beta = jnp.zeros((DIM,), jnp.float32)
        Wq = jax.random.normal(ks[3], (DIM, INNER), jnp.float32) * DIM ** (-0.5)
        Wkv = jax.random.normal(ks[4], (DIM_MEDIA, 2 * INNER), jnp.float32) * DIM_MEDIA ** (-0.5)
        Wout = jax.random.normal(ks[5], (INNER, DIM), jnp.float32) * INNER ** (-0.5)
        return {'x': x, 'media': media, 'media_mask': media_mask, 'ln_gamma': ln_gamma, 'ln_beta': ln_beta, 'Wq': Wq, 'Wkv': Wkv, 'Wout': Wout}
    _L3_xattn_all = _L3_xattn_setup()
    _L3_xattn_in = {k: v for k, v in _L3_xattn_all.items() if k in ('ln_gamma', 'ln_beta', 'Wq', 'Wkv', 'Wout')}
    del _L3_xattn_all

    def _L3_ffn_setup():
        import jax, jax.numpy as jnp
        import numpy as np
        D = 128
        H = 256
        E = 8
        TOP_K = 2
        N_SHARED = 1
        B, S = (2, 128)
        key = jax.random.key(seed)
        ks = jax.random.split(key, 12)
        sc = 0.02
        return {'hidden': jax.random.normal(ks[0], (B, S, D), jnp.float32), 'router_w': jax.random.normal(ks[1], (D, E), jnp.float32) * sc, 'router_b': jnp.zeros((E,), jnp.float32), 'sw1': jax.random.normal(ks[2], (D, H), jnp.float32) * sc, 'sb1': jnp.zeros((H,), jnp.float32), 'sw2': jax.random.normal(ks[3], (H, D), jnp.float32) * sc, 'sb2': jnp.zeros((D,), jnp.float32), 'rw1': jax.random.normal(ks[4], (E, D, H), jnp.float32) * sc, 'rb1': jnp.zeros((E, H), jnp.float32), 'rw2': jax.random.normal(ks[5], (E, H, D), jnp.float32) * sc, 'rb2': jnp.zeros((E, D), jnp.float32)}
    _L3_ffn_all = _L3_ffn_setup()
    _L3_ffn_in = {k: v for k, v in _L3_ffn_all.items() if k in ('router_w', 'router_b', 'sw1', 'sb1', 'sw2', 'sb2', 'rw1', 'rb1', 'rw2', 'rb2')}
    del _L3_ffn_all
    return {'x': x, 'ctx_1024': ctx_1024, 'mask_BxS2_bf1': mask_BxS2_bf1, 'mask_Bx1xSxS2_fk1': mask_Bx1xSxS2_fk1, 'mask_BxS2_bk0': mask_BxS2_bk0, 'L0_xattn_Wq': _L0_xattn_in['Wq'], 'L0_xattn_bq': _L0_xattn_in['bq'], 'L0_xattn_Wk': _L0_xattn_in['Wk'], 'L0_xattn_bk': _L0_xattn_in['bk'], 'L0_xattn_Wv': _L0_xattn_in['Wv'], 'L0_xattn_bv': _L0_xattn_in['bv'], 'L0_xattn_Wo': _L0_xattn_in['Wo'], 'L0_xattn_bo': _L0_xattn_in['bo'], 'L0_ffn_Wg': _L0_ffn_in['Wg'], 'L0_ffn_gamma': _L0_ffn_in['gamma'], 'L0_ffn_beta': _L0_ffn_in['beta'], 'L0_ffn_W1': _L0_ffn_in['W1'], 'L0_ffn_b1': _L0_ffn_in['b1'], 'L0_ffn_W2': _L0_ffn_in['W2'], 'L0_ffn_b2': _L0_ffn_in['b2'], 'L1_xattn_ln_x_g': _L1_xattn_in['ln_x_g'], 'L1_xattn_ln_x_b': _L1_xattn_in['ln_x_b'], 'L1_xattn_ln_l_g': _L1_xattn_in['ln_l_g'], 'L1_xattn_ln_l_b': _L1_xattn_in['ln_l_b'], 'L1_xattn_qn_g': _L1_xattn_in['qn_g'], 'L1_xattn_kn_g': _L1_xattn_in['kn_g'], 'L1_xattn_Wq': _L1_xattn_in['Wq'], 'L1_xattn_Wkv': _L1_xattn_in['Wkv'], 'L1_xattn_Wout': _L1_xattn_in['Wout'], 'L1_xattn_bout': _L1_xattn_in['bout'], 'L1_ffn_router_w': _L1_ffn_in['router_w'], 'L1_ffn_actor_w1': _L1_ffn_in['actor_w1'], 'L1_ffn_actor_b1': _L1_ffn_in['actor_b1'], 'L1_ffn_actor_w2': _L1_ffn_in['actor_w2'], 'L1_ffn_actor_b2': _L1_ffn_in['actor_b2'], 'L1_ffn_gate_w': _L1_ffn_in['gate_w'], 'L1_ffn_up_w': _L1_ffn_in['up_w'], 'L1_ffn_down_w': _L1_ffn_in['down_w'], 'L2_xattn_wq': _L2_xattn_in['wq'], 'L2_xattn_bq': _L2_xattn_in['bq'], 'L2_xattn_wk': _L2_xattn_in['wk'], 'L2_xattn_bk': _L2_xattn_in['bk'], 'L2_xattn_wv': _L2_xattn_in['wv'], 'L2_xattn_bv': _L2_xattn_in['bv'], 'L2_xattn_wo': _L2_xattn_in['wo'], 'L2_xattn_bo': _L2_xattn_in['bo'], 'L2_ffn_P_w': _L2_ffn_in['P_w'], 'L2_ffn_U1': _L2_ffn_in['U1'], 'L2_ffn_U2': _L2_ffn_in['U2'], 'L2_ffn_U3': _L2_ffn_in['U3'], 'L2_ffn_W1': _L2_ffn_in['W1'], 'L2_ffn_W2': _L2_ffn_in['W2'], 'L2_ffn_b2': _L2_ffn_in['b2'], 'L3_xattn_ln_gamma': _L3_xattn_in['ln_gamma'], 'L3_xattn_ln_beta': _L3_xattn_in['ln_beta'], 'L3_xattn_Wq': _L3_xattn_in['Wq'], 'L3_xattn_Wkv': _L3_xattn_in['Wkv'], 'L3_xattn_Wout': _L3_xattn_in['Wout'], 'L3_ffn_router_w': _L3_ffn_in['router_w'], 'L3_ffn_router_b': _L3_ffn_in['router_b'], 'L3_ffn_sw1': _L3_ffn_in['sw1'], 'L3_ffn_sb1': _L3_ffn_in['sb1'], 'L3_ffn_sw2': _L3_ffn_in['sw2'], 'L3_ffn_sb2': _L3_ffn_in['sb2'], 'L3_ffn_rw1': _L3_ffn_in['rw1'], 'L3_ffn_rb1': _L3_ffn_in['rb1'], 'L3_ffn_rw2': _L3_ffn_in['rw2'], 'L3_ffn_rb2': _L3_ffn_in['rb2']}

def reference(x, ctx_1024, mask_BxS2_bf1, mask_Bx1xSxS2_fk1, mask_BxS2_bk0, L0_xattn_Wq, L0_xattn_bq, L0_xattn_Wk, L0_xattn_bk, L0_xattn_Wv, L0_xattn_bv, L0_xattn_Wo, L0_xattn_bo, L0_ffn_Wg, L0_ffn_gamma, L0_ffn_beta, L0_ffn_W1, L0_ffn_b1, L0_ffn_W2, L0_ffn_b2, L1_xattn_ln_x_g, L1_xattn_ln_x_b, L1_xattn_ln_l_g, L1_xattn_ln_l_b, L1_xattn_qn_g, L1_xattn_kn_g, L1_xattn_Wq, L1_xattn_Wkv, L1_xattn_Wout, L1_xattn_bout, L1_ffn_router_w, L1_ffn_actor_w1, L1_ffn_actor_b1, L1_ffn_actor_w2, L1_ffn_actor_b2, L1_ffn_gate_w, L1_ffn_up_w, L1_ffn_down_w, L2_xattn_wq, L2_xattn_bq, L2_xattn_wk, L2_xattn_bk, L2_xattn_wv, L2_xattn_bv, L2_xattn_wo, L2_xattn_bo, L2_ffn_P_w, L2_ffn_U1, L2_ffn_U2, L2_ffn_U3, L2_ffn_W1, L2_ffn_W2, L2_ffn_b2, L3_xattn_ln_gamma, L3_xattn_ln_beta, L3_xattn_Wq, L3_xattn_Wkv, L3_xattn_Wout, L3_ffn_router_w, L3_ffn_router_b, L3_ffn_sw1, L3_ffn_sb1, L3_ffn_sw2, L3_ffn_sb2, L3_ffn_rw1, L3_ffn_rb1, L3_ffn_rw2, L3_ffn_rb2):
    import jax
    import jax.numpy as jnp

    def _L0_xattn_ref(query, key, value, Wq, bq, Wk, bk, Wv, bv, Wo, bo, query_chunk_size):
        import jax, jax.numpy as jnp
        import numpy as np
        import math
        B, T, S, C, H = (2, 256, 256, 128, 16)
        D = C // H

        def _proj_heads(x, W, b):
            y = x @ W.T + b
            Bv, L, _ = y.shape
            return y.reshape(Bv, L, H, D).transpose(0, 2, 1, 3)
        q = _proj_heads(query, Wq, bq) * (1.0 / math.sqrt(D))
        k = _proj_heads(key, Wk, bk)
        v = _proj_heads(value, Wv, bv)
        scores = jnp.einsum('bhqd,bhkd->bhqk', q, k)
        attn = jax.nn.softmax(scores, axis=-1)
        out = jnp.einsum('bhqk,bhkd->bhqd', attn, v)
        out = out.transpose(0, 2, 1, 3).reshape(query.shape[0], query.shape[1], C)
        return out @ Wo.T + bo

    def _L0_ffn_ref(x, Wg, gamma, beta, W1, b1, W2, b2):
        import jax, jax.numpy as jnp
        import numpy as np
        E, K, D, F = (8, 2, 128, 512)
        EPS = 1e-06
        B, S = (2, 128)
        orig_shape = x.shape
        xf = x.reshape(-1, orig_shape[-1])
        scores = xf @ Wg
        w, idx = jax.lax.top_k(scores, K)
        w = jax.nn.softmax(w, axis=-1)
        mu = jnp.mean(xf, axis=-1, keepdims=True)
        var = jnp.var(xf, axis=-1, keepdims=True)
        xhat = (xf - mu) * jax.lax.rsqrt(var + EPS)
        normed = xhat[None, :, :] * gamma[:, None, :] + beta[:, None, :]
        h = jax.nn.relu(jnp.einsum('end,edf->enf', normed, W1) + b1[:, None, :])
        out = jnp.einsum('enf,efd->end', h, W2) + b2[:, None, :] + xf[None, :, :]
        cw = jnp.sum(w[..., None] * jax.nn.one_hot(idx, E, dtype=w.dtype), axis=1)
        y = jnp.einsum('ne,end->nd', cw, out)
        return y.reshape(orig_shape)

    def _L1_xattn_ref(x, latents, mask, ln_x_g, ln_x_b, ln_l_g, ln_l_b, qn_g, kn_g, Wq, Wkv, Wout, bout):
        import jax, jax.numpy as jnp
        import numpy as np
        DIM = 128
        DIM_LATENT = 128
        DIM_HEAD = 64
        HEADS = 16
        INNER = HEADS * DIM_HEAD

        def layernorm(x, g, b, eps=1e-05):
            m = jnp.mean(x, axis=-1, keepdims=True)
            v = jnp.mean((x - m) ** 2, axis=-1, keepdims=True)
            return (x - m) / jnp.sqrt(v + eps) * g + b

        def rmsnorm(x, gamma, eps=1e-08):
            n = jnp.linalg.norm(x, axis=-1, keepdims=True) * x.shape[-1] ** (-0.5)
            return x / jnp.maximum(n, eps) * gamma
        b, n, _ = x.shape
        m = latents.shape[1]
        h, d = (HEADS, DIM_HEAD)
        scale = d ** (-0.5)
        xn = layernorm(x, ln_x_g, ln_x_b)
        ln = layernorm(latents, ln_l_g, ln_l_b)
        q = (ln @ Wq).reshape(b, m, h, d).transpose(0, 2, 1, 3)
        kv = jnp.concatenate([xn @ Wkv, ln @ Wkv], axis=1)
        kv = kv.reshape(b, n + m, 2, h, d)
        k = kv[:, :, 0].transpose(0, 2, 1, 3)
        v = kv[:, :, 1].transpose(0, 2, 1, 3)
        qn = rmsnorm(q, qn_g) * scale
        kn = rmsnorm(k, kn_g)
        sim = jnp.einsum('bhid,bhjd->bhij', qn, kn)
        max_neg = -jnp.finfo(sim.dtype).max
        padded_mask = jnp.concatenate([mask, jnp.ones((b, m), bool)], axis=1)
        sim = jnp.where(padded_mask[:, None, None, :], sim, max_neg)
        attn = jax.nn.softmax(sim.astype(jnp.float32), axis=-1).astype(sim.dtype)
        out = jnp.einsum('bhij,bhjd->bhid', attn, v)
        out = out.transpose(0, 2, 1, 3).reshape(b, m, h * d)
        return out @ Wout + bout

    def _L1_ffn_ref(hidden_states, router_w, actor_w1, actor_b1, actor_w2, actor_b2, gate_w, up_w, down_w):
        import jax, jax.numpy as jnp
        import numpy as np
        B, S, H, E, I, MAX_K, A_HID = (2, 256, 128, 8, 336, 6, 50)
        probs = jax.nn.softmax(jnp.einsum('bsh,eh->bse', hidden_states, router_w).astype(jnp.float32), axis=-1)
        a_h = jax.nn.gelu(jnp.einsum('bsh,ah->bsa', hidden_states, actor_w1) + actor_b1)
        actor_logits = jnp.clip(jnp.einsum('bsa,ka->bsk', a_h, actor_w2) + actor_b2, -30.0, 30.0)
        sampled_k = jnp.argmax(actor_logits, axis=-1) + 1
        order = jnp.argsort(-probs, axis=-1)
        rank = jnp.argsort(order, axis=-1)
        mask = rank < sampled_k[..., None]
        scores = jnp.where(mask, probs, 0.0).astype(hidden_states.dtype)
        out = jnp.zeros_like(hidden_states)
        for e in range(E):
            g = jnp.einsum('bsh,ih->bsi', hidden_states, gate_w[e])
            u = jnp.einsum('bsh,ih->bsi', hidden_states, up_w[e])
            y = jnp.einsum('bsi,hi->bsh', jax.nn.silu(g) * u, down_w[e])
            out = out + scores[..., e:e + 1] * y
        return out

    def _L2_xattn_ref(v, k, q, mask, wq, bq, wk, bk, wv, bv, wo, bo):
        import jax, jax.numpy as jnp
        import numpy as np
        D_MODEL = 128
        NUM_HEADS = 16
        DEPTH = D_MODEL // NUM_HEADS
        B, S = (2, 256)

        def _split_heads(x):
            b, s, _ = x.shape
            return x.reshape(b, s, NUM_HEADS, DEPTH).transpose(0, 2, 1, 3)
        qh = _split_heads(q @ wq.T + bq)
        kh = _split_heads(k @ wk.T + bk)
        vh = _split_heads(v @ wv.T + bv)
        score = jnp.einsum('bhqd,bhkd->bhqk', qh, kh) / jnp.sqrt(jnp.float32(DEPTH))
        score = score + mask * jnp.float32(-1000000000.0)
        attn = jax.nn.softmax(score, axis=-1)
        out = jnp.einsum('bhqk,bhkd->bhqd', attn, vh)
        out = out.transpose(0, 2, 1, 3).reshape(out.shape[0], -1, D_MODEL)
        return out @ wo.T + bo

    def _L2_ffn_ref(x, P_w, U1, U2, U3, W1, W2, b2):
        import jax, jax.numpy as jnp
        import numpy as np
        K = 3
        TAU = 1.0
        EPS = 1e-08

        def _route_dense(z, k, tau):
            topi = jax.lax.top_k(z, k)[1]
            topv = jnp.take_along_axis(z, topi, axis=1)
            w = jax.nn.softmax(topv / (tau + EPS), axis=1)
            N, L = z.shape
            dw = jnp.zeros((N, L), z.dtype)
            dw = dw.at[jnp.arange(N)[:, None], topi].add(w)
            return dw

        def _apply_mixture(x, dw, W):
            y = jnp.zeros((x.shape[0], W.shape[1]), x.dtype)
            for e in range(W.shape[0]):
                y = y + x @ W[e].T * dw[:, e:e + 1]
            return y
        B, T, D = x.shape
        x_flat = x.reshape(B * T, D)
        x_addr = x_flat @ P_w.T
        dw1 = _route_dense(x_addr @ U1.T, K, TAU)
        dw2 = _route_dense(x_addr @ U2.T, K, TAU)
        dw3 = _route_dense(x_addr @ U3.T, K, TAU)
        h = _apply_mixture(x_flat, dw1, W1)
        h = jax.nn.gelu(h, approximate=False)
        y = _apply_mixture(h, dw2, W2)
        y = y + dw3 @ b2
        return y.reshape(B, T, -1)

    def _L3_xattn_ref(x, media, media_mask, ln_gamma, ln_beta, Wq, Wkv, Wout):
        import jax, jax.numpy as jnp
        import numpy as np
        DIM = 128
        DIM_MEDIA = 128
        DIM_HEAD = 64
        HEADS = 8
        INNER = DIM_HEAD * HEADS
        B, N_TOK, N_LAT = (4, 512, 128)
        LN_EPS = 1e-05
        scale = DIM_HEAD ** (-0.5)
        mu = jnp.mean(x, axis=-1, keepdims=True)
        var = jnp.mean(jnp.square(x - mu), axis=-1, keepdims=True)
        xn = (x - mu) * jax.lax.rsqrt(var + LN_EPS) * ln_gamma + ln_beta
        q = xn @ Wq * scale
        kv = media @ Wkv
        k, v = jnp.split(kv, 2, axis=-1)

        def to_heads(t):
            b, n, _ = t.shape
            return t.reshape(b, n, HEADS, DIM_HEAD).transpose(0, 2, 1, 3)
        q, k, v = (to_heads(q), to_heads(k), to_heads(v))
        sim = jnp.einsum('bhid,bhjd->bhij', q, k)
        neg_inf = jnp.float32(-jnp.inf)
        sim = jnp.where(media_mask[:, None, None, :], sim, neg_inf)
        sim = sim - jax.lax.stop_gradient(jnp.max(sim, axis=-1, keepdims=True))
        attn = jax.nn.softmax(sim, axis=-1)
        out = jnp.einsum('bhij,bhjd->bhid', attn, v)
        out = out.transpose(0, 2, 1, 3).reshape(out.shape[0], out.shape[2], INNER)
        return out @ Wout

    def _L3_ffn_ref(hidden, router_w, router_b, sw1, sb1, sw2, sb2, rw1, rb1, rw2, rb2):
        import jax, jax.numpy as jnp
        import numpy as np
        D = 128
        H = 256
        E = 8
        TOP_K = 2
        N_SHARED = 1
        B, S = (2, 128)
        b, s, d = hidden.shape
        T = b * s
        flat = hidden.reshape(T, d)
        router_logits = flat @ router_w + router_b
        router_probs = jax.nn.softmax(router_logits, axis=-1)
        topk_probs, topk_idx = jax.lax.top_k(router_probs, TOP_K)
        weights = jnp.zeros_like(router_probs).at[jnp.arange(T)[:, None], topk_idx].add(topk_probs)
        sh = jax.nn.gelu(flat @ sw1 + sb1, approximate=False)
        shared_out = (sh @ sw2 + sb2) / N_SHARED
        h1 = jax.nn.gelu(jnp.einsum('td,edh->teh', flat, rw1) + rb1[None], approximate=False)
        expert_out = jnp.einsum('teh,ehd->ted', h1, rw2) + rb2[None]
        mixed = jnp.einsum('ted,te->td', expert_out, weights)
        return (shared_out + mixed).reshape(b, s, d)
    x = x + _L0_xattn_ref(_layernorm(x, axis=-1), ctx_1024, ctx_1024, L0_xattn_Wq, L0_xattn_bq, L0_xattn_Wk, L0_xattn_bk, L0_xattn_Wv, L0_xattn_bv, L0_xattn_Wo, L0_xattn_bo, 128)
    x = x + _L0_ffn_ref(_layernorm(x, axis=-1), L0_ffn_Wg, L0_ffn_gamma, L0_ffn_beta, L0_ffn_W1, L0_ffn_b1, L0_ffn_W2, L0_ffn_b2)
    x = x + _L1_xattn_ref(ctx_1024, _layernorm(x, axis=-1), mask_BxS2_bf1, L1_xattn_ln_x_g, L1_xattn_ln_x_b, L1_xattn_ln_l_g, L1_xattn_ln_l_b, L1_xattn_qn_g, L1_xattn_kn_g, L1_xattn_Wq, L1_xattn_Wkv, L1_xattn_Wout, L1_xattn_bout)
    x = x + _L1_ffn_ref(_layernorm(x, axis=-1), L1_ffn_router_w, L1_ffn_actor_w1, L1_ffn_actor_b1, L1_ffn_actor_w2, L1_ffn_actor_b2, L1_ffn_gate_w, L1_ffn_up_w, L1_ffn_down_w)
    x = x + _L2_xattn_ref(ctx_1024, ctx_1024, _layernorm(x, axis=-1), mask_Bx1xSxS2_fk1, L2_xattn_wq, L2_xattn_bq, L2_xattn_wk, L2_xattn_bk, L2_xattn_wv, L2_xattn_bv, L2_xattn_wo, L2_xattn_bo)
    x = x + _L2_ffn_ref(_layernorm(x, axis=-1), L2_ffn_P_w, L2_ffn_U1, L2_ffn_U2, L2_ffn_U3, L2_ffn_W1, L2_ffn_W2, L2_ffn_b2)
    x = x + _L3_xattn_ref(_layernorm(x, axis=-1), ctx_1024, mask_BxS2_bk0, L3_xattn_ln_gamma, L3_xattn_ln_beta, L3_xattn_Wq, L3_xattn_Wkv, L3_xattn_Wout)
    x = x + _L3_ffn_ref(_layernorm(x, axis=-1), L3_ffn_router_w, L3_ffn_router_b, L3_ffn_sw1, L3_ffn_sb1, L3_ffn_sw2, L3_ffn_sb2, L3_ffn_rw1, L3_ffn_rb1, L3_ffn_rw2, L3_ffn_rb2)
    return x

_drawn_inputs = setup_inputs


def setup_inputs(seed=0):
    import zlib

    import numpy as np

    out = dict(_drawn_inputs(seed))
    spreads = {'L0_ffn_gamma': (1.0, 0.2),
     'L0_ffn_beta': (0.0, 0.355),
     'L0_ffn_b1': (0.0, 0.359),
     'L0_ffn_b2': (0.0, 0.1),
     'L1_xattn_ln_x_g': (1.0, 0.6),
     'L1_xattn_ln_x_b': (0.0, 0.8),
     'L1_xattn_ln_l_g': (1.0, 0.6),
     'L1_xattn_ln_l_b': (0.0, 0.8),
     'L1_xattn_qn_g': (1.0, 0.6),
     'L1_xattn_kn_g': (1.0, 0.6),
     'L1_xattn_bout': (0.0, 0.1),
     'L1_ffn_actor_b1': (0.0, 0.1),
     'L1_ffn_actor_b2': (0.0, 0.8),
     'L2_xattn_bq': (0.0, 0.496),
     'L2_xattn_bk': (0.0, 2.0),
     'L2_xattn_bv': (0.0, 0.1),
     'L2_xattn_bo': (0.0, 0.1),
     'L3_xattn_ln_gamma': (1.0, 0.6),
     'L3_xattn_ln_beta': (0.0, 0.483),
     'L3_ffn_router_b': (0.0, 0.8),
     'L3_ffn_sb1': (0.0, 0.8),
     'L3_ffn_sb2': (0.0, 0.43),
     'L3_ffn_rb1': (0.0, 0.8),
     'L3_ffn_rb2': (0.0, 0.8)}
    factors = {'L0_xattn_bk': 64.0,
     'L1_xattn_Wq': 6.991,
     'L1_ffn_router_w': 8.0,
     'L1_ffn_gate_w': 8.0,
     'L1_ffn_up_w': 8.0,
     'L1_ffn_down_w': 8.0,
     'L2_ffn_P_w': 2.733,
     'L2_ffn_U1': 8.0,
     'L2_ffn_U2': 8.0,
     'L2_ffn_U3': 2.726,
     'L2_ffn_W1': 8.0,
     'L2_ffn_W2': 8.0,
     'L3_ffn_router_w': 6.372,
     'L3_ffn_sw1': 3.709,
     'L3_ffn_sw2': 3.363,
     'L3_ffn_rw1': 8.0,
     'L3_ffn_rw2': 8.0}
    for name, (base, spread) in spreads.items():
        noise = np.random.default_rng([zlib.crc32(name.encode()), seed]).standard_normal(out[name].shape)
        drawn = base * np.exp(spread * noise) if base else spread * noise
        out[name] = jnp.asarray(drawn.astype(out[name].dtype))
    for name, factor in factors.items():
        out[name] = (out[name] * factor).astype(out[name].dtype)
    return out
```

```python
from contextlib import ExitStack

import concourse.bass as bass
from concourse import mybir

F32 = mybir.dt.float32
U8 = mybir.dt.uint8
U32 = mybir.dt.uint32
ALU = mybir.AluOpType
ACT = mybir.ActivationFunctionType
AX = mybir.AxisListType

P = 128
BATCH, SEQ, KEYS = 4, 512, 77
TILES = BATCH * SEQ // P
TPB = SEQ // P
HALVES = 2
NORM_EPS = 1e-5

VECS = {}
for _name, _n in (("L0_bq", 1), ("L0_bk", 1), ("L2_bq", 1), ("L2_bk", 1), ("L1_xg", 1), ("L1_xb", 1), ("L1_lg", 1), ("L1_lb", 1), ("L1_qg", 1),
                  ("L1_kg", 1), ("L1f_b1", 1), ("L3_g", 1), ("L3_b", 1)):
    VECS[_name] = (sum(n for _, n in VECS.values()), _n)
NVEC = sum(n for _, n in VECS.values())
ROWS = ["L0_bv", "L0_bo", "L1_bout", "L2_bv", "L2_bo", "L3f_rb", "L1f_b2"]


class Core:

    def __init__(self, nc, ctx, dram, layers):
        self.nc, self.ctx, self.dram, self.layers = nc, ctx, dram, layers
        self.ps = ctx.enter_context(nc.psum_tensor("banks", [P, 8, 512], F32))
        self.resid = self.sb(ctx, "resid", [P, TILES, P])
        self.normT = self.sb(ctx, "normT", [P, TILES * P])
        self.ident = self.sb(ctx, "ident", [P, P])
        self.vecs = self.sb(ctx, "vecs", [P, NVEC])
        self.rows = self.sb(ctx, "rows", [P, len(ROWS), P])
        self.ctxT = self.sb(ctx, "ctxT", [P, BATCH, KEYS])
        self.head16 = self.sb(ctx, "head16", [P, 16])
        self.pairsum = self.sb(ctx, "pairsum", [P, P])
        self.count12 = self.sb(ctx, "count12", [P, 12])

    def sb(self, ctx, name, shape, dt=F32):
        return ctx.enter_context(self.nc.sbuf_tensor(f"sb_{name}", shape, dt))

    def sem(self, name):
        return self.nc.alloc_semaphore(name)

    def retire(self, before):
        self.nc.clear_and_free_semaphores(self.nc.allocated_since(before))
        self.nc.all_engine_barrier()

    def pair(self, name):
        return [self.sem(f"{name}{u}") for u in range(HALVES)]

    def vec(self, name, i=0):
        at = VECS[name][0] + i
        return self.vecs[:, at:at + 1]

    def row(self, name):
        return self.rows[:, ROWS.index(name), :]


class InOrder:

    def __init__(self, eng, sem):
        self.eng, self.sem, self.n = eng, sem, 0

    def __call__(self, ins, base=0):
        self.n += 1
        ins.then_inc(self.sem, 1)
        self.eng.wait_ge(self.sem, base + self.n)


def bcast(ap, dims):
    for i, d in enumerate(dims):
        if d is not None:
            ap = ap.unsqueeze(i + 1)
    shape = [ap.shape[0]] + [s if d is None else d for d, s in zip(dims, ap.shape[1:])]
    return ap.broadcast_to(shape)


def constants(c):
    nc, d = c.nc, c.dram
    loaded, built = c.sem("loaded"), c.sem("built")
    counts = c.ctx.enter_context(nc.sbuf_tensor("counts", [P, 12], mybir.dt.int32))
    with nc.Block() as block:
        @block.sync
        def _(sp):
            sp.dma_start(c.resid[:], d["x"]).then_inc(loaded, 16)
            sp.dma_start(c.vecs[:], d["vecs"]).then_inc(loaded, 16)
            sp.dma_start(c.rows[:], d["rows"]).then_inc(loaded, 16)
            sp.dma_start(c.ctxT[:], d["ctxT"]).then_inc(loaded, 16)
            sp.wait_ge(loaded, 64)

        @block.gpsimd
        def _(pool):
            step = InOrder(pool, built)
            pool.memset(c.ident[:], 0.0)
            pool.memset(c.head16[:], 1.0)
            pool.memset(c.pairsum[:], 0.0)
            step(pool.iota(counts[:], pattern=[[1, 12]], base=0, channel_multiplier=0))
            pool.tensor_copy(c.count12[:], counts[:])
            pool.affine_select(out=c.ident[:], in_=c.ident[:], compare_op=ALU.not_equal, fill=1.0, base=0,
                               pattern=[[-1, P]], channel_multiplier=1)
            step(pool.affine_select(out=c.head16[:], in_=c.head16[:], compare_op=ALU.is_ge, fill=0.0, base=0,
                                    pattern=[[-8, 16]], channel_multiplier=1))
            step(pool.affine_select(out=c.head16[:], in_=c.head16[:], compare_op=ALU.is_ge, fill=0.0, base=7,
                                    pattern=[[8, 16]], channel_multiplier=-1))
            step(pool.memset(c.pairsum[0:64, 0:64], 1.0))
            step(pool.memset(c.pairsum[64:128, 64:128], 1.0))


class Norm:

    def __init__(self, c, ctx, tag, inner_eps=None, gain=None, shift=None, banks=0):
        self.c, self.inner_eps, self.gain, self.shift = c, inner_eps, gain, shift
        self.banks = c.ps[:, banks:banks + HALVES, :]
        self.stats = c.sb(ctx, f"{tag}_stats", [P, TILES, 6])
        self.mean = c.sb(ctx, f"{tag}_mean", [P, TILES])
        self.var = c.sb(ctx, f"{tag}_var", [P, TILES])
        self.std = c.sb(ctx, f"{tag}_std", [P, TILES])
        self.std2 = c.sb(ctx, f"{tag}_std2", [P, TILES])
        self.rstd = c.sb(ctx, f"{tag}_rstd", [P, TILES])
        self.scale = c.sb(ctx, f"{tag}_scale", [P, TILES])
        self.work = c.sb(ctx, f"{tag}_work", [P, 3, TILES])
        self.stage = c.sb(ctx, f"{tag}_stage", [P, HALVES, TPB, P])
        self.order = c.sem(f"{tag}_norm_order")
        self.var_ready, self.std_ready = c.sem(f"{tag}_var_ready"), c.sem(f"{tag}_std_ready")
        self.staged, self.turned, self.ready = (c.sem(f"{tag}_{n}") for n in ("norm_staged", "norm_turned", "norm_ready"))

    def vector(self, dve):
        c, step = self.c, InOrder(dve, self.order)
        with dve.Fori(0, TPB) as q:
            for t in range(BATCH):
                last = dve.bn_stats(self.stats[:, bass.ds(q * BATCH + t, 1), :].rearrange("p a s -> p (a s)"),
                                    c.resid[:, bass.ds(q * BATCH + t, 1), :].rearrange("p a d -> p (a d)"))
            last.then_inc(self.order, 1)
        step.n = TPB
        dve.wait_ge(self.order, TPB)
        me, mo = self.stats[:, :, 1], self.stats[:, :, 4]
        half, gap, spread = (self.work[:, i, :] for i in range(3))
        dve.tensor_tensor(half, me, mo, ALU.add)
        dve.tensor_tensor(spread, self.stats[:, :, 2], self.stats[:, :, 5], ALU.add)
        step(dve.tensor_tensor(gap, me, mo, ALU.subtract))
        dve.tensor_scalar(self.mean[:], half, 0.5, None, ALU.mult)
        step(dve.tensor_tensor(gap, gap, gap, ALU.mult))
        step(dve.tensor_scalar(spread, spread, 1.0 / P, None, ALU.mult))
        step(dve.scalar_tensor_tensor(out=self.var[:], in0=gap, scalar=0.25, in1=spread, op0=ALU.mult, op1=ALU.add))
        dve.tensor_scalar(gap, self.var[:], NORM_EPS, None, ALU.add).then_inc(self.var_ready, 1)
        dve.wait_ge(self.std_ready, 1)
        step(dve.reciprocal(self.rstd[:], self.std[:]))
        scale = self.rstd
        if self.inner_eps is not None:
            step(dve.tensor_tensor(half, self.var[:], self.rstd[:], ALU.mult))
            step(dve.tensor_tensor(half, half, self.rstd[:], ALU.mult))
            dve.tensor_scalar(spread, half, self.inner_eps, None, ALU.add).then_inc(self.var_ready, 1)
            dve.wait_ge(self.std_ready, 2)
            step(dve.reciprocal(half, self.std2[:]))
            step(dve.tensor_tensor(self.scale[:], half, self.rstd[:], ALU.mult))
            scale = self.scale
        for b in range(BATCH):
            if b >= HALVES:
                dve.wait_ge(self.turned, b - HALVES + 1)
            for t in range(TPB):
                n = b * TPB + t
                last = dve.tensor_scalar(self.stage[:, b % HALVES, t, :], c.resid[:, n, :], self.mean[:, n:n + 1], scale[:, n:n + 1],
                                         ALU.subtract, ALU.mult)
            last.then_inc(self.staged, 1)

    def tensor(self, pe):
        for b in range(BATCH):
            pe.wait_ge(self.staged, b + 1)
            if b >= HALVES:
                pe.wait_ge(self.ready, b - HALVES + 1)
            for t in range(TPB):
                last = pe.transpose(self.banks[:, b % HALVES, t * P:(t + 1) * P], self.stage[:, b % HALVES, t, :], self.c.ident[:])
            last.then_inc(self.turned, 1)

    def scalar(self, act):
        act.wait_ge(self.var_ready, 1)
        act.activation(self.std[:], self.work[:, 1, :], ACT.Sqrt).then_inc(self.std_ready, 1)
        if self.inner_eps is not None:
            act.wait_ge(self.var_ready, 2)
            act.activation(self.std2[:], self.work[:, 2, :], ACT.Sqrt).then_inc(self.std_ready, 1)
        for b in range(BATCH):
            act.wait_ge(self.turned, b + 1)
            out = self.c.normT[:, b * SEQ:(b + 1) * SEQ]
            if self.gain is None:
                ins = act.activation(out, self.banks[:, b % HALVES, :], ACT.Copy)
            else:
                ins = act.activation(out, self.banks[:, b % HALVES, :], ACT.Identity, bias=self.shift, scale=self.gain)
            ins.then_inc(self.ready, 1)

    def wait(self, eng, b=BATCH - 1):
        eng.wait_ge(self.ready, b + 1)


def cross_attention(c, tag, H, D, score_scale, mask, **norm_args):
    nc, ps = c.nc, c.ps
    FB = H * D // P
    HB = H // FB
    GROUP = 4
    COLS = P // GROUP if FB == 1 else D
    GROUPS = H // GROUP
    PROBS = TPB
    biased = FB == 1
    with ExitStack() as ctx:
        wq, wk, wv = (c.sb(ctx, f"{tag}_w{n}", [P, FB * P]) for n in "qkv")
        wo = c.sb(ctx, f"{tag}_wo", [P, FB, P])
        bq = c.sb(ctx, f"{tag}_bq", [P, 1])
        kT = c.sb(ctx, f"{tag}_kT", [P, FB, BATCH * KEYS])
        kdiag = c.sb(ctx, f"{tag}_kdiag", [P, BATCH, FB, HB, KEYS])
        v_all, v_now = c.sb(ctx, f"{tag}_v_all", [KEYS, BATCH, H, COLS]), c.sb(ctx, f"{tag}_v_now", [KEYS, H, COLS])
        qT = c.sb(ctx, f"{tag}_qT", [P, FB, SEQ])
        prob, top = c.sb(ctx, f"{tag}_prob", [P, PROBS, H * KEYS]), c.sb(ctx, f"{tag}_top", [P, HALVES, H])
        probT = c.sb(ctx, f"{tag}_probT", [KEYS, H, P])
        rsum = c.sb(ctx, f"{tag}_rsum", [P, PROBS, H])
        mixedT = c.sb(ctx, f"{tag}_mixedT", [P, FB * P])
        masks = c.sb(ctx, f"{tag}_masks", [P, TILES, KEYS]) if mask == "scaled" else None
        keep = c.sb(ctx, f"{tag}_keep", [P, BATCH, KEYS], U8) if mask == "barred" else None
        barred = c.sb(ctx, f"{tag}_barred", [P, BATCH, KEYS]) if mask == "barred" else None
        norm = Norm(c, ctx, tag, banks=3 if FB == 1 else 2, **norm_args)
        w_in, mask_in, order, prepared, bias_added = (c.sem(f"{tag}_{n}") for n in ("w_in", "mask_in", "order", "prepared", "bias_added"))
        k_done, kT_ready, kdiag_ready, v_done, v_clear, v_ready, v_placed = (c.sem(f"{tag}_{n}") for n in (
            "k_done", "kT_ready", "kdiag_ready", "v_done", "v_clear", "v_ready", "v_placed"))
        q_done, q_ready, scored, masked, shifted, exped = (c.sem(f"{tag}_{n}") for n in (
            "q_done", "q_ready", "scored", "masked", "shifted", "exped"))
        summed, normed, turned, turn_read, pv_done, mixed_ready, y_done, y_added = (c.sem(f"{tag}_{n}") for n in (
            "summed", "normed", "turned", "turn_read", "pv_done", "mixed_ready", "y_done", "y_added"))
        score_read = shifted if mask is None else masked
        PV, Y, Q = 5, 6, 7
        if FB == 1:
            KV, TURN = (0, 1), 3
            flat = ps[:, 0:3, :].rearrange("p b n -> p (b n)")[:, 0:H * KEYS]
            cuts = [(a, min(a + 512, H * KEYS)) for a in range(0, H * KEYS, 512)]
            heads = flat.rearrange("p (g h k) -> p g h k", g=1, h=H)
        else:
            KV, TURN = (0, 1, 4, 5), 2
            heads = ps[:, 0:2, 0:H // 2 * KEYS].rearrange("p g (h k) -> p g h k", h=H // 2)
        G = heads.shape[1]
        HALF = H // 2

        def later(n, k):
            return not isinstance(n, int) or 0 <= n + k < TILES

        with nc.Block() as block:
            @block.sync
            def _(sp):
                for sb, name in ((wk, "wk"), (wv, "wv"), (wq, "wq"), (wo, "wo")):
                    sp.dma_start(sb[:], c.dram[f"{tag}_{name}"]).then_inc(w_in, 16)
                if mask is not None:
                    sp.dma_start((masks if keep is None else keep)[:], c.dram[f"{tag}_mask"]).then_inc(mask_in, 16)

            @block.gpsimd
            def _(pool):
                pool.memset(v_all[:], 0.0).then_inc(v_clear, 1)
                member = c.head16[:].rearrange("p (a g) -> p g a", g=GROUP) if FB == 1 else c.pairsum[:, 0:P:D].unsqueeze(1)
                for j in range(FB):
                    pool.wait_ge(kT_ready, j + 1)
                    for b in range(BATCH):
                        pool.tensor_tensor(kdiag[:, b, j].rearrange("p (g a) k -> p g a k", g=member.shape[1]),
                                           bcast(kT[:, j, b * KEYS:(b + 1) * KEYS], list(member.shape[1:]) + [None]),
                                           bcast(member, [None, None, KEYS]), ALU.mult).then_inc(kdiag_ready, 1)
                if biased:
                    norm.wait(pool)
                    pool.tensor_tensor(c.resid[:], c.resid[:], bcast(c.row(f"{tag}_bo"), [TILES, None]), ALU.add).then_inc(bias_added, 1)

                def place_v(b):
                    pool.tensor_copy(v_now[:].rearrange("k h v -> k (h v)"), v_all[:, bass.ds(b, 1)].rearrange("k b h v -> k (b h v)")).then_inc(v_placed, 1)

                def divide(n, i):
                    for x in range(2):
                        pool.wait_ge(summed, n * 2 + x + 1)
                        half = slice(x * HALF, (x + 1) * HALF)
                        grid = prob[:, i % PROBS, :].rearrange("p (h k) -> p h k", h=H)[:, half]
                        pool.tensor_tensor(grid, grid, bcast(rsum[:, i % PROBS, half], [None, KEYS]), ALU.mult).then_inc(normed, 1)

                def tile(n, b, i):
                    if not isinstance(n, int) and i == TPB - 1:
                        pool.wait_ge(pv_done, n + 1)
                        place_v(b + 1)
                    if later(n, 1):
                        divide(n + 1, i + 1)

                pool.wait_ge(v_ready, GROUP)
                place_v(0)
                divide(0, 0)
                tile(0, 0, 0)
                with pool.Fori(0, BATCH - 1) as b:
                    for i in range(1, TPB + 1):
                        tile(b * TPB + i, b, i)
                for i in range(1, TPB):
                    tile((BATCH - 1) * TPB + i, BATCH - 1, i)

            @block.tensor
            def _(pe):
                pe.wait_ge(w_in, 64)
                for j in range(FB):
                    pe.matmul(ps[:, KV[j], 0:BATCH * KEYS], wk[:, j * P:(j + 1) * P], c.ctxT[:].rearrange("p b k -> p (b k)"),
                              start=True, stop=True).then_inc(k_done, 1)
                for b in range(BATCH):
                    if FB > 1:
                        pe.wait_ge(kT_ready, b + 1)
                    at = ps[0:KEYS, KV[1], b * P:(b + 1) * P] if FB == 1 else ps[0:KEYS, KV[b], :]
                    pe.matmul(at, c.ctxT[:, b, :], wv[:], start=True, stop=True).then_inc(v_done, 1)
                norm.tensor(pe)

                def queries(b, j):
                    if j > 0:
                        pe.wait_ge(q_ready, b * FB + j)
                    pe.matmul(ps[:, Q, :], wq[:, j * P:(j + 1) * P], c.normT[:, bass.ds(b * SEQ, SEQ)], start=True, stop=True).then_inc(q_done, 1)

                def scores(n, b, i):
                    if i % TPB == 0:
                        pe.wait_ge(q_ready, b * FB + FB)
                    if later(n, -1):
                        pe.wait_ge(score_read, n)
                    t = i % TPB * P
                    keys = kdiag[:, bass.ds(b, 1)]
                    if FB == 1:
                        for a, e in cuts:
                            last = pe.matmul(flat[:, a:e], qT[:, 0, t:t + P], keys.rearrange("p b j h k -> p (b j h k)")[:, a:e], start=True, stop=True)
                    else:
                        for j in range(FB):
                            last = pe.matmul(ps[:, j // 2, j % 2 * HB * KEYS:(j % 2 + 1) * HB * KEYS], qT[:, j, t:t + P],
                                             keys[:, :, j].rearrange("p b h k -> p (b h k)"), start=True, stop=True)
                    last.then_inc(scored, 1)

                def turn(n, i, g):
                    pe.wait_ge(normed, n * 2 + g * 2 // GROUPS + 1)
                    if g >= 2:
                        pe.wait_ge(turn_read, n * GROUPS + g - 1)
                    for a in range(GROUP):
                        h = g * GROUP + a
                        last = pe.transpose(ps[0:KEYS, TURN + g % 2, a * P:(a + 1) * P], prob[:, i % PROBS, h * KEYS:(h + 1) * KEYS], c.ident[:])
                    last.then_inc(turned, 1)

                def product(n, b, i, g):
                    if g == 0 and i % TPB == 0:
                        pe.wait_ge(v_placed, b + 1)
                    pe.wait_ge(turn_read, n * GROUPS + g + 1)
                    for a in range(GROUP):
                        h = g * GROUP + a
                        if FB == 1:
                            last = pe.matmul(ps[a * COLS:(a + 1) * COLS, PV, 0:P], v_now[:, h, :], probT[:, h, :], start=(g == 0), stop=(g == GROUPS - 1))
                        else:
                            last = pe.matmul(ps[h % 2 * D:(h % 2 + 1) * D, PV, h // 2 * P:(h // 2 + 1) * P], v_now[:, h, :], probT[:, h, :], start=True, stop=True)
                    if g == GROUPS - 1:
                        last.then_inc(pv_done, 1)

                def output(n):
                    pe.wait_ge(mixed_ready, n + 1)
                    pe.wait_ge(y_added, n + 1)
                    for j in range(FB):
                        last = pe.matmul(ps[:, Y, 0:P], mixedT[:, j * P:(j + 1) * P], wo[:, j, :], start=(j == 0), stop=(j == FB - 1))
                    last.then_inc(y_done, 1)

                def tile(n, b, i):
                    now = b + i // TPB
                    project = list(range(FB)) if not isinstance(n, int) and i == 1 else []

                    def next_queries():
                        if project:
                            queries(b + 1, project.pop(0))

                    next_queries()
                    turn(n, i, 0)
                    next_queries()
                    turn(n, i, 1)
                    next_queries()
                    if later(n, -1):
                        output(n - 1)
                    product(n, now, i, 0)
                    next_queries()
                    for g in range(1, GROUPS):
                        if g + 1 < GROUPS:
                            turn(n, i, g + 1)
                        product(n, now, i, g)
                    if later(n, 3):
                        scores(n + 3, b + (i + 3) // TPB, i + 3)

                pe.wait_ge(kdiag_ready, BATCH * FB)
                pe.wait_ge(v_ready, GROUP)
                norm.wait(pe, 0)
                for j in range(FB):
                    queries(0, j)
                for n in range(3):
                    scores(n, 0, n)
                norm.wait(pe)
                tile(0, 0, 0)
                with pe.Fori(0, BATCH - 1) as b:
                    for i in range(1, TPB + 1):
                        tile(b * TPB + i, b, i)
                for i in range(1, TPB):
                    tile((BATCH - 1) * TPB + i, BATCH - 1, i)
                output(TILES - 1)

            @block.scalar
            def _(act):
                if biased:
                    act.wait_ge(k_done, 1)
                    act.activation(kT[:, 0, :], ps[:, KV[0], 0:BATCH * KEYS], ACT.Identity, bias=c.vec(f"{tag}_bk")).then_inc(kT_ready, 1)
                else:
                    for j in range(FB):
                        act.wait_ge(k_done, j + 1)
                        act.activation(kT[:, j, :], ps[:, KV[j], 0:BATCH * KEYS], ACT.Copy).then_inc(kT_ready, 1)
                norm.scalar(act)

                def queries(b, j):
                    act.wait_ge(q_done, b * FB + j + 1)
                    if biased:
                        act.activation(qT[:, j, :], ps[:, Q, :], ACT.Identity, bias=bq[:], scale=score_scale).then_inc(q_ready, 1)
                    else:
                        act.activation(qT[:, j, :], ps[:, Q, :], ACT.Copy, scale=score_scale).then_inc(q_ready, 1)

                def exps(n, i):
                    act.wait_ge(shifted, n + 1)
                    act.activation(prob[:, i % PROBS, :], prob[:, i % PROBS, :], ACT.Exp).then_inc(exped, 1)

                def group_turned(n, g):
                    act.wait_ge(turned, n * GROUPS + g + 1)
                    act.activation(probT[:, g * GROUP:(g + 1) * GROUP, :].rearrange("k h t -> k (h t)"), ps[0:KEYS, TURN + g % 2, :], ACT.Copy).then_inc(turn_read, 1)

                def mixed(n):
                    act.wait_ge(pv_done, n + 1)
                    act.activation(mixedT[:], ps[:, PV, 0:FB * P], ACT.Copy).then_inc(mixed_ready, 1)

                def tile(n, b, i):
                    project = list(range(FB)) if not isinstance(n, int) and i == 1 else []
                    for g in range(GROUPS):
                        if project:
                            queries(b + 1, project.pop(0))
                        group_turned(n, g)
                    for j in project:
                        queries(b + 1, j)
                    if later(n, 2):
                        exps(n + 2, i + 2)
                    mixed(n)

                if biased:
                    act.wait_ge(prepared, 1)
                for j in range(FB):
                    queries(0, j)
                exps(0, 0)
                exps(1, 1)
                tile(0, 0, 0)
                with act.Fori(0, BATCH - 1) as b:
                    for i in range(1, TPB + 1):
                        tile(b * TPB + i, b, i)
                for i in range(1, TPB):
                    tile((BATCH - 1) * TPB + i, BATCH - 1, i)

            @block.vector
            def _(dve):
                if biased:
                    dve.tensor_scalar(bq[:], c.vec(f"{tag}_bq"), score_scale, None, ALU.mult).then_inc(prepared, 1)
                if mask is not None:
                    dve.wait_ge(mask_in, 16)
                if mask == "barred":
                    dve.tensor_scalar(barred[:], keep[:], -1.0, 1e38, ALU.add, ALU.mult).then_inc(prepared, 1)
                dve.wait_ge(v_clear, 1)
                for g in range(GROUP):
                    if FB == 1:
                        dve.wait_ge(v_done, BATCH)
                        dve.tensor_tensor(v_all[:].rearrange("k b (g a) v -> k b g a v", g=GROUP)[:, :, g, :, g * D:(g + 1) * D],
                                          ps[0:KEYS, KV[1], :].rearrange("k (b a g v) -> k b g a v", b=BATCH, a=GROUP, g=GROUP)[:, :, g],
                                          bcast(c.row(f"{tag}_bv")[0:KEYS].rearrange("k (a g v) -> k g a v", a=GROUP, g=GROUP)[:, g], [BATCH, None, None]),
                                          ALU.add).then_inc(v_ready, 1)
                    else:
                        dve.wait_ge(v_done, g + 1)
                        dve.tensor_copy(v_all[:, g], ps[0:KEYS, KV[g], :].rearrange("k (h v) -> k h v", h=H)).then_inc(v_ready, 1)
                norm.vector(dve)
                step = InOrder(dve, order)

                def shift(n, b, i, base):
                    grid = prob[:, i % PROBS, :].rearrange("p (g h k) -> p g h k", g=G, k=KEYS)
                    best = top[:, i % 2, :].rearrange("p (g h) -> p g h", g=G)
                    dve.wait_ge(scored, n + 1)
                    source = heads
                    if mask == "scaled":
                        dve.scalar_tensor_tensor(out=grid.rearrange("p g h k -> p (g h) k"), in0=bcast(masks[:, bass.ds(n, 1), :].rearrange("p a k -> p (a k)"), [H, None]),
                                                 scalar=-1e9, in1=heads.rearrange("p g h k -> p (g h) k"), op0=ALU.mult, op1=ALU.add).then_inc(masked, 1)
                    if mask == "barred":
                        dve.tensor_tensor(grid, heads, bcast(barred[:, bass.ds(b, 1), :].rearrange("p b k -> p (b k)"), [G, H // G, None]),
                                          ALU.add).then_inc(masked, 1)
                    if mask is not None:
                        dve.wait_ge(masked, n + 1)
                        source = grid
                    step(dve.tensor_reduce(best, source, AX.X, ALU.max), base)
                    dve.tensor_tensor(grid, source, bcast(best, [None, None, KEYS]), ALU.subtract).then_inc(shifted, 1)

                def add_up(n, i, base):
                    dve.wait_ge(exped, n + 1)
                    for x in range(2):
                        half = slice(x * HALF, (x + 1) * HALF)
                        sums = rsum[:, i % PROBS, half]
                        step(dve.tensor_reduce(sums, prob[:, i % PROBS, :].rearrange("p (h k) -> p h k", h=H)[:, half], AX.X, ALU.add), base)
                        dve.reciprocal(sums, sums).then_inc(summed, 1)

                def add(n):
                    dve.wait_ge(y_done, n + 1)
                    x = c.resid[:, bass.ds(n, 1), :].rearrange("p t d -> p (t d)")
                    dve.tensor_tensor(x, ps[:, Y, 0:P], x, ALU.add).then_inc(y_added, 1)

                def tile(n, b, i, base):
                    if later(n, 2):
                        shift(n + 2, b + (i + 2) // TPB, i + 2, base)
                    if later(n, 1):
                        add_up(n + 1, i + 1, base)
                    if later(n, -1):
                        add(n - 1)

                dve.engine_nop().then_inc(y_added, 1)
                if mask == "barred":
                    dve.wait_ge(prepared, 1)
                shift(0, 0, 0, 0)
                shift(1, 0, 1, 0)
                add_up(0, 0, 0)
                tile(0, 0, 0, 0)
                if biased:
                    dve.wait_ge(bias_added, 1)
                first, PER = step.n, 3 * TPB
                with dve.Fori(0, BATCH - 1) as b:
                    step.n = first
                    for i in range(1, TPB + 1):
                        tile(b * TPB + i, b, i, b * PER)
                for i in range(1, TPB):
                    tile((BATCH - 1) * TPB + i, BATCH - 1, i, (BATCH - 2) * PER)
                add(TILES - 1)
                dve.wait_ge(y_added, TILES + 1)


class TopK:

    def __init__(self, c, ctx, tag, width, k):
        self.c, self.width, self.k = c, width, k
        self.top = c.sb(ctx, f"{tag}_top", [P, TILES, 8])
        self.place = c.sb(ctx, f"{tag}_place", [P, TILES, 8], U32)
        self.placef = c.sb(ctx, f"{tag}_placef", [P, TILES, 8])
        self.hit = c.sb(ctx, f"{tag}_hit", [P, TILES, width, k])

    def find(self, dve, step, rows):
        for n in range(TILES):
            last = dve.max(self.top[:, n, :], rows[:, n, :])
        step(last)
        for n in range(TILES):
            last = dve.max_index(self.place[:, n, :], self.top[:, n, :], rows[:, n, :])
        step(last)
        step(dve.tensor_copy(self.placef[:], self.place[:]))

    def spread(self, dve, step, weights, out):
        places = self.placef[:, :, 0:self.k]
        step(dve.tensor_tensor(self.hit[:], bcast(self.c.count12[:, 0:self.width], [TILES, None, self.k]),
                               bcast(places, [None, self.width, None]), ALU.is_equal))
        step(dve.tensor_tensor(self.hit[:], self.hit[:], bcast(weights, [None, self.width, None]), ALU.mult))
        step(dve.tensor_reduce(out, self.hit[:], AX.X, ALU.add))


class Softmax:

    def __init__(self, c, ctx, tag, n):
        self.c, self.n = c, n
        self.lead = c.sb(ctx, f"{tag}_lead", [P, TILES])
        self.exps = c.sb(ctx, f"{tag}_exps", [P, TILES, n])
        self.shifted, self.exped = c.sem(f"{tag}_rows_shifted"), c.sem(f"{tag}_rows_exped")

    def vector(self, dve, step, rows, lead=None):
        if lead is None:
            step(dve.tensor_reduce(self.lead[:], rows, AX.X, ALU.max))
            lead = self.lead[:]
        dve.tensor_tensor(self.exps[:], rows, bcast(lead, [None, self.n]), ALU.subtract).then_inc(self.shifted, 1)
        dve.wait_ge(self.exped, 1)
        step(dve.tensor_reduce(self.lead[:], self.exps[:], AX.X, ALU.add))
        step(dve.reciprocal(self.lead[:], self.lead[:]))
        step(dve.tensor_tensor(self.exps[:], self.exps[:], bcast(self.lead[:], [None, self.n]), ALU.mult))

    def scalar(self, act):
        act.wait_ge(self.shifted, 1)
        act.activation(self.exps[:], self.exps[:], ACT.Exp).then_inc(self.exped, 1)


class TopTwo:
    E, FIRST = 8, 0

    def __init__(self, c, ctx, norm):
        self.c, self.norm = c, norm
        self.wg = c.sb(ctx, "L0f_wg", [P, self.E])
        self.rows = c.sb(ctx, "L0f_rows", [P, TILES, self.E])
        self.weight = c.sb(ctx, "L0f_weight", [P, TILES, self.E])
        self.total = c.sb(ctx, "L0f_total", [P, TILES])
        self.own = c.sb(ctx, "L0f_own", [P, TILES, P])
        self.top = TopK(c, ctx, "L0f", self.E, 2)
        self.soft = Softmax(c, ctx, "L0f", 2)
        self.w_in, self.scored, self.order = c.sem("L0f_wg_in"), c.sem("L0f_scored"), c.sem("L0f_route_order")

    def sync(self, sp):
        sp.dma_start(self.wg[:], self.c.dram["L0f_wg"]).then_inc(self.w_in, 16)

    def tensor(self, pe):
        pe.wait_ge(self.w_in, 16)
        for n in range(TILES):
            last = pe.matmul(self.c.ps[:, 7, n * self.E:(n + 1) * self.E], self.c.normT[:, n * P:(n + 1) * P], self.wg[:], start=True, stop=True)
        last.then_inc(self.scored, 1)

    def scalar(self, act):
        self.soft.scalar(act)

    def vector(self, dve):
        c, norm, step = self.c, self.norm, InOrder(dve, self.order)
        dve.wait_ge(self.scored, 1)
        step(dve.tensor_tensor(self.rows[:], c.ps[:, 7, 0:TILES * self.E].rearrange("p (n e) -> p n e", n=TILES),
                               bcast(norm.std2[:], [None, self.E]), ALU.mult))
        self.top.find(dve, step, self.rows)
        self.soft.vector(dve, step, self.top.top[:, :, 0:2], self.top.top[:, :, 0])
        self.top.spread(dve, step, self.soft.exps[:], self.weight[:])
        step(dve.tensor_reduce(self.total[:], self.weight[:], AX.X, ALU.add))
        step(dve.tensor_tensor(self.total[:], self.total[:], norm.rstd[:], ALU.mult))
        step(dve.tensor_tensor(self.own[:], c.resid[:], bcast(norm.mean[:], [None, P]), ALU.subtract))
        step(dve.tensor_tensor(self.own[:], self.own[:], bcast(self.total[:], [None, P]), ALU.mult))
        step(dve.tensor_tensor(c.resid[:], c.resid[:], self.own[:], ALU.add))


class Sampled:
    E, FIRST = 8, 0
    HID, KMAX = 50, 6

    def __init__(self, c, ctx, norm):
        self.c = c
        self.wr = c.sb(ctx, "L1f_wr", [P, self.E])
        self.a1 = c.sb(ctx, "L1f_a1", [P, self.HID])
        self.a2 = c.sb(ctx, "L1f_a2", [self.HID, self.KMAX])
        self.hid = c.sb(ctx, "L1f_hid", [self.HID, TILES * P])
        self.rows = c.sb(ctx, "L1f_rows", [P, TILES, self.E])
        self.choice = c.sb(ctx, "L1f_choice", [P, TILES, 8])
        self.keep = c.sb(ctx, "L1f_keep", [P, TILES, self.E])
        self.weight = c.sb(ctx, "L1f_weight", [P, TILES, self.E])
        self.top = TopK(c, ctx, "L1f", self.E, self.E)
        self.pick = TopK(c, ctx, "L1f_pick", 8, 1)
        self.soft = Softmax(c, ctx, "L1f", self.E)
        self.w_in, self.scored, self.order = c.sem("L1f_wr_in"), c.sem("L1f_scored"), c.sem("L1f_route_order")
        self.hid_done, self.hid_ready, self.filled = c.sem("L1f_actor_done"), c.sem("L1f_actor_ready"), c.sem("L1f_filled")

    def sync(self, sp):
        for sb, name in ((self.wr, "L1f_wr"), (self.a1, "L1f_a1"), (self.a2, "L1f_a2")):
            sp.dma_start(sb[:], self.c.dram[name]).then_inc(self.w_in, 16)

    def tensor(self, pe):
        c = self.c
        pe.wait_ge(self.w_in, 48)
        for b in range(BATCH):
            pe.matmul(c.ps[0:self.HID, b, :], self.a1[:], c.normT[:, b * SEQ:(b + 1) * SEQ], start=True, stop=True).then_inc(self.hid_done, 1)
        for n in range(TILES):
            last = pe.matmul(c.ps[:, 7, n * self.E:(n + 1) * self.E], c.normT[:, n * P:(n + 1) * P], self.wr[:], start=True, stop=True)
        last.then_inc(self.scored, 1)
        pe.wait_ge(self.hid_ready, BATCH)
        for n in range(TILES):
            last = pe.matmul(c.ps[:, 6, n * 8:n * 8 + self.KMAX], self.hid[:, n * P:(n + 1) * P], self.a2[:], start=True, stop=True)
        last.then_inc(self.scored, 1)

    def scalar(self, act):
        for b in range(BATCH):
            act.wait_ge(self.hid_done, b + 1)
            act.activation(self.hid[:, b * SEQ:(b + 1) * SEQ], self.c.ps[0:self.HID, b, :], ACT.Gelu_apprx_tanh,
                           bias=self.c.vec("L1f_b1")[0:self.HID]).then_inc(self.hid_ready, 1)
        self.soft.scalar(act)

    def vector(self, dve):
        c, step = self.c, InOrder(dve, self.order)
        step(dve.memset(self.choice[:], -1e30))
        dve.wait_ge(self.scored, 1)
        step(dve.tensor_copy(self.rows[:], c.ps[:, 7, 0:TILES * self.E].rearrange("p (n e) -> p n e", n=TILES)))
        self.soft.vector(dve, step, self.rows[:])
        self.top.find(dve, step, self.soft.exps)
        dve.wait_ge(self.scored, 2)
        logits = self.choice[:, :, 0:self.KMAX]
        step(dve.tensor_tensor(logits, c.ps[:, 6, 0:TILES * 8].rearrange("p (n k) -> p n k", n=TILES)[:, :, 0:self.KMAX],
                               bcast(c.row("L1f_b2")[:, 0:self.KMAX], [TILES, None]), ALU.add))
        step(dve.tensor_scalar(logits, logits, -30.0, 30.0, ALU.max, ALU.min))
        self.pick.find(dve, step, self.choice)
        step(dve.tensor_tensor(self.keep[:], bcast(c.count12[:, 0:self.E], [TILES, None]),
                               bcast(self.pick.placef[:, :, 0], [None, self.E]), ALU.is_le))
        step(dve.tensor_tensor(self.keep[:], self.keep[:], self.top.top[:], ALU.mult))
        self.top.spread(dve, step, self.keep[:], self.weight[:])


class TopProbs:
    E, FIRST = 9, 1

    def __init__(self, c, ctx, norm):
        self.c = c
        self.wr = c.sb(ctx, "L3f_wr", [P, 8])
        self.rows = c.sb(ctx, "L3f_rows", [P, TILES, 8])
        self.weight = c.sb(ctx, "L3f_weight", [P, TILES, 9])
        self.top = TopK(c, ctx, "L3f", 8, 2)
        self.soft = Softmax(c, ctx, "L3f", 8)
        self.w_in, self.scored, self.order = c.sem("L3f_wr_in"), c.sem("L3f_scored"), c.sem("L3f_route_order")

    def sync(self, sp):
        sp.dma_start(self.wr[:], self.c.dram["L3f_wr"]).then_inc(self.w_in, 16)

    def tensor(self, pe):
        pe.wait_ge(self.w_in, 16)
        for n in range(TILES):
            last = pe.matmul(self.c.ps[:, 7, n * 8:(n + 1) * 8], self.c.normT[:, n * P:(n + 1) * P], self.wr[:], start=True, stop=True)
        last.then_inc(self.scored, 1)

    def scalar(self, act):
        self.soft.scalar(act)

    def vector(self, dve):
        c, step = self.c, InOrder(dve, self.order)
        step(dve.memset(self.weight[:], 1.0))
        dve.wait_ge(self.scored, 1)
        step(dve.tensor_tensor(self.rows[:], c.ps[:, 7, 0:TILES * 8].rearrange("p (n e) -> p n e", n=TILES),
                               bcast(c.row("L3f_rb")[:, 0:8], [TILES, None]), ALU.add))
        self.soft.vector(dve, step, self.rows[:])
        self.top.find(dve, step, self.soft.exps)
        self.top.spread(dve, step, self.top.top[:, :, 0:2], self.weight[:, :, 1:9])


def experts(c, tag, router_kind, kind, R, F, inner_eps=None):
    nc, ps = c.nc, c.ps
    gated, folded = kind == "swiglu", kind == "relu"
    W1 = 2 * R * F if gated else R * F
    GAIN, SHIFT = W1 + F, W1 + F + 1
    PACKED = {"relu": SHIFT + 1, "gelu": W1 + F, "swiglu": W1}[kind]
    SLOTS = F if gated else 4
    YBANK = 6 if gated else 4
    func = {"relu": ACT.Relu, "gelu": ACT.Gelu, "swiglu": ACT.Silu}[kind]
    with ExitStack() as ctx:
        norm = Norm(c, ctx, tag, inner_eps)
        route = router_kind(c, ctx, norm)
        E = route.E
        PAIRS = E // HALVES
        tail_expert = E % HALVES
        w1 = c.sb(ctx, f"{tag}_w1", [P, HALVES, PACKED])
        w2 = c.sb(ctx, f"{tag}_w2", [R, HALVES, F, P])
        hid = c.sb(ctx, f"{tag}_hidden", [R, HALVES, F, SEQ])
        w1g = c.sb(ctx, f"{tag}_w1g", [P, HALVES, W1]) if folded else w1
        b1 = c.sb(ctx, f"{tag}_b1", [P, HALVES, F]) if folded else None
        gate = c.sb(ctx, f"{tag}_gate", [R, F, SEQ]) if gated else None
        w_in = c.pair(f"{tag}_w_in")
        hid_done, gate_ready, hid_ready = (c.sem(f"{tag}_{n}") for n in ("hid_done", "gate_ready", "hid_ready"))
        out_done, out_added = c.sem(f"{tag}_out_done"), c.pair(f"{tag}_out_added")
        scaled, shift_done, shift_ready = c.sem(f"{tag}_scaled"), c.sem(f"{tag}_shift_done"), c.sem(f"{tag}_shift_ready")
        if not gated:
            b2 = c.sb(ctx, f"{tag}_b2", [E, P])
            weightT = c.sb(ctx, f"{tag}_weightT", [E, TILES * P])
            b2_in, wT_done, wT_ready, b2_done = (c.sem(f"{tag}_{n}") for n in ("b2_in", "wT_done", "wT_ready", "b2_done"))
        routed = c.sem(f"{tag}_routed")
        MM = 2 if gated else 1

        def steps(eng, make, use):
            def run(q, us, after):
                at = [(q, u, b) for u in us for b in range(BATCH)]
                for now, then in zip(at, at[1:] + [after]):
                    if then is not None:
                        make(*then)
                    use(*now)

            make(0, 0, 0)
            with eng.Fori(0, PAIRS - 1) as q:
                run(q, range(HALVES), (q + 1, 0, 0))
            run(PAIRS - 1, range(HALVES), (PAIRS, 0, 0) if tail_expert else None)
            if tail_expert:
                run(PAIRS, range(1), None)

        with nc.Block() as block:
            @block.sync
            def _(sp):
                def load(e, u):
                    sp.dma_start(w1[:, u, :], c.dram[f"{tag}_{'gu' if gated else 'w1'}"][bass.ds(e, 1)].rearrange(
                        "e d g f -> (e d) (g f)" if gated else "e d f -> (e d) f")).then_inc(w_in[u], 16)
                    sp.dma_start(w2[:, u], c.dram[f"{tag}_{'dn' if gated else 'w2'}"][bass.ds(e, 1)].rearrange(
                        "e r f d -> (e r) f d")).then_inc(w_in[u], 16)

                route.sync(sp)
                if not gated:
                    sp.dma_start(b2[:], c.dram[f"{tag}_b2"]).then_inc(b2_in, 16)
                for u in range(HALVES):
                    load(u, u)
                with sp.Fori(1, PAIRS) as q:
                    for u in range(HALVES):
                        sp.wait_ge(out_done, (q * HALVES + u - 1) * BATCH)
                        load(q * HALVES + u, u)
                if tail_expert:
                    sp.wait_ge(out_done, (E - 2) * BATCH)
                    load(E - 1, 0)

            if folded:
                @block.gpsimd
                def _(pool):
                    with pool.Fori(0, PAIRS) as q:
                        for u in range(HALVES):
                            pool.wait_ge(w_in[u], q * 32 + 32)
                            pool.tensor_tensor(w1g[:, u, :], w1[:, u, 0:W1], w1[:, u, GAIN:GAIN + 1].broadcast_to([P, W1]), ALU.mult).then_inc(scaled, 1)

            @block.tensor
            def _(pe):
                norm.tensor(pe)
                norm.wait(pe)
                route.tensor(pe)
                if gated:
                    pe.wait_ge(routed, 1)

                def hidden(q, u, b):
                    e = q * HALVES + u
                    s = e * BATCH + b
                    if b == 0:
                        pe.wait_ge(w_in[u], q * 32 + 32)
                        if folded:
                            pe.wait_ge(scaled, e + 1)
                            pe.wait_ge(shift_ready, e)
                            for f in range(F):
                                last = pe.matmul(ps[:, 6, f:f + 1], w1[:, u, f * R:(f + 1) * R],
                                                 w1[:, u, SHIFT:SHIFT + 1], start=True, stop=True)
                            last.then_inc(shift_done, 1)
                    pe.wait_ge(hid_ready, s * F)
                    for f in range(F):
                        slot = (b * F + f) % SLOTS
                        for m in range(MM):
                            pe.matmul(ps[0:R, m * SLOTS + slot, :], w1g[:, u, (m * F + f) * R:(m * F + f + 1) * R],
                                      c.normT[:, b * SEQ:(b + 1) * SEQ], start=True, stop=True).then_inc(hid_done, 1)

                def result(q, u, b):
                    s = (q * HALVES + u) * BATCH + b
                    pe.wait_ge(hid_ready, s * F + F)
                    pe.wait_ge(out_added[b % 2], (q * HALVES + u) * (BATCH // 2) + b // 2)
                    for t in range(TPB):
                        for f in range(F):
                            last = pe.matmul(ps[:, YBANK + b % 2, t * P:(t + 1) * P], hid[:, b % 2, f, t * P:(t + 1) * P],
                                             w2[:, u, f, :], start=(f == 0), stop=(f == F - 1))
                    last.then_inc(out_done, 1)

                steps(pe, hidden, result)

                if not gated:
                    pe.wait_ge(b2_in, 16)
                    pe.wait_ge(routed, 1)
                    pe.wait_ge(hid_ready, E * BATCH * F)
                    for n in range(TILES):
                        last = pe.transpose(ps[0:E, n // TPB, n % TPB * P:(n % TPB + 1) * P], route.weight[:, n, :], c.ident[:])
                        if n % TPB == TPB - 1:
                            last.then_inc(wT_done, 1)
                    for b in range(BATCH):
                        pe.wait_ge(wT_ready, b + 1)
                        pe.wait_ge(out_added[b % 2], E * (BATCH // 2) + b // 2)
                        for t in range(TPB):
                            last = pe.matmul(ps[:, YBANK + b % 2, t * P:(t + 1) * P], weightT[:, (b * TPB + t) * P:(b * TPB + t + 1) * P],
                                             b2[:], start=True, stop=True)
                        last.then_inc(b2_done, 1)

            @block.scalar
            def _(act):
                norm.scalar(act)
                route.scalar(act)

                def activate(q, u, b):
                    e = q * HALVES + u
                    s = e * BATCH + b
                    if folded and b == 0:
                        act.wait_ge(shift_ready, e + 1)
                    for f in range(F):
                        slot = (b * F + f) % SLOTS
                        act.wait_ge(hid_done, (s * F + f) * MM + 1)
                        if gated:
                            act.activation(gate[:, f, :], ps[0:R, slot, :], func).then_inc(gate_ready, 1)
                        else:
                            bias = b1[:, u, f:f + 1] if folded else w1[:, u, W1 + f:W1 + f + 1]
                            act.activation(hid[:, b % 2, f, :], ps[0:R, slot, :], func, bias=bias).then_inc(hid_ready, 1)

                steps(act, activate, lambda q, u, b: None)
                if not gated:
                    for b in range(BATCH):
                        act.wait_ge(wT_done, b + 1)
                        act.activation(weightT[:, b * SEQ:(b + 1) * SEQ], ps[0:E, b, :], ACT.Copy).then_inc(wT_ready, 1)

            @block.vector
            def _(dve):
                norm.vector(dve)
                route.vector(dve)
                dve.engine_nop().then_inc(routed, 1)
                flat = route.weight[:].rearrange("p n e -> p (n e)")

                def add(q, u, b):
                    e = q * HALVES + u
                    s = e * BATCH + b
                    dve.wait_ge(out_done, s + 1)
                    dve.wait_ge(out_added[b % 2], e * (BATCH // 2) + b // 2)
                    for t in range(TPB):
                        n = b * TPB + t
                        last = dve.scalar_tensor_tensor(out=c.resid[:, n, :], in0=ps[:, YBANK + b % 2, t * P:(t + 1) * P],
                                                        scalar=flat[:, bass.ds(n * E + e, 1)], in1=c.resid[:, n, :],
                                                        op0=ALU.mult, op1=ALU.add)
                    last.then_inc(out_added[b % 2], 1)

                def finish_hidden(q, u, b):
                    e = q * HALVES + u
                    s = e * BATCH + b
                    if folded and b == 0:
                        dve.wait_ge(shift_done, e + 1)
                        dve.tensor_tensor(b1[:, u, :], ps[:, 6, 0:F], w1[:, u, W1:W1 + F], ALU.add).then_inc(shift_ready, 1)
                    for f in range(F if gated else 0):
                        dve.wait_ge(gate_ready, s * F + f + 1)
                        dve.wait_ge(hid_done, (s * F + f) * MM + 2)
                        dve.tensor_tensor(hid[:, b % 2, f, :], gate[:, f, :], ps[0:R, SLOTS + f, :], ALU.mult).then_inc(hid_ready, 1)

                steps(dve, finish_hidden, add)
                if not gated:
                    for b in range(BATCH):
                        dve.wait_ge(b2_done, b + 1)
                        x = c.resid[:, b * TPB:(b + 1) * TPB, :]
                        dve.tensor_tensor(x, ps[:, YBANK + b % 2, :].rearrange("p (t d) -> p t d", t=TPB), x, ALU.add).then_inc(out_added[b % 2], 1)
                for h in range(2):
                    dve.wait_ge(out_added[h], E * 2 + (0 if gated else 2))


def latent_attention(c):
    nc, ps = c.nc, c.ps
    PAIRS, D = 8, 64
    NK = SEQ + KEYS
    KB = 5
    BK = (NK + KB - 1) // KB
    STEPS = 2 * TPB
    TURNS = PAIRS * BATCH
    RING = 4
    AHEAD = 3
    Q, V4, NORMS, Y, V1, KL, KC, NKL = range(STEPS)
    FOR = {Q: 1, V4: 1, NORMS: 1, Y: -1, V1: 1, KL: 2, KC: 2, NKL: 2}
    PROLOGUE = [(KL, 0), (KC, 0), (NKL, 0), (Q, 0), (V4, 0), (NORMS, 0), (V1, 0), (KL, 1), (KC, 1), (NKL, 1)]
    with ExitStack() as ctx:
        norm = Norm(c, ctx, "L1", inner_eps=1e-5, gain=c.vec("L1_lg"), shift=c.vec("L1_lb"))
        keysT = c.sb(ctx, "L1_keysT", [P, BATCH, KB * BK])
        w_all = c.sb(ctx, "L1_w_all", [P, PAIRS + 1, 3, P])
        wq, wk = c.sb(ctx, "L1_wq", [P, P]), c.sb(ctx, "L1_wk", [P, P])
        wo = c.sb(ctx, "L1_wo", [P, PAIRS + 1, P])
        keep, barred = c.sb(ctx, "L1_keep", [P, BATCH, KEYS], U8), c.sb(ctx, "L1_barred", [P, BATCH, KEYS])
        cx, cstage = c.sb(ctx, "L1_cx", [KEYS, BATCH, P]), c.sb(ctx, "L1_cstage", [KEYS, BATCH, P])
        cstats, cwork = c.sb(ctx, "L1_cstats", [KEYS, BATCH, 6]), c.sb(ctx, "L1_cwork", [KEYS, 6, BATCH])
        gains = c.sb(ctx, "L1_gains", [P, 1])
        q2, kT = c.sb(ctx, "L1_q2", [P, 2, 2, SEQ]), c.sb(ctx, "L1_kT", [P, 2, NK])
        v, qinv = c.sb(ctx, "L1_v", [BK, 2, KB, P]), c.sb(ctx, "L1_qinv", [P, 2, STEPS])
        ksq, qsq = c.sb(ctx, "L1_ksq", [P, NK]), c.sb(ctx, "L1_qsq", [P, SEQ])
        kinv, qms = c.sb(ctx, "L1_kinv", [P, NK]), c.sb(ctx, "L1_qms", [P, STEPS])
        top, low, sums, rsums = (c.sb(ctx, f"L1_{n}", [P, RING]) for n in ("top", "low", "sums", "rsums"))
        prob, probT = c.sb(ctx, "L1_prob", [P, RING, KB * BK]), c.sb(ctx, "L1_probT", [BK, RING, KB, P])
        mixedT = c.sb(ctx, "L1_mixedT", [P, SEQ])
        w_in, ctx_in, keep_in, filled, tokens_in = (c.sem(f"L1_{n}") for n in ("w_in", "ctx_in", "keep_in", "filled", "tokens_in"))
        corder, cvar_ready, cstd_ready, cstaged, cturned, ctx_ready = (c.sem(f"L1_{n}") for n in (
            "corder", "cvar_ready", "cstd_ready", "cstaged", "cturned", "ctx_ready"))
        order, act_order, prepared, bias_added = (c.sem(f"L1_{n}") for n in ("order", "act_order", "prepared", "bias_added"))
        w_ready, side_done, side_read, squared = (c.sem(f"L1_{n}") for n in ("w_ready", "side_done", "side_read", "squared"))
        kinv_ready, qinv_ready, k_ready = (c.sem(f"L1_{n}") for n in ("kinv_ready", "qinv_ready", "k_ready"))
        scored, bounded, exped, summed, normed, turned, turn_read, mix_done, mixed_ready = (c.sem(f"L1_{n}") for n in (
            "scored", "bounded", "exped", "summed", "normed", "turned", "turn_read", "mix_done", "mixed_ready"))
        S = [ps[:, 2 * i:2 * i + 2, :].rearrange("p b n -> p (b n)") for i in range(2)]
        PT = ps[0:BK, 4:6, :].rearrange("p b n -> p (b n)")
        O, side = ps[:, 6, :], ps[:, 7, :]

        def use_of(turn, s):
            return len(PROLOGUE) + turn * STEPS + s

        def squares(turn, kind):
            return turn * 3 + {KL: 1, KC: 2, Q: 3}[kind]

        def scalings(turn, kind):
            return turn * 2 + {NKL: 1, NORMS: 2}[kind]

        def turns(eng, body):
            with eng.Fori(0, PAIRS) as p:
                for b in range(BATCH):
                    body(p, b, p * BATCH + b)

        def batch_of(b, kind):
            return (b + FOR[kind]) % BATCH

        with nc.Block() as block:
            @block.sync
            def _(sp):
                sp.dma_start(cx[:], c.dram["ctx"]).then_inc(ctx_in, 16)
                sp.dma_start(keep[:], c.dram["keep_L1"]).then_inc(keep_in, 16)
                weights = c.dram["L1_w"].rearrange("j p w f -> p j w f")
                sp.dma_start(w_all[:, 0:PAIRS], weights).then_inc(w_in, 16)
                sp.dma_start(w_all[:, PAIRS:PAIRS + 1], weights[:, 0:1]).then_inc(w_in, 16)
                out_rows = c.dram["L1_wo"].rearrange("j p d -> p j d")
                sp.dma_start(wo[:, 1:PAIRS + 1], out_rows).then_inc(w_in, 16)
                sp.dma_start(wo[:, 0:1], out_rows[:, 0:1]).then_inc(w_in, 16)

            @block.gpsimd
            def _(pool):
                pool.memset(q2[:], 0.0)
                pool.memset(prob[:], 0.0)
                pool.memset(v[:, 1], 0.0)
                pool.memset(keysT[:, :, NK:KB * BK], 0.0).then_inc(filled, 1)
                pool.memset(probT[:], 0.0).then_inc(turn_read, 1)

                def take_weights(to, p, kind):
                    pool.tensor_copy(to[:], w_all[:, bass.ds(p, 1), kind].rearrange("p j f -> p (j f)")).then_inc(w_ready, 1)

                pool.wait_ge(w_in, 64)
                take_weights(wk, 0, 1)
                take_weights(wq, 0, 0)

                def scale_keys(turn, w, kind):
                    a, e = (0, SEQ) if kind == NKL else (SEQ, NK)
                    pool.wait_ge(kinv_ready, scalings(turn, kind))
                    pool.tensor_tensor(kT[:, w, a:e], kT[:, w, a:e], kinv[:, a:e], ALU.mult).then_inc(k_ready, 1)

                def divide(now, s):
                    pool.wait_ge(summed, now + 1)
                    x = prob[:, s % RING, 0:NK]
                    pool.tensor_tensor(x, x, rsums[:, s % RING:s % RING + 1].broadcast_to([P, NK]), ALU.mult).then_inc(normed, 1)

                scale_keys(0, 0, NKL)
                scale_keys(0, 0, NORMS)
                norm.wait(pool)
                pool.tensor_tensor(c.resid[:], c.resid[:], bcast(c.row("L1_bout"), [TILES, None]), ALU.add).then_inc(bias_added, 1)
                for s in range(AHEAD - 1):
                    divide(s, s)

                def body(p, b, turn):
                    for s in range(STEPS):
                        if b == 2 and s == 0:
                            pool.wait_ge(side_done, use_of(turn, KC) - STEPS + 1)
                            take_weights(wk, p + 1, 1)
                        if b == 2 and s == 2:
                            pool.wait_ge(side_done, use_of(turn, Q) + 1)
                            take_weights(wq, p + 1, 0)
                        divide(turn * STEPS + s + AHEAD - 1, s + AHEAD - 1)
                        if s == 1:
                            scale_keys(turn + 1, (b + 1) % 2, NKL)
                        if s == 4:
                            scale_keys(turn + 1, (b + 1) % 2, NORMS)

                turns(pool, body)

            @block.tensor
            def _(pe):
                pe.wait_ge(cstaged, 1)
                for b in range(BATCH):
                    last = pe.transpose(ps[:, 2, b * KEYS:(b + 1) * KEYS], cstage[:, b, :], c.ident[0:KEYS, 0:KEYS])
                last.then_inc(cturned, 1)
                norm.tensor(pe)
                pe.wait_ge(tokens_in, BATCH)
                pe.wait_ge(ctx_ready, 1)
                pe.wait_ge(filled, 1)

                def use_side(kind, at, turn, b, p):
                    if not isinstance(at, int) or at > 0:
                        pe.wait_ge(side_read, at)
                    tokens, context = keysT[:, b, 0:SEQ], keysT[:, b, SEQ:NK]
                    if kind == KL:
                        last = pe.matmul(side, wk[:], tokens, start=True, stop=True)
                    elif kind == KC:
                        last = pe.matmul(side[:, 0:KEYS], wk[:], context, start=True, stop=True)
                    elif kind == Q:
                        last = pe.matmul(side, wq[:], tokens, start=True, stop=True)
                    elif kind == NKL:
                        pe.wait_ge(squared, squares(turn, KL))
                        last = pe.matmul(side, c.pairsum[:], ksq[:, 0:SEQ], start=True, stop=True)
                    elif kind == NORMS:
                        pe.wait_ge(squared, squares(turn, Q))
                        pe.matmul(side[:, 0:KEYS], c.pairsum[:], ksq[:, SEQ:NK], start=True, stop=True)
                        for t in range(TPB):
                            last = pe.matmul(side[:, P + 2 * t:P + 2 * t + 2], qsq[:, t * P:(t + 1) * P], c.pairsum[:, 0:P:D], start=True, stop=True)
                    elif kind == Y:
                        pe.wait_ge(mixed_ready, turn + 2)
                        for t in range(TPB):
                            last = pe.matmul(side[:, t * P:(t + 1) * P], mixedT[:, t * P:(t + 1) * P], wo[:, bass.ds(p, 1)].rearrange("p j d -> p (j d)"),
                                             start=True, stop=True)
                    else:
                        wv = w_all[:, bass.ds(p, 1), 2].rearrange("p j f -> p (j f)")
                        for k in range(KB - 1) if kind == V4 else [KB - 1]:
                            last = pe.matmul(side[0:BK, k % 4 * P:(k % 4 + 1) * P], keysT[:, b, k * BK:(k + 1) * BK], wv, start=True, stop=True)
                    last.then_inc(side_done, 1)

                def scores(turn, s, w):
                    if s == 0:
                        pe.wait_ge(k_ready, scalings(turn, NORMS))
                    q = q2[:, w, s % 2, s // 2 * P:(s // 2 + 1) * P]
                    pe.matmul(S[s % 2][:, 0:SEQ], q, kT[:, w, 0:SEQ], start=True, stop=True)
                    pe.matmul(S[s % 2][:, SEQ:NK], q, kT[:, w, SEQ:NK], start=True, stop=True).then_inc(scored, 1)

                def turn_step(now, s):
                    pe.wait_ge(normed, now + 1)
                    pe.wait_ge(turn_read, now + 1)
                    for k in range(KB):
                        last = pe.transpose(PT[:, k * P:(k + 1) * P], prob[:, s % RING, k * BK:(k + 1) * BK], c.ident[:])
                    last.then_inc(turned, 1)

                def product(now, t, w):
                    pe.wait_ge(turn_read, now + 1)
                    for k in range(KB):
                        for h in range(2):
                            last = pe.matmul(O[h * D:(h + 1) * D, t * P:(t + 1) * P], v[:, w, k, h * D:(h + 1) * D], probT[:, (2 * t + h) % RING, k, :],
                                             start=(k == 0), stop=(k == KB - 1))
                    if t == TPB - 1:
                        last.then_inc(mix_done, 1)

                pe.wait_ge(w_ready, 2)
                for at, (kind, turn) in enumerate(PROLOGUE):
                    use_side(kind, at, turn, turn, 0)
                for s in range(AHEAD):
                    if s == 2:
                        pe.wait_ge(exped, 1)
                    scores(0, s, 0)
                pe.wait_ge(turn_read, 1)
                pe.matmul(O, probT[:, 0, 0, :], probT[:, 0, 0:4].rearrange("k b t -> k (b t)"), start=True, stop=True)

                def body(p, b, turn):
                    w = b % 2
                    for s in range(STEPS):
                        now = turn * STEPS + s
                        turn_step(now, s)
                        to = s + AHEAD
                        pe.wait_ge(exped, now + AHEAD - 1)
                        scores(turn + to // STEPS, to % STEPS, (b + to // STEPS) % 2)
                        if s == 0:
                            product(now, TPB - 1, 1 - w)
                        elif s % 2 == 0:
                            if s == 2:
                                pe.wait_ge(mixed_ready, turn + 1)
                                pe.wait_ge(side_read, use_of(turn, V1) - STEPS + 1)
                            product(now, s // 2 - 1, w)
                        kind = s
                        if kind == KL and b == 2:
                            pe.wait_ge(w_ready, p * 2 + 3)
                        if kind == Q and b == 3:
                            pe.wait_ge(w_ready, p * 2 + 4)
                        pair = p + (b + FOR[kind]) // BATCH
                        use_side(kind, use_of(turn, s), turn + FOR[kind], batch_of(b, kind), pair + 1 if kind == Y else pair)

                turns(pe, body)
                product(TURNS * STEPS, TPB - 1, 1)
                use_side(Y, use_of(TURNS, 0), TURNS - 1, BATCH - 1, PAIRS)

            @block.scalar
            def _(act):
                act.wait_ge(cvar_ready, 1)
                act.activation(cwork[:, 4, :], cwork[:, 3, :], ACT.Sqrt).then_inc(cstd_ready, 1)
                act.wait_ge(cturned, 1)
                act.activation(keysT[:, :, SEQ:NK], ps[:, 2, 0:BATCH * KEYS].rearrange("p (b k) -> p b k", b=BATCH), ACT.Identity,
                               bias=c.vec("L1_xb"), scale=c.vec("L1_xg")).then_inc(ctx_ready, 1)
                norm.scalar(act)
                norm.wait(act)
                for b in range(BATCH):
                    act.activation(keysT[:, b, 0:SEQ], c.normT[:, b * SEQ:(b + 1) * SEQ], ACT.Copy).then_inc(tokens_in, 1)
                act.preload_act_table_set("natural_log_exp_and_others")
                step = InOrder(act, act_order)

                def square(kind, at, turn, w):
                    if kind == Q:
                        act.wait_ge(side_done, at + 1)
                        act.activation(qsq[:], side, ACT.Square).then_inc(squared, 1)
                    else:
                        act.wait_ge(side_read, at + 1)
                        a, e = (0, SEQ) if kind == KL else (SEQ, NK)
                        act.activation(ksq[:, a:e], kT[:, w, a:e], ACT.Square).then_inc(squared, 1)

                def invert(kind, at, w, base):
                    act.wait_ge(side_read, at + 1)
                    if kind == NKL:
                        step(act.activation(kinv[:, 0:SEQ], kinv[:, 0:SEQ], ACT.Ln), base)
                        act.activation(kinv[:, 0:SEQ], kinv[:, 0:SEQ], ACT.Exp, scale=-0.5).then_inc(kinv_ready, 1)
                    else:
                        act.activation(kinv[:, SEQ:NK], kinv[:, SEQ:NK], ACT.Ln)
                        step(act.activation(qms[:], qms[:], ACT.Ln), base)
                        act.activation(kinv[:, SEQ:NK], kinv[:, SEQ:NK], ACT.Exp, scale=-0.5).then_inc(kinv_ready, 1)
                        act.activation(qinv[:, w, :], qms[:], ACT.Exp, scale=-0.5).then_inc(qinv_ready, 1)

                def exps(now, s, w):
                    i = s % RING
                    act.wait_ge(bounded, now + 1)
                    act.activation(prob[:, i, 0:NK], S[s % 2][:, 0:NK], ACT.Exp, bias=low[:, i:i + 1], scale=qinv[:, w, s:s + 1],
                                   accum_out=sums[:, i:i + 1]).then_inc(exped, 1)

                def mixed(turn):
                    act.wait_ge(mix_done, turn + 1)
                    act.activation(mixedT[:], O, ACT.Copy).then_inc(mixed_ready, 1)

                act.wait_ge(filled, 1)
                for at, (kind, turn) in enumerate(PROLOGUE[:-1]):
                    if kind in (KL, KC, Q):
                        square(kind, at, turn, turn)
                    if kind in (NKL, NORMS):
                        invert(kind, at, turn, 0)
                for s in range(AHEAD - 1):
                    exps(s, s, 0)
                first, LINKS = step.n, 2

                def body(p, b, turn):
                    step.n = first
                    for s in range(STEPS):
                        at = use_of(turn, s) - 1
                        if s == Q + 1:
                            square(Q, at, turn + 1, None)
                        act.wait_ge(turned, turn * STEPS + s + 1)
                        act.activation(probT[:, s % RING].rearrange("k b t -> k (b t)"), PT[:, 0:KB * P], ACT.Copy).then_inc(turn_read, 1)
                        to = s + AHEAD - 1
                        exps(turn * STEPS + to, to % STEPS, (b + to // STEPS) % 2)
                        if s == 1:
                            mixed(turn)
                        if s == (NKL + 1) % STEPS:
                            invert(NKL, at, None, turn * LINKS)
                        if s == NORMS + 1:
                            invert(NORMS, at, (b + 1) % 2, turn * LINKS)
                        if s in (KL + 1, KC + 1):
                            square(s - 1, at, turn + 2, b % 2)

                turns(act, body)
                mixed(TURNS)

            @block.vector
            def _(dve):
                cstep = InOrder(dve, corder)
                dve.wait_ge(ctx_in, 16)
                for b in range(BATCH):
                    last = dve.bn_stats(cstats[:, b, :], cx[:, b, :])
                cstep(last)
                half, gap, spread, var, std, mean = (cwork[:, i, :] for i in range(6))
                dve.tensor_tensor(half, cstats[:, :, 1], cstats[:, :, 4], ALU.add)
                dve.tensor_tensor(spread, cstats[:, :, 2], cstats[:, :, 5], ALU.add)
                cstep(dve.tensor_tensor(gap, cstats[:, :, 1], cstats[:, :, 4], ALU.subtract))
                dve.tensor_scalar(mean, half, 0.5, None, ALU.mult)
                cstep(dve.tensor_tensor(gap, gap, gap, ALU.mult))
                cstep(dve.tensor_scalar(spread, spread, 1.0 / P, NORM_EPS, ALU.mult, ALU.add))
                dve.scalar_tensor_tensor(out=var, in0=gap, scalar=0.25, in1=spread, op0=ALU.mult, op1=ALU.add).then_inc(cvar_ready, 1)
                dve.wait_ge(cstd_ready, 1)
                cstep(dve.reciprocal(half, std))
                for b in range(BATCH):
                    last = dve.tensor_scalar(cstage[:, b, :], cx[:, b, :], mean[:, b:b + 1], half[:, b:b + 1], ALU.subtract, ALU.mult)
                last.then_inc(cstaged, 1)
                norm.vector(dve)
                dve.wait_ge(keep_in, 16)
                dve.tensor_scalar(barred[:], keep[:], -1.0, 1e30, ALU.add, ALU.mult).then_inc(prepared, 1)
                dve.tensor_tensor(gains[:], c.vec("L1_qg"), c.vec("L1_kg"), ALU.mult).then_inc(prepared, 1)
                dve.wait_ge(prepared, 2)
                dve.tensor_scalar(gains[:], gains[:], D ** -0.5, None, ALU.mult).then_inc(prepared, 1)
                dve.wait_ge(prepared, 3)
                dve.wait_ge(filled, 1)
                step = InOrder(dve, order)

                def bound(turn, s, b, base):
                    w, i = b % 2, s % RING
                    dve.wait_ge(scored, turn * STEPS + s + 1)
                    if s == 0:
                        dve.wait_ge(qinv_ready, turn + 1)
                    masked = S[s % 2][:, SEQ:NK]
                    step(dve.tensor_tensor(masked, masked, barred[:, b, :], ALU.add), base)
                    step(dve.tensor_reduce(top[:, i:i + 1], S[s % 2][:, 0:NK], AX.X, ALU.max), base)
                    dve.tensor_scalar(low[:, i:i + 1], top[:, i:i + 1], qinv[:, w, s:s + 1], -1.0, ALU.mult, ALU.mult).then_inc(bounded, 1)

                def invert_sum(now, s):
                    i = s % RING
                    dve.wait_ge(exped, now + 1)
                    dve.reciprocal(rsums[:, i:i + 1], sums[:, i:i + 1]).then_inc(summed, 1)

                def read_side(kind, at, turn, b):
                    w = b % 2
                    dve.wait_ge(side_done, at + 1)
                    if kind == Y:
                        x = c.resid[:, b * TPB:(b + 1) * TPB, :]
                        last = dve.tensor_tensor(x, side.rearrange("p (t d) -> p t d", t=TPB), x, ALU.add)
                    elif kind == KL:
                        last = dve.tensor_copy(kT[:, w, 0:SEQ], side)
                    elif kind == KC:
                        last = dve.tensor_copy(kT[:, w, SEQ:NK], side[:, 0:KEYS])
                    elif kind == Q:
                        dve.wait_ge(squared, squares(turn, Q))
                        dve.tensor_scalar(q2[0:D, w, 0, :], side[0:D, :], gains[0:D], None, ALU.mult)
                        last = dve.tensor_scalar(q2[D:P, w, 1, :], side[D:P, :], gains[D:P], None, ALU.mult)
                    elif kind == V4:
                        last = dve.tensor_copy(v[:, w, 0:KB - 1, :].rearrange("k b d -> k (b d)"), side[0:BK, :])
                    elif kind == V1:
                        last = dve.tensor_copy(v[:, w, KB - 1, :], side[0:BK, 0:P])
                    elif kind == NKL:
                        last = dve.tensor_scalar(kinv[:, 0:SEQ], side, 1.0 / D, 1e-16, ALU.mult, ALU.max)
                    else:
                        dve.tensor_scalar(kinv[:, SEQ:NK], side[:, 0:KEYS], 1.0 / D, 1e-16, ALU.mult, ALU.max)
                        last = dve.tensor_scalar(qms[:], side[:, P:P + STEPS], 1.0 / D, 1e-16, ALU.mult, ALU.max)
                    last.then_inc(side_read, 1)

                for at, (kind, turn) in enumerate(PROLOGUE[:-1]):
                    read_side(kind, at, turn, turn)
                for s in range(AHEAD):
                    if s > 0:
                        invert_sum(s - 1, s - 1)
                    bound(0, s, 0, 0)
                first, LINKS = step.n, 2 * STEPS
                dve.wait_ge(bias_added, 1)

                def body(p, b, turn):
                    step.n = first
                    for s in range(STEPS):
                        kind = (s - 1) % STEPS
                        ahead = FOR[kind] - (s == 0)
                        read_side(kind, use_of(turn, s) - 1, turn + ahead, (b + ahead) % BATCH)
                        to = s + AHEAD - 1
                        invert_sum(turn * STEPS + to, to)
                        to = s + AHEAD
                        bound(turn + to // STEPS, to % STEPS, (b + to // STEPS) % BATCH, turn * LINKS)

                turns(dve, body)
                read_side(NKL, use_of(TURNS, 0) - 1, TURNS + 1, 1)
                read_side(Y, use_of(TURNS, 0), TURNS - 1, BATCH - 1)
                dve.wait_ge(side_read, use_of(TURNS, 0) + 1)


def mixture_addressed(c):
    nc, ps, tag = c.nc, c.ps, "L2f"
    L, HID, ADDR, K = 12, 512, 64, 3
    FB = HID // P
    BANKS = 4
    TURN = 4
    with ExitStack() as ctx:
        norm = Norm(c, ctx, tag)
        pw, um = c.sb(ctx, "L2f_pw", [P, ADDR]), c.sb(ctx, "L2f_u", [ADDR, 3 * L])
        addr = c.sb(ctx, "L2f_addr", [ADDR, TILES * P])
        rows = c.sb(ctx, "L2f_rows", [P, 3, TILES, L])
        weight = c.sb(ctx, "L2f_weight", [P, 3, TILES, L])
        top = [TopK(c, ctx, f"L2f{r}", L, K) for r in range(3)]
        soft = [Softmax(c, ctx, f"L2f{r}", K) for r in range(3)]
        w1, w2 = c.sb(ctx, "L2f_w1", [P, HALVES, HID]), c.sb(ctx, "L2f_w2", [P, HALVES, FB, 2 * P])
        hid = c.sb(ctx, "L2f_hid", [P, TILES, HID])
        act_hid = c.sb(ctx, "L2f_act_hid", [P, HALVES, HID])
        hidT = c.sb(ctx, "L2f_hidT", [P, FB, TILES * P])
        b2, weightT = c.sb(ctx, "L2f_b2", [L, P]), c.sb(ctx, "L2f_weightT", [L, TILES * P])
        small_in, w1_in, w2_in = c.sem("L2f_small_in"), c.pair("L2f_w1_in"), c.pair("L2f_w2_in")
        addr_done, addr_ready, scored, order = (c.sem(f"L2f_{n}") for n in ("addr_done", "addr_ready", "scored", "order"))
        cleared, first_done, second_done = c.sem("L2f_cleared"), c.sem("L2f_first_done"), c.sem("L2f_second_done")
        first_added = [c.sem(f"L2f_first_added{i}") for i in range(BANKS)]
        second_added = [c.sem(f"L2f_second_added{i}") for i in range(BANKS)]
        gelu_ready, turned, turn_read = c.pair("L2f_gelu_ready"), c.pair("L2f_hid_turned"), c.pair("L2f_turn_read")
        third_ready, wT_done, wT_ready, b2_done = (c.sem(f"L2f_{n}") for n in ("third_ready", "wT_done", "wT_ready", "b2_done"))

        with nc.Block() as block:
            @block.sync
            def _(sp):
                for sb, name in ((pw, "L2f_pw"), (um, "L2f_u"), (b2, "L2f_b2")):
                    sp.dma_start(sb[:], c.dram[name]).then_inc(small_in, 16)

                def load1(e, u):
                    sp.dma_start(w1[:, u, :], c.dram["L2f_w1"][bass.ds(e, 1)].rearrange("e d f -> (e d) f")).then_inc(w1_in[u], 16)

                def load2(g, u):
                    sp.dma_start(w2[:, u], c.dram["L2f_w2"][bass.ds(g, 1)].rearrange("g p f e d -> (g p) f (e d)")).then_inc(w2_in[u], 16)

                for u in range(HALVES):
                    load1(u, u)
                    load2(u, u)
                with sp.Fori(1, L // HALVES) as q:
                    for u in range(HALVES):
                        sp.wait_ge(first_done, (q * HALVES + u - 1) * TILES)
                        load1(q * HALVES + u, u)
                with sp.Fori(1, L // 2 // HALVES) as q:
                    for u in range(HALVES):
                        sp.wait_ge(second_done, (q * HALVES + u - 1) * TILES)
                        load2(q * HALVES + u, u)

            @block.gpsimd
            def _(pool):
                pool.memset(hid[:], 0.0).then_inc(cleared, 1)

            @block.tensor
            def _(pe):
                norm.tensor(pe)
                norm.wait(pe)
                pe.wait_ge(small_in, 48)
                for b in range(BATCH):
                    pe.matmul(ps[0:ADDR, 4 + b % 2, :], pw[:], c.normT[:, b * SEQ:(b + 1) * SEQ], start=True, stop=True).then_inc(addr_done, 1)
                    pe.wait_ge(addr_ready, b + 1)
                for n in range(TILES):
                    last = pe.matmul(ps[:, 6 + n // 8, n % 8 * 64:n % 8 * 64 + 3 * L], addr[:, n * P:(n + 1) * P], um[:], start=True, stop=True)
                last.then_inc(scored, 1)
                with pe.Fori(0, L // HALVES) as q:
                    for u in range(HALVES):
                        pe.wait_ge(w1_in[u], q * 16 + 16)
                        for n in range(TILES):
                            pe.wait_ge(first_added[n % BANKS], (q * HALVES + u) * (TILES // BANKS) + n // BANKS)
                            pe.matmul(ps[:, n % BANKS, :], c.normT[:, n * P:(n + 1) * P], w1[:, u, :], start=True, stop=True).then_inc(first_done, 1)
                with pe.Fori(0, TILES // HALVES) as q:
                    for u in range(HALVES):
                        pe.wait_ge(gelu_ready[u], q + 1)
                        pe.wait_ge(turn_read[u], q)
                        for f in range(FB):
                            last = pe.transpose(ps[:, TURN + u, f * P:(f + 1) * P], act_hid[:, u, f * P:(f + 1) * P], c.ident[:])
                        last.then_inc(turned[u], 1)
                for u in range(HALVES):
                    pe.wait_ge(turn_read[u], TILES // HALVES)
                with pe.Fori(0, L // 2 // HALVES) as q:
                    for u in range(HALVES):
                        pe.wait_ge(w2_in[u], q * 16 + 16)
                        for n in range(TILES):
                            pe.wait_ge(second_added[n % BANKS], (q * HALVES + u) * (TILES // BANKS) + n // BANKS)
                            for f in range(FB):
                                last = pe.matmul(ps[:, n % BANKS, 0:2 * P], hidT[:, f, n * P:(n + 1) * P], w2[:, u, f, :], start=(f == 0), stop=(f == FB - 1))
                            last.then_inc(second_done, 1)
                pe.wait_ge(third_ready, 1)
                for b in range(BATCH):
                    for t in range(TPB):
                        last = pe.transpose(ps[0:L, 4 + b, t * P:(t + 1) * P], weight[:, 2, b * TPB + t, :], c.ident[:])
                    last.then_inc(wT_done, 1)
                for b in range(BATCH):
                    pe.wait_ge(second_added[b], L // 2 * (TILES // BANKS))
                    pe.wait_ge(wT_ready, b + 1)
                    for t in range(TPB):
                        last = pe.matmul(ps[:, b, t * P:(t + 1) * P], weightT[:, (b * TPB + t) * P:(b * TPB + t + 1) * P], b2[:], start=True, stop=True)
                    last.then_inc(b2_done, 1)

            @block.scalar
            def _(act):
                norm.scalar(act)
                for b in range(BATCH):
                    act.wait_ge(addr_done, b + 1)
                    act.activation(addr[:, b * SEQ:(b + 1) * SEQ], ps[0:ADDR, 4 + b % 2, :], ACT.Copy).then_inc(addr_ready, 1)
                for r in range(3):
                    soft[r].scalar(act)
                for i in range(BANKS):
                    act.wait_ge(first_added[i], L * (TILES // BANKS))
                with act.Fori(0, TILES // HALVES) as q:
                    for u in range(HALVES):
                        act.wait_ge(turned[u], q)
                        act.activation(act_hid[:, u, :], hid[:, bass.ds(q * HALVES + u, 1), :].rearrange("p a f -> p (a f)"),
                                       ACT.Gelu).then_inc(gelu_ready[u], 1)
                for b in range(BATCH):
                    act.wait_ge(wT_done, b + 1)
                    act.activation(weightT[:, b * SEQ:(b + 1) * SEQ], ps[0:L, 4 + b, :], ACT.Copy).then_inc(wT_ready, 1)

            @block.vector
            def _(dve):
                norm.vector(dve)
                step = InOrder(dve, order)
                dve.wait_ge(scored, 1)
                for r in range(3):
                    last = dve.tensor_copy(rows[:, r].rearrange("p (a n) e -> p a n e", a=2),
                                           ps[:, 6:8, :].rearrange("p a (n w) -> p a n w", n=8)[:, :, :, r * L:(r + 1) * L])
                step(last)

                def routed(r):
                    top[r].find(dve, step, rows[:, r])
                    soft[r].vector(dve, step, top[r].top[:, :, 0:K], top[r].top[:, :, 0])
                    top[r].spread(dve, step, soft[r].exps[:], weight[:, r])

                for r in range(3):
                    routed(r)
                dve.engine_nop().then_inc(third_ready, 1)
                flat = weight[:].rearrange("p r n e -> p (r n e)")
                dve.wait_ge(cleared, 1)
                with dve.Fori(0, L // HALVES) as q:
                    for u in range(HALVES):
                        e = q * HALVES + u
                        for n in range(TILES):
                            dve.wait_ge(first_done, e * TILES + n + 1)
                            dve.wait_ge(first_added[n % BANKS], e * (TILES // BANKS) + n // BANKS)
                            dve.scalar_tensor_tensor(out=hid[:, n, :], in0=ps[:, n % BANKS, :], scalar=flat[:, bass.ds(n * L + e, 1)], in1=hid[:, n, :],
                                                     op0=ALU.mult, op1=ALU.add).then_inc(first_added[n % BANKS], 1)
                with dve.Fori(0, TILES // HALVES) as q:
                    for u in range(HALVES):
                        dve.wait_ge(turned[u], q + 1)
                        dve.tensor_copy(hidT[:, :, bass.ds((q * HALVES + u) * P, P)], ps[:, TURN + u, :].rearrange("p (f t) -> p f t", f=FB)).then_inc(turn_read[u], 1)
                with dve.Fori(0, L // 2 // HALVES) as q:
                    for u in range(HALVES):
                        g = q * HALVES + u
                        for n in range(TILES):
                            dve.wait_ge(second_done, g * TILES + n + 1)
                            dve.wait_ge(second_added[n % BANKS], g * (TILES // BANKS) + n // BANKS)
                            for i in range(2):
                                ins = dve.scalar_tensor_tensor(out=c.resid[:, n, :], in0=ps[:, n % BANKS, i * P:(i + 1) * P],
                                                               scalar=flat[:, bass.ds(TILES * L + n * L + g * 2 + i, 1)], in1=c.resid[:, n, :],
                                                               op0=ALU.mult, op1=ALU.add)
                                if i == 0:
                                    ins.then_inc(order, 1)
                                    dve.wait_ge(order, step.n + g * TILES + n + 1)
                            ins.then_inc(second_added[n % BANKS], 1)
                for b in range(BATCH):
                    dve.wait_ge(b2_done, b + 1)
                    x = c.resid[:, b * TPB:(b + 1) * TPB, :]
                    dve.tensor_tensor(x, ps[:, b, :].rearrange("p (t d) -> p t d", t=TPB), x, ALU.add).then_inc(second_added[b], 1)
                for b in range(BATCH):
                    dve.wait_ge(second_added[b], L // 2 * (TILES // BANKS) + 1)


def program(nc, dram, out, layers=(0, 8)):
    with ExitStack() as ctx:
        c = Core(nc, ctx, dram, layers)
        constants(c)
        steps = [
            lambda: cross_attention(c, "L0", 16, 8, 8 ** -0.5, None),
            lambda: experts(c, "L0f", TopTwo, "relu", P, 4, inner_eps=1e-6),
            lambda: latent_attention(c),
            lambda: experts(c, "L1f", Sampled, "swiglu", 112, 3),
            lambda: cross_attention(c, "L2", 16, 8, 8 ** -0.5, "scaled"),
            lambda: mixture_addressed(c),
            lambda: cross_attention(c, "L3", 8, 64, 64 ** -0.5, "barred", inner_eps=1e-5, gain=c.vec("L3_g"), shift=c.vec("L3_b")),
            lambda: experts(c, "L3f", TopProbs, "gelu", P, 2),
        ]
        for step in steps[layers[0]:layers[1]]:
            taken = nc.snapshot_sems()
            step()
            c.retire(taken)
        stored = c.sem("stored")
        with nc.Block() as block:
            @block.sync
            def _(sp):
                sp.dma_start(out, c.resid[:]).then_inc(stored, 16)
                sp.wait_ge(stored, 16)


def laid_out(i):
    import numpy as np
    a = {k: np.asarray(v) for k, v in i.items()}
    cols = lambda v: v.reshape(-1, P).T
    twice = lambda v: np.tile(v, 2)[:, None]
    b1 = np.zeros((P, 1), np.float32)
    b1[:50, 0] = a["L1_ffn_actor_b1"]
    vecs = {
        "L0_bq": cols(a["L0_xattn_bq"]), "L0_bk": cols(a["L0_xattn_bk"]), "L2_bq": cols(a["L2_xattn_bq"]), "L2_bk": cols(a["L2_xattn_bk"]),
        "L1_xg": cols(a["L1_xattn_ln_x_g"]), "L1_xb": cols(a["L1_xattn_ln_x_b"]), "L1_lg": cols(a["L1_xattn_ln_l_g"]), "L1_lb": cols(a["L1_xattn_ln_l_b"]),
        "L1_qg": twice(a["L1_xattn_qn_g"]), "L1_kg": twice(a["L1_xattn_kn_g"]), "L1f_b1": b1,
        "L3_g": cols(a["L3_xattn_ln_gamma"]), "L3_b": cols(a["L3_xattn_ln_beta"]),
    }
    rows = np.zeros((len(ROWS), P), np.float32)
    for n, k in enumerate(["L0_xattn_bv", "L0_xattn_bo", "L1_xattn_bout", "L2_xattn_bv", "L2_xattn_bo", "L3_ffn_router_b", "L1_ffn_actor_b2"]):
        rows[n, :a[k].size] = a[k]
    E = 8
    packed = lambda w, b, *more: np.concatenate([w, b.reshape(len(b), -1, P).transpose(0, 2, 1), *(m[:, :, None] for m in more)], 2)
    both = lambda n: np.concatenate([a[f"L3_ffn_s{n}"][None], a[f"L3_ffn_r{n}"]])
    ctx = a["ctx_1024"]
    got = {
        "x": a["x"].reshape(TILES, P, P).transpose(1, 0, 2),
        "vecs": np.concatenate([vecs[k] for k in VECS], 1),
        "rows": np.broadcast_to(rows, (P, *rows.shape)),
        "ctxT": ctx.transpose(2, 0, 1),
        "ctx": ctx.transpose(1, 0, 2),
        **{f"L0_w{n}": a[f"L0_xattn_W{n}"].T for n in "qkv"}, "L0_wo": a["L0_xattn_Wo"].T[:, None],
        **{f"L2_w{n}": a[f"L2_xattn_w{n}"].T for n in "qkv"}, "L2_wo": a["L2_xattn_wo"].T[:, None],
        "L2_mask": a["mask_Bx1xSxS2_fk1"].reshape(TILES, P, KEYS).transpose(1, 0, 2),
        "keep_L1": np.broadcast_to(a["mask_BxS2_bf1"], (P, BATCH, KEYS)),
        "L3_mask": np.broadcast_to(a["mask_BxS2_bk0"], (P, BATCH, KEYS)),
        "L0f_wg": a["L0_ffn_Wg"], "L0f_w1": packed(a["L0_ffn_W1"], a["L0_ffn_b1"], a["L0_ffn_gamma"], a["L0_ffn_beta"]), "L0f_b2": a["L0_ffn_b2"],
        "L0f_w2": a["L0_ffn_W2"].reshape(E, 4, P, P).transpose(0, 2, 1, 3),
        "L1_w": np.stack([a["L1_xattn_Wq"].reshape(P, 8, P), a["L1_xattn_Wkv"][:, :1024].reshape(P, 8, P), a["L1_xattn_Wkv"][:, 1024:].reshape(P, 8, P)], 2).transpose(1, 0, 2, 3),
        "L1_wo": a["L1_xattn_Wout"].reshape(8, P, P),
        "L1f_wr": a["L1_ffn_router_w"].T, "L1f_a1": a["L1_ffn_actor_w1"].T, "L1f_a2": a["L1_ffn_actor_w2"].T,
        "L1f_gu": np.stack([a["L1_ffn_gate_w"].transpose(0, 2, 1), a["L1_ffn_up_w"].transpose(0, 2, 1)], 2),
        "L1f_dn": a["L1_ffn_down_w"].transpose(0, 2, 1).reshape(E, 3, 112, P).transpose(0, 2, 1, 3),
        "L2f_pw": a["L2_ffn_P_w"].T, "L2f_u": np.concatenate([a[f"L2_ffn_U{n}"] for n in (1, 2, 3)]).T,
        "L2f_w1": a["L2_ffn_W1"].transpose(0, 2, 1),
        "L2f_w2": a["L2_ffn_W2"].reshape(6, 2, P, 4, P).transpose(0, 4, 3, 1, 2),
        "L2f_b2": a["L2_ffn_b2"],
        "L3_wq": a["L3_xattn_Wq"], "L3_wk": a["L3_xattn_Wkv"][:, :512], "L3_wv": a["L3_xattn_Wkv"][:, 512:], "L3_wo": a["L3_xattn_Wout"].reshape(4, P, P).transpose(1, 0, 2),
        "L3f_wr": a["L3_ffn_router_w"], "L3f_b2": both("b2"), "L3f_w1": packed(both("w1"), both("b1")),
        "L3f_w2": both("w2").reshape(9, 2, P, P).transpose(0, 2, 1, 3),
    }
    return {k: np.ascontiguousarray(v) for k, v in got.items()}


def kernel(**inputs):
    import concourse.bacc as bacc
    from concourse.bass_utils import run_bass_kernel_spmd

    arrays = laid_out(inputs)
    nc = bacc.Bacc("TRN2", target_bir_lowering=False, num_devices=1)
    dram = {k: nc.dram_tensor(k, v.shape, mybir.dt.from_np(v.dtype), kind="ExternalInput").ap() for k, v in arrays.items()}
    out = nc.dram_tensor("out", (P, TILES, P), F32, kind="ExternalOutput").ap()
    program(nc, dram, out)
    done = run_bass_kernel_spmd(nc, [arrays], core_ids=[0])
    return done.results[0]["out"].transpose(1, 0, 2).reshape(BATCH, SEQ, P)
```

```python
from contextlib import ExitStack

import concourse.bass as bass
from concourse import mybir

F32 = mybir.dt.float32
U8 = mybir.dt.uint8
U32 = mybir.dt.uint32
ALU = mybir.AluOpType
ACT = mybir.ActivationFunctionType
AX = mybir.AxisListType

P = 128
BATCH, SEQ, KEYS = 4, 512, 77
TILES = BATCH * SEQ // P
TPB = SEQ // P
HALVES = 2
NORM_EPS = 1e-5

VECS = {}
for _name, _n in (("L0_bq", 1), ("L0_bk", 1), ("L2_bq", 1), ("L2_bk", 1), ("L1_xg", 1), ("L1_xb", 1), ("L1_lg", 1), ("L1_lb", 1), ("L1_qg", 1),
                  ("L1_kg", 1), ("L1f_b1", 1), ("L3_g", 1), ("L3_b", 1)):
    VECS[_name] = (sum(n for _, n in VECS.values()), _n)
NVEC = sum(n for _, n in VECS.values())
ROWS = ["L0_bv", "L0_bo", "L1_bout", "L2_bv", "L2_bo", "L3f_rb", "L1f_b2"]


class Core:

    def __init__(self, nc, ctx, dram, layers):
        self.nc, self.ctx, self.dram, self.layers = nc, ctx, dram, layers
        self.ps = ctx.enter_context(nc.psum_tensor("banks", [P, 8, 512], F32))
        self.resid = self.sb(ctx, "resid", [P, TILES, P])
        self.normT = self.sb(ctx, "normT", [P, TILES * P])
        self.ident = self.sb(ctx, "ident", [P, P])
        self.vecs = self.sb(ctx, "vecs", [P, NVEC])
        self.rows = self.sb(ctx, "rows", [P, len(ROWS), P])
        self.ctxT = self.sb(ctx, "ctxT", [P, BATCH, KEYS])
        self.head16 = self.sb(ctx, "head16", [P, 16])
        self.pairsum = self.sb(ctx, "pairsum", [P, P])
        self.count12 = self.sb(ctx, "count12", [P, 12])

    def sb(self, ctx, name, shape, dt=F32):
        return ctx.enter_context(self.nc.sbuf_tensor(f"sb_{name}", shape, dt))

    def sem(self, name):
        return self.nc.alloc_semaphore(name)

    def retire(self, before):
        self.nc.clear_and_free_semaphores(self.nc.allocated_since(before))
        self.nc.all_engine_barrier()

    def pair(self, name):
        return [self.sem(f"{name}{u}") for u in range(HALVES)]

    def vec(self, name, i=0):
        at = VECS[name][0] + i
        return self.vecs[:, at:at + 1]

    def row(self, name):
        return self.rows[:, ROWS.index(name), :]


class InOrder:

    def __init__(self, eng, sem):
        self.eng, self.sem, self.n = eng, sem, 0

    def __call__(self, ins, base=0):
        self.n += 1
        ins.then_inc(self.sem, 1)
        self.eng.wait_ge(self.sem, base + self.n)


def bcast(ap, dims):
    for i, d in enumerate(dims):
        if d is not None:
            ap = ap.unsqueeze(i + 1)
    shape = [ap.shape[0]] + [s if d is None else d for d, s in zip(dims, ap.shape[1:])]
    return ap.broadcast_to(shape)


def constants(c):
    nc, d = c.nc, c.dram
    loaded, built = c.sem("loaded"), c.sem("built")
    counts = c.ctx.enter_context(nc.sbuf_tensor("counts", [P, 12], mybir.dt.int32))
    with nc.Block() as block:
        @block.sync
        def _(sp):
            sp.dma_start(c.resid[:], d["x"]).then_inc(loaded, 16)
            sp.dma_start(c.vecs[:], d["vecs"]).then_inc(loaded, 16)
            sp.dma_start(c.rows[:], d["rows"]).then_inc(loaded, 16)
            sp.dma_start(c.ctxT[:], d["ctxT"]).then_inc(loaded, 16)
            sp.wait_ge(loaded, 64)

        @block.gpsimd
        def _(pool):
            step = InOrder(pool, built)
            pool.memset(c.ident[:], 0.0)
            pool.memset(c.head16[:], 1.0)
            pool.memset(c.pairsum[:], 0.0)
            step(pool.iota(counts[:], pattern=[[1, 12]], base=0, channel_multiplier=0))
            pool.tensor_copy(c.count12[:], counts[:])
            pool.affine_select(out=c.ident[:], in_=c.ident[:], compare_op=ALU.not_equal, fill=1.0, base=0,
                               pattern=[[-1, P]], channel_multiplier=1)
            step(pool.affine_select(out=c.head16[:], in_=c.head16[:], compare_op=ALU.is_ge, fill=0.0, base=0,
                                    pattern=[[-8, 16]], channel_multiplier=1))
            step(pool.affine_select(out=c.head16[:], in_=c.head16[:], compare_op=ALU.is_ge, fill=0.0, base=7,
                                    pattern=[[8, 16]], channel_multiplier=-1))
            step(pool.memset(c.pairsum[0:64, 0:64], 1.0))
            step(pool.memset(c.pairsum[64:128, 64:128], 1.0))


class Norm:

    def __init__(self, c, ctx, tag, inner_eps=None, gain=None, shift=None, banks=0):
        self.c, self.inner_eps, self.gain, self.shift = c, inner_eps, gain, shift
        self.banks = c.ps[:, banks:banks + HALVES, :]
        self.stats = c.sb(ctx, f"{tag}_stats", [P, TILES, 6])
        self.mean = c.sb(ctx, f"{tag}_mean", [P, TILES])
        self.var = c.sb(ctx, f"{tag}_var", [P, TILES])
        self.std = c.sb(ctx, f"{tag}_std", [P, TILES])
        self.std2 = c.sb(ctx, f"{tag}_std2", [P, TILES])
        self.rstd = c.sb(ctx, f"{tag}_rstd", [P, TILES])
        self.scale = c.sb(ctx, f"{tag}_scale", [P, TILES])
        self.bias = c.sb(ctx, f"{tag}_bias", [P, TILES])
        self.work = c.sb(ctx, f"{tag}_work", [P, 3, TILES])
        self.stage = c.sb(ctx, f"{tag}_stage", [P, HALVES, TPB, P])
        self.order = c.sem(f"{tag}_norm_order")
        self.var_ready, self.std_ready = c.sem(f"{tag}_var_ready"), c.sem(f"{tag}_std_ready")
        self.scaled, self.turned, self.ready = (c.sem(f"{tag}_{n}") for n in ("norm_scaled", "norm_turned", "norm_ready"))
        self.staged = c.pair(f"{tag}_norm_staged")

    def vector(self, dve):
        c, step = self.c, InOrder(dve, self.order)
        for n in range(TILES):
            last = dve.bn_stats(self.stats[:, n, :], c.resid[:, n, :])
        step(last)
        me, mo = self.stats[:, :, 1], self.stats[:, :, 4]
        half, gap, spread = (self.work[:, i, :] for i in range(3))
        dve.tensor_tensor(half, me, mo, ALU.add)
        dve.tensor_tensor(spread, self.stats[:, :, 2], self.stats[:, :, 5], ALU.add)
        step(dve.tensor_tensor(gap, me, mo, ALU.subtract))
        dve.tensor_scalar(self.mean[:], half, 0.5, None, ALU.mult)
        step(dve.tensor_tensor(gap, gap, gap, ALU.mult))
        step(dve.tensor_scalar(spread, spread, 1.0 / P, None, ALU.mult))
        step(dve.scalar_tensor_tensor(out=self.var[:], in0=gap, scalar=0.25, in1=spread, op0=ALU.mult, op1=ALU.add))
        dve.tensor_scalar(gap, self.var[:], NORM_EPS, None, ALU.add).then_inc(self.var_ready, 1)
        dve.wait_ge(self.std_ready, 1)
        step(dve.reciprocal(self.rstd[:], self.std[:]))
        if self.inner_eps is not None:
            step(dve.tensor_tensor(half, self.var[:], self.rstd[:], ALU.mult))
            step(dve.tensor_tensor(half, half, self.rstd[:], ALU.mult))
            dve.tensor_scalar(spread, half, self.inner_eps, None, ALU.add).then_inc(self.var_ready, 1)
            dve.wait_ge(self.std_ready, 2)
            step(dve.reciprocal(half, self.std2[:]))
            step(dve.tensor_tensor(self.scale[:], half, self.rstd[:], ALU.mult))
        scale = self.rstd if self.inner_eps is None else self.scale
        dve.scalar_tensor_tensor(out=self.bias[:], in0=self.mean[:], scalar=-1.0, in1=scale[:], op0=ALU.mult, op1=ALU.mult).then_inc(self.scaled, 1)
        for b in range(0, BATCH, HALVES):
            if b >= HALVES:
                dve.wait_ge(self.turned, b - HALVES + 1)
            for t in range(TPB):
                n = b * TPB + t
                last = dve.tensor_scalar(self.stage[:, 0, t, :], c.resid[:, n, :], self.mean[:, n:n + 1], scale[:, n:n + 1], ALU.subtract, ALU.mult)
            last.then_inc(self.staged[0], 1)

    def tensor(self, pe):
        for b in range(BATCH):
            pe.wait_ge(self.staged[b % HALVES], b // HALVES + 1)
            if b >= HALVES:
                pe.wait_ge(self.ready, b - HALVES + 1)
            for t in range(TPB):
                last = pe.transpose(self.banks[:, b % HALVES, t * P:(t + 1) * P], self.stage[:, b % HALVES, t, :], self.c.ident[:])
            last.then_inc(self.turned, 1)

    def scalar(self, act):
        act.wait_ge(self.var_ready, 1)
        act.activation(self.std[:], self.work[:, 1, :], ACT.Sqrt).then_inc(self.std_ready, 1)
        if self.inner_eps is not None:
            act.wait_ge(self.var_ready, 2)
            act.activation(self.std2[:], self.work[:, 2, :], ACT.Sqrt).then_inc(self.std_ready, 1)
        scale = self.rstd if self.inner_eps is None else self.scale
        act.wait_ge(self.scaled, 1)
        for b in range(BATCH):
            if b % HALVES == 0:
                for t in range(TPB):
                    n = (b + 1) * TPB + t
                    last = act.activation(self.stage[:, 1, t, :], self.c.resid[:, n, :], ACT.Identity, bias=self.bias[:, n:n + 1], scale=scale[:, n:n + 1])
                last.then_inc(self.staged[1], 1)
            act.wait_ge(self.turned, b + 1)
            out = self.c.normT[:, b * SEQ:(b + 1) * SEQ]
            if self.gain is None:
                ins = act.activation(out, self.banks[:, b % HALVES, :], ACT.Copy)
            else:
                ins = act.activation(out, self.banks[:, b % HALVES, :], ACT.Identity, bias=self.shift, scale=self.gain)
            ins.then_inc(self.ready, 1)

    def wait(self, eng, b=BATCH - 1):
        eng.wait_ge(self.ready, b + 1)


def cross_attention(c, tag, H, D, score_scale, mask, **norm_args):
    nc, ps = c.nc, c.ps
    FB = H * D // P
    HB = H // FB
    GROUP = 4
    COLS = P // GROUP if FB == 1 else D
    GROUPS = H // GROUP
    PROBS = TPB
    biased = FB == 1
    with ExitStack() as ctx:
        wq, wk, wv = (c.sb(ctx, f"{tag}_w{n}", [P, FB * P]) for n in "qkv")
        wo = c.sb(ctx, f"{tag}_wo", [P, FB, P])
        bq = c.sb(ctx, f"{tag}_bq", [P, 1])
        kT = c.sb(ctx, f"{tag}_kT", [P, FB, BATCH * KEYS])
        kdiag = c.sb(ctx, f"{tag}_kdiag", [P, BATCH, FB, HB, KEYS])
        v_all, v_now = c.sb(ctx, f"{tag}_v_all", [KEYS, BATCH, H, COLS]), c.sb(ctx, f"{tag}_v_now", [KEYS, H, COLS])
        qT = c.sb(ctx, f"{tag}_qT", [P, FB, SEQ])
        prob, top = c.sb(ctx, f"{tag}_prob", [P, PROBS, H * KEYS]), c.sb(ctx, f"{tag}_top", [P, HALVES, H])
        probT = c.sb(ctx, f"{tag}_probT", [KEYS, H, P])
        rsum = c.sb(ctx, f"{tag}_rsum", [P, PROBS, H])
        mixedT = c.sb(ctx, f"{tag}_mixedT", [P, FB * P])
        masks = c.sb(ctx, f"{tag}_masks", [P, TILES, KEYS]) if mask == "scaled" else None
        keep = c.sb(ctx, f"{tag}_keep", [P, BATCH, KEYS], U8) if mask == "barred" else None
        barred = c.sb(ctx, f"{tag}_barred", [P, BATCH, KEYS]) if mask == "barred" else None
        norm = Norm(c, ctx, tag, banks=3 if FB == 1 else 2, **norm_args)
        w_in, mask_in, order, prepared, bias_added = (c.sem(f"{tag}_{n}") for n in ("w_in", "mask_in", "order", "prepared", "bias_added"))
        k_done, kT_ready, kdiag_ready, v_done, v_clear, v_ready, v_placed = (c.sem(f"{tag}_{n}") for n in (
            "k_done", "kT_ready", "kdiag_ready", "v_done", "v_clear", "v_ready", "v_placed"))
        q_done, q_ready, scored, masked, shifted, exped = (c.sem(f"{tag}_{n}") for n in (
            "q_done", "q_ready", "scored", "masked", "shifted", "exped"))
        summed, normed, turned, turn_read, pv_done, mixed_ready, y_done, y_added = (c.sem(f"{tag}_{n}") for n in (
            "summed", "normed", "turned", "turn_read", "pv_done", "mixed_ready", "y_done", "y_added"))
        score_read = shifted if mask is None else masked
        PV, Y, Q = 5, 6, (7, 4)
        if FB == 1:
            K_AT, V_AT, TURN = (0,), Y, 3
            flat = ps[:, 0:3, :].rearrange("p b n -> p (b n)")[:, 0:H * KEYS]
            cuts = [(a, min(a + 512, H * KEYS)) for a in range(0, H * KEYS, 512)]
            heads = flat.rearrange("p (g h k) -> p g h k", g=1, h=H)
        else:
            K_AT, V_AT, TURN = (0, 1, 4, 5), (0, 1, 4, 5), 2
            heads = ps[:, 0:2, 0:H // 2 * KEYS].rearrange("p g (h k) -> p g h k", h=H // 2)
        G = heads.shape[1]
        HALF = H // 2

        def later(n, k):
            return not isinstance(n, int) or 0 <= n + k < TILES

        with nc.Block() as block:
            @block.sync
            def _(sp):
                for sb, name in ((wk, "wk"), (wv, "wv"), (wq, "wq"), (wo, "wo")):
                    sp.dma_start(sb[:], c.dram[f"{tag}_{name}"]).then_inc(w_in, 16)
                if mask is not None:
                    sp.dma_start((masks if keep is None else keep)[:], c.dram[f"{tag}_mask"]).then_inc(mask_in, 16)

            @block.gpsimd
            def _(pool):
                if biased:
                    pool.memset(v_all[:], 0.0).then_inc(v_clear, 1)
                member = c.head16[:].rearrange("p (a g) -> p g a", g=GROUP) if FB == 1 else c.pairsum[:, 0:P:D].unsqueeze(1)
                for j in range(FB):
                    pool.wait_ge(kT_ready, j + 1)
                    for b in range(BATCH):
                        pool.tensor_tensor(kdiag[:, b, j].rearrange("p (g a) k -> p g a k", g=member.shape[1]),
                                           bcast(kT[:, j, b * KEYS:(b + 1) * KEYS], list(member.shape[1:]) + [None]),
                                           bcast(member, [None, None, KEYS]), ALU.mult).then_inc(kdiag_ready, 1)
                if biased:
                    norm.wait(pool)
                    pool.tensor_tensor(c.resid[:], c.resid[:], bcast(c.row(f"{tag}_bo"), [TILES, None]), ALU.add).then_inc(bias_added, 1)

                def divide(n, i):
                    for x in range(2):
                        pool.wait_ge(summed, n * 2 + x + 1)
                        half = slice(x * HALF, (x + 1) * HALF)
                        grid = prob[:, i % PROBS, :].rearrange("p (h k) -> p h k", h=H)[:, half]
                        pool.tensor_tensor(grid, grid, bcast(rsum[:, i % PROBS, half], [None, KEYS]), ALU.mult).then_inc(normed, 1)

                for n in range(2):
                    divide(n, n)
                with pool.Fori(0, BATCH - 1) as b:
                    for i in range(TPB):
                        divide(b * TPB + i + 2, i + 2)
                for n in range(TILES - TPB + 2, TILES):
                    divide(n, n)

            @block.tensor
            def _(pe):
                pe.wait_ge(w_in, 64)
                for j in range(FB):
                    pe.matmul(ps[:, K_AT[j], 0:BATCH * KEYS], wk[:, j * P:(j + 1) * P], c.ctxT[:].rearrange("p b k -> p (b k)"),
                              start=True, stop=True).then_inc(k_done, 1)
                for b in range(BATCH):
                    if FB > 1:
                        pe.wait_ge(kT_ready, b + 1)
                    at = ps[0:KEYS, V_AT, b * P:(b + 1) * P] if FB == 1 else ps[0:KEYS, V_AT[b], :]
                    pe.matmul(at, c.ctxT[:, b, :], wv[:], start=True, stop=True).then_inc(v_done, 1)
                norm.tensor(pe)

                def queries(b, j):
                    if j >= 2:
                        pe.wait_ge(q_ready, b * FB + j - 1)
                    pe.matmul(ps[:, Q[j % 2], :], wq[:, j * P:(j + 1) * P], c.normT[:, bass.ds(b * SEQ, SEQ)], start=True, stop=True).then_inc(q_done, 1)

                def scores(n, b, i):
                    if i == 0:
                        pe.wait_ge(q_ready, b * FB + FB)
                    if later(n, -1):
                        pe.wait_ge(score_read, n)
                    t = i * P
                    keys = kdiag[:, bass.ds(b, 1)]
                    if FB == 1:
                        for a, e in cuts:
                            last = pe.matmul(flat[:, a:e], qT[:, 0, t:t + P], keys.rearrange("p b j h k -> p (b j h k)")[:, a:e], start=True, stop=True)
                    else:
                        for j in range(FB):
                            last = pe.matmul(ps[:, j // 2, j % 2 * HB * KEYS:(j % 2 + 1) * HB * KEYS], qT[:, j, t:t + P],
                                             keys[:, :, j].rearrange("p b h k -> p (b h k)"), start=True, stop=True)
                    last.then_inc(scored, 1)

                def turn(n, i, g):
                    pe.wait_ge(normed, n * 2 + g * 2 // GROUPS + 1)
                    if g >= 2:
                        pe.wait_ge(turn_read, n * GROUPS + g - 1)
                    for a in range(GROUP):
                        h = g * GROUP + a
                        last = pe.transpose(ps[0:KEYS, TURN + g % 2, a * P:(a + 1) * P], prob[:, i, h * KEYS:(h + 1) * KEYS], c.ident[:])
                    last.then_inc(turned, 1)

                def product(n, b, i, g):
                    if g == 0 and i == 0:
                        pe.wait_ge(v_placed, b + 1)
                    pe.wait_ge(turn_read, n * GROUPS + g + 1)
                    for a in range(GROUP):
                        h = g * GROUP + a
                        if FB == 1:
                            last = pe.matmul(ps[a * COLS:(a + 1) * COLS, PV, 0:P], v_now[:, h, :], probT[:, h, :], start=(g == 0), stop=(g == GROUPS - 1))
                        else:
                            last = pe.matmul(ps[h % 2 * D:(h % 2 + 1) * D, PV, h // 2 * P:(h // 2 + 1) * P], v_now[:, h, :], probT[:, h, :], start=True, stop=True)
                    if g == GROUPS - 1:
                        last.then_inc(pv_done, 1)

                def output(n):
                    pe.wait_ge(mixed_ready, n + 1)
                    pe.wait_ge(y_added, n + 1)
                    for j in range(FB):
                        last = pe.matmul(ps[:, Y, 0:P], mixedT[:, j * P:(j + 1) * P], wo[:, j, :], start=(j == 0), stop=(j == FB - 1))
                    last.then_inc(y_done, 1)

                def tile(n, b, i):
                    more = later(n, TPB)
                    project = list(range(FB)) if i == 0 and more else []

                    def next_queries():
                        if project:
                            queries(b + 1, project.pop(0))

                    next_queries()
                    turn(n, i, 0)
                    next_queries()
                    turn(n, i, 1)
                    next_queries()
                    product(n, b, i, 0)
                    next_queries()
                    for g in range(1, GROUPS):
                        if g + 1 < GROUPS:
                            turn(n, i, g + 1)
                        product(n, b, i, g)
                    if more:
                        scores(n + TPB, b + 1, i)
                    output(n)

                pe.wait_ge(kdiag_ready, BATCH * FB)
                if not biased:
                    pe.wait_ge(v_ready, BATCH)
                norm.wait(pe, 0)
                for j in range(FB):
                    queries(0, j)
                for n in range(TPB):
                    scores(n, 0, n)
                norm.wait(pe)
                with pe.Fori(0, BATCH - 1) as b:
                    for i in range(TPB):
                        tile(b * TPB + i, b, i)
                for i in range(TPB):
                    tile((BATCH - 1) * TPB + i, BATCH - 1, i)

            @block.scalar
            def _(act):
                if biased:
                    act.wait_ge(k_done, 1)
                    act.activation(kT[:, 0, :], ps[:, K_AT[0], 0:BATCH * KEYS], ACT.Identity, bias=c.vec(f"{tag}_bk")).then_inc(kT_ready, 1)
                else:
                    for j in range(FB):
                        act.wait_ge(k_done, j + 1)
                        act.activation(kT[:, j, :], ps[:, K_AT[j], 0:BATCH * KEYS], ACT.Copy).then_inc(kT_ready, 1)
                    for b in range(BATCH):
                        act.wait_ge(v_done, b + 1)
                        act.activation(v_all[:, b].rearrange("k h v -> k (h v)"), ps[0:KEYS, V_AT[b], :], ACT.Copy).then_inc(v_ready, 1)
                norm.scalar(act)

                def queries(b, j):
                    act.wait_ge(q_done, b * FB + j + 1)
                    if biased:
                        act.activation(qT[:, j, :], ps[:, Q[j % 2], :], ACT.Identity, bias=bq[:], scale=score_scale).then_inc(q_ready, 1)
                    else:
                        act.activation(qT[:, j, :], ps[:, Q[j % 2], :], ACT.Copy, scale=score_scale).then_inc(q_ready, 1)

                def exps(n, i):
                    act.wait_ge(shifted, n + 1)
                    act.activation(prob[:, i % PROBS, :], prob[:, i % PROBS, :], ACT.Exp).then_inc(exped, 1)

                def group_turned(n, g):
                    act.wait_ge(turned, n * GROUPS + g + 1)
                    act.activation(probT[:, g * GROUP:(g + 1) * GROUP, :].rearrange("k h t -> k (h t)"), ps[0:KEYS, TURN + g % 2, :], ACT.Copy).then_inc(turn_read, 1)

                def mixed(n):
                    act.wait_ge(pv_done, n + 1)
                    act.activation(mixedT[:], ps[:, PV, 0:FB * P], ACT.Copy).then_inc(mixed_ready, 1)

                def tile(n, b, i):
                    project = list(range(FB)) if i == 0 and later(n, TPB) else []
                    for g in range(GROUPS):
                        if project:
                            queries(b + 1, project.pop(0))
                        group_turned(n, g)
                    for j in project:
                        queries(b + 1, j)
                    mixed(n)
                    if later(n, 3):
                        exps(n + 3, i + 3)

                if biased:
                    act.wait_ge(prepared, 1)
                for j in range(FB):
                    queries(0, j)
                for n in range(3):
                    exps(n, n)
                with act.Fori(0, BATCH - 1) as b:
                    for i in range(TPB):
                        tile(b * TPB + i, b, i)
                for i in range(TPB):
                    tile((BATCH - 1) * TPB + i, BATCH - 1, i)

            @block.vector
            def _(dve):
                if biased:
                    dve.tensor_scalar(bq[:], c.vec(f"{tag}_bq"), score_scale, None, ALU.mult).then_inc(prepared, 1)
                if mask is not None:
                    dve.wait_ge(mask_in, 16)
                if mask == "barred":
                    dve.tensor_scalar(barred[:], keep[:], -1.0, 1e38, ALU.add, ALU.mult).then_inc(prepared, 1)
                norm.vector(dve)
                if biased:
                    dve.wait_ge(v_clear, 1)
                    dve.wait_ge(v_done, BATCH)
                    for g in range(GROUP):
                        dve.tensor_tensor(v_all[:].rearrange("k b (g a) v -> k b g a v", g=GROUP)[:, :, g, :, g * D:(g + 1) * D],
                                          ps[0:KEYS, V_AT, :].rearrange("k (b a g v) -> k b g a v", b=BATCH, a=GROUP, g=GROUP)[:, :, g],
                                          bcast(c.row(f"{tag}_bv")[0:KEYS].rearrange("k (a g v) -> k g a v", a=GROUP, g=GROUP)[:, g], [BATCH, None, None]),
                                          ALU.add).then_inc(v_ready, 1)
                step = InOrder(dve, order)

                def shift(n, b, i, base):
                    grid = prob[:, i % PROBS, :].rearrange("p (g h k) -> p g h k", g=G, k=KEYS)
                    best = top[:, i % 2, :].rearrange("p (g h) -> p g h", g=G)
                    dve.wait_ge(scored, n + 1)
                    source = heads
                    if mask == "scaled":
                        dve.scalar_tensor_tensor(out=grid.rearrange("p g h k -> p (g h) k"), in0=bcast(masks[:, bass.ds(n, 1), :].rearrange("p a k -> p (a k)"), [H, None]),
                                                 scalar=-1e9, in1=heads.rearrange("p g h k -> p (g h) k"), op0=ALU.mult, op1=ALU.add).then_inc(masked, 1)
                    if mask == "barred":
                        dve.tensor_tensor(grid, heads, bcast(barred[:, bass.ds(b, 1), :].rearrange("p b k -> p (b k)"), [G, H // G, None]),
                                          ALU.add).then_inc(masked, 1)
                    if mask is not None:
                        dve.wait_ge(masked, n + 1)
                        source = grid
                    step(dve.tensor_reduce(best, source, AX.X, ALU.max), base)
                    dve.tensor_tensor(grid, source, bcast(best, [None, None, KEYS]), ALU.subtract).then_inc(shifted, 1)

                def add_up(n, i, base):
                    dve.wait_ge(exped, n + 1)
                    for x in range(2):
                        half = slice(x * HALF, (x + 1) * HALF)
                        sums = rsum[:, i % PROBS, half]
                        step(dve.tensor_reduce(sums, prob[:, i % PROBS, :].rearrange("p (h k) -> p h k", h=H)[:, half], AX.X, ALU.add), base)
                        dve.reciprocal(sums, sums).then_inc(summed, 1)

                def add(n):
                    dve.wait_ge(y_done, n + 1)
                    x = c.resid[:, bass.ds(n, 1), :].rearrange("p t d -> p (t d)")
                    dve.tensor_tensor(x, ps[:, Y, 0:P], x, ALU.add).then_inc(y_added, 1)

                def place_v(b):
                    dve.tensor_copy(v_now[:].rearrange("k h v -> k (h v)"), v_all[:, bass.ds(b, 1)].rearrange("k b h v -> k (b h v)")).then_inc(v_placed, 1)

                def tile(n, b, i, base):
                    if later(n, 3):
                        shift(n + 3, b + (i + 3) // TPB, i + 3, base)
                    if later(n, 2):
                        add_up(n + 2, i + 2, base)
                    add(n)
                    if i == TPB - 1 and later(n, 1):
                        place_v(b + 1)

                dve.wait_ge(v_ready, BATCH if not biased else GROUP)
                place_v(0)
                dve.engine_nop().then_inc(y_added, 1)
                if mask == "barred":
                    dve.wait_ge(prepared, 1)
                for n in range(3):
                    shift(n, 0, n, 0)
                    if n > 0:
                        add_up(n - 1, n - 1, 0)
                if biased:
                    dve.wait_ge(bias_added, 1)
                first, PER = step.n, 3 * TPB
                with dve.Fori(0, BATCH - 1) as b:
                    step.n = first
                    for i in range(TPB):
                        tile(b * TPB + i, b, i, b * PER)
                for i in range(TPB):
                    tile((BATCH - 1) * TPB + i, BATCH - 1, i, (BATCH - 2) * PER)
                dve.wait_ge(y_added, TILES + 1)


class TopK:

    def __init__(self, c, ctx, tag, width, k):
        self.c, self.width, self.k = c, width, k
        self.top = c.sb(ctx, f"{tag}_top", [P, TILES, 8])
        self.place = c.sb(ctx, f"{tag}_place", [P, TILES, 8], U32)
        self.placef = c.sb(ctx, f"{tag}_placef", [P, TILES, 8])
        self.hit = c.sb(ctx, f"{tag}_hit", [P, TILES, width, k])

    def find(self, dve, step, rows):
        for n in range(TILES):
            last = dve.max(self.top[:, n, :], rows[:, n, :])
        step(last)
        for n in range(TILES):
            last = dve.max_index(self.place[:, n, :], self.top[:, n, :], rows[:, n, :])
        step(last)
        step(dve.tensor_copy(self.placef[:], self.place[:]))

    def spread(self, dve, step, weights, out):
        places = self.placef[:, :, 0:self.k]
        step(dve.tensor_tensor(self.hit[:], bcast(self.c.count12[:, 0:self.width], [TILES, None, self.k]),
                               bcast(places, [None, self.width, None]), ALU.is_equal))
        step(dve.tensor_tensor(self.hit[:], self.hit[:], bcast(weights, [None, self.width, None]), ALU.mult))
        step(dve.tensor_reduce(out, self.hit[:], AX.X, ALU.add))


class Softmax:

    def __init__(self, c, ctx, tag, n):
        self.c, self.n = c, n
        self.lead = c.sb(ctx, f"{tag}_lead", [P, TILES])
        self.exps = c.sb(ctx, f"{tag}_exps", [P, TILES, n])
        self.shifted, self.exped = c.sem(f"{tag}_rows_shifted"), c.sem(f"{tag}_rows_exped")

    def vector(self, dve, step, rows, lead=None):
        if lead is None:
            step(dve.tensor_reduce(self.lead[:], rows, AX.X, ALU.max))
            lead = self.lead[:]
        dve.tensor_tensor(self.exps[:], rows, bcast(lead, [None, self.n]), ALU.subtract).then_inc(self.shifted, 1)
        dve.wait_ge(self.exped, 1)
        step(dve.tensor_reduce(self.lead[:], self.exps[:], AX.X, ALU.add))
        step(dve.reciprocal(self.lead[:], self.lead[:]))
        step(dve.tensor_tensor(self.exps[:], self.exps[:], bcast(self.lead[:], [None, self.n]), ALU.mult))

    def scalar(self, act):
        act.wait_ge(self.shifted, 1)
        act.activation(self.exps[:], self.exps[:], ACT.Exp).then_inc(self.exped, 1)


class TopTwo:
    E, FIRST = 8, 0

    def __init__(self, c, ctx, norm):
        self.c, self.norm = c, norm
        self.wg = c.sb(ctx, "L0f_wg", [P, self.E])
        self.rows = c.sb(ctx, "L0f_rows", [P, TILES, self.E])
        self.weight = c.sb(ctx, "L0f_weight", [P, TILES, self.E])
        self.total = c.sb(ctx, "L0f_total", [P, TILES])
        self.own = c.sb(ctx, "L0f_own", [P, TILES, P])
        self.top = TopK(c, ctx, "L0f", self.E, 2)
        self.soft = Softmax(c, ctx, "L0f", 2)
        self.w_in, self.scored, self.order = c.sem("L0f_wg_in"), c.sem("L0f_scored"), c.sem("L0f_route_order")

    def sync(self, sp):
        sp.dma_start(self.wg[:], self.c.dram["L0f_wg"]).then_inc(self.w_in, 16)

    def tensor(self, pe):
        pe.wait_ge(self.w_in, 16)
        for n in range(TILES):
            last = pe.matmul(self.c.ps[:, 7, n * self.E:(n + 1) * self.E], self.c.normT[:, n * P:(n + 1) * P], self.wg[:], start=True, stop=True)
        last.then_inc(self.scored, 1)

    def scalar(self, act):
        self.soft.scalar(act)

    def vector(self, dve):
        c, norm, step = self.c, self.norm, InOrder(dve, self.order)
        dve.wait_ge(self.scored, 1)
        step(dve.tensor_tensor(self.rows[:], c.ps[:, 7, 0:TILES * self.E].rearrange("p (n e) -> p n e", n=TILES),
                               bcast(norm.std2[:], [None, self.E]), ALU.mult))
        self.top.find(dve, step, self.rows)
        self.soft.vector(dve, step, self.top.top[:, :, 0:2], self.top.top[:, :, 0])
        self.top.spread(dve, step, self.soft.exps[:], self.weight[:])
        step(dve.tensor_reduce(self.total[:], self.weight[:], AX.X, ALU.add))
        step(dve.tensor_tensor(self.total[:], self.total[:], norm.rstd[:], ALU.mult))
        for n in range(TILES):
            last = dve.tensor_scalar(self.own[:, n, :], c.resid[:, n, :], norm.mean[:, n:n + 1], self.total[:, n:n + 1], ALU.subtract, ALU.mult)
        step(last)
        step(dve.tensor_tensor(c.resid[:], c.resid[:], self.own[:], ALU.add))


class Sampled:
    E, FIRST = 8, 0
    HID, KMAX = 50, 6

    def __init__(self, c, ctx, norm):
        self.c = c
        self.wr = c.sb(ctx, "L1f_wr", [P, self.E])
        self.a1 = c.sb(ctx, "L1f_a1", [P, self.HID])
        self.a2 = c.sb(ctx, "L1f_a2", [self.HID, self.KMAX])
        self.hid = c.sb(ctx, "L1f_hid", [self.HID, TILES * P])
        self.rows = c.sb(ctx, "L1f_rows", [P, TILES, self.E])
        self.choice = c.sb(ctx, "L1f_choice", [P, TILES, 8])
        self.keep = c.sb(ctx, "L1f_keep", [P, TILES, self.E])
        self.weight = c.sb(ctx, "L1f_weight", [P, TILES, self.E])
        self.top = TopK(c, ctx, "L1f", self.E, self.E)
        self.pick = TopK(c, ctx, "L1f_pick", 8, 1)
        self.soft = Softmax(c, ctx, "L1f", self.E)
        self.w_in, self.scored, self.order = c.sem("L1f_wr_in"), c.sem("L1f_scored"), c.sem("L1f_route_order")
        self.hid_done, self.hid_ready = c.sem("L1f_actor_done"), c.sem("L1f_actor_ready")

    def sync(self, sp):
        for sb, name in ((self.wr, "L1f_wr"), (self.a1, "L1f_a1"), (self.a2, "L1f_a2")):
            sp.dma_start(sb[:], self.c.dram[name]).then_inc(self.w_in, 16)

    def tensor(self, pe):
        c = self.c
        pe.wait_ge(self.w_in, 48)
        for n in range(TILES):
            last = pe.matmul(c.ps[:, 7, n * self.E:(n + 1) * self.E], c.normT[:, n * P:(n + 1) * P], self.wr[:], start=True, stop=True)
        last.then_inc(self.scored, 1)
        for b in range(BATCH):
            pe.matmul(c.ps[0:self.HID, b, :], self.a1[:], c.normT[:, b * SEQ:(b + 1) * SEQ], start=True, stop=True).then_inc(self.hid_done, 1)
        pe.wait_ge(self.hid_ready, BATCH)
        for n in range(TILES):
            last = pe.matmul(c.ps[:, 6, n * 8:n * 8 + self.KMAX], self.hid[:, n * P:(n + 1) * P], self.a2[:], start=True, stop=True)
        last.then_inc(self.scored, 1)

    def scalar(self, act):
        for b in range(BATCH):
            act.wait_ge(self.hid_done, b + 1)
            act.activation(self.hid[:, b * SEQ:(b + 1) * SEQ], self.c.ps[0:self.HID, b, :], ACT.Gelu_apprx_tanh,
                           bias=self.c.vec("L1f_b1")[0:self.HID]).then_inc(self.hid_ready, 1)
        self.soft.scalar(act)

    def vector(self, dve):
        c, step = self.c, InOrder(dve, self.order)
        step(dve.memset(self.choice[:], -1e30))
        dve.wait_ge(self.scored, 1)
        step(dve.tensor_copy(self.rows[:], c.ps[:, 7, 0:TILES * self.E].rearrange("p (n e) -> p n e", n=TILES)))
        self.soft.vector(dve, step, self.rows[:])
        self.top.find(dve, step, self.soft.exps)
        dve.wait_ge(self.scored, 2)
        logits = self.choice[:, :, 0:self.KMAX]
        step(dve.tensor_tensor(logits, c.ps[:, 6, 0:TILES * 8].rearrange("p (n k) -> p n k", n=TILES)[:, :, 0:self.KMAX],
                               bcast(c.row("L1f_b2")[:, 0:self.KMAX], [TILES, None]), ALU.add))
        step(dve.tensor_scalar(logits, logits, -30.0, 30.0, ALU.max, ALU.min))
        self.pick.find(dve, step, self.choice)
        step(dve.tensor_tensor(self.keep[:], bcast(c.count12[:, 0:self.E], [TILES, None]),
                               bcast(self.pick.placef[:, :, 0], [None, self.E]), ALU.is_le))
        step(dve.tensor_tensor(self.keep[:], self.keep[:], self.top.top[:], ALU.mult))
        self.top.spread(dve, step, self.keep[:], self.weight[:])


class TopProbs:
    E, FIRST = 9, 1

    def __init__(self, c, ctx, norm):
        self.c = c
        self.wr = c.sb(ctx, "L3f_wr", [P, 8])
        self.rows = c.sb(ctx, "L3f_rows", [P, TILES, 8])
        self.weight = c.sb(ctx, "L3f_weight", [P, TILES, 9])
        self.top = TopK(c, ctx, "L3f", 8, 2)
        self.soft = Softmax(c, ctx, "L3f", 8)
        self.w_in, self.scored, self.order = c.sem("L3f_wr_in"), c.sem("L3f_scored"), c.sem("L3f_route_order")

    def sync(self, sp):
        sp.dma_start(self.wr[:], self.c.dram["L3f_wr"]).then_inc(self.w_in, 16)

    def tensor(self, pe):
        pe.wait_ge(self.w_in, 16)
        for n in range(TILES):
            last = pe.matmul(self.c.ps[:, 7, n * 8:(n + 1) * 8], self.c.normT[:, n * P:(n + 1) * P], self.wr[:], start=True, stop=True)
        last.then_inc(self.scored, 1)

    def scalar(self, act):
        self.soft.scalar(act)

    def vector(self, dve):
        c, step = self.c, InOrder(dve, self.order)
        step(dve.memset(self.weight[:], 1.0))
        dve.wait_ge(self.scored, 1)
        step(dve.tensor_tensor(self.rows[:], c.ps[:, 7, 0:TILES * 8].rearrange("p (n e) -> p n e", n=TILES),
                               bcast(c.row("L3f_rb")[:, 0:8], [TILES, None]), ALU.add))
        self.soft.vector(dve, step, self.rows[:])
        self.top.find(dve, step, self.soft.exps)
        self.top.spread(dve, step, self.top.top[:, :, 0:2], self.weight[:, :, 1:9])


def experts(c, tag, router_kind, kind, R, F, inner_eps=None):
    nc, ps = c.nc, c.ps
    gated, folded = kind == "swiglu", kind == "relu"
    W1 = 2 * R * F if gated else R * F
    GAIN, SHIFT = W1 + F, W1 + F + 1
    PACKED = {"relu": SHIFT + 1, "gelu": W1 + F, "swiglu": W1}[kind]
    SLOTS = F if gated else 4
    YBANK = 6 if gated else 4
    func = {"relu": ACT.Relu, "gelu": ACT.Gelu, "swiglu": ACT.Silu}[kind]
    with ExitStack() as ctx:
        norm = Norm(c, ctx, tag, inner_eps, banks=6)
        route = router_kind(c, ctx, norm)
        E = route.E
        PAIRS = E // HALVES
        tail_expert = E % HALVES
        w1 = c.sb(ctx, f"{tag}_w1", [P, HALVES, PACKED])
        w2 = c.sb(ctx, f"{tag}_w2", [R, HALVES, F, P])
        hid = c.sb(ctx, f"{tag}_hidden", [R, HALVES, F, SEQ])
        w1g = c.sb(ctx, f"{tag}_w1g", [P, HALVES, W1]) if folded else w1
        b1 = c.sb(ctx, f"{tag}_b1", [P, HALVES, F]) if folded else None
        gate = c.sb(ctx, f"{tag}_gate", [R, F, SEQ]) if gated else None
        w_in = c.pair(f"{tag}_w_in")
        hid_done, gate_ready, hid_ready = (c.sem(f"{tag}_{n}") for n in ("hid_done", "gate_ready", "hid_ready"))
        out_done, out_added = c.sem(f"{tag}_out_done"), c.pair(f"{tag}_out_added")
        scaled, shift_done, shift_ready = c.sem(f"{tag}_scaled"), c.sem(f"{tag}_shift_done"), c.sem(f"{tag}_shift_ready")
        if not gated:
            b2 = c.sb(ctx, f"{tag}_b2", [E, P])
            weightT = c.sb(ctx, f"{tag}_weightT", [E, SEQ])
            b2_in, wT_done, wT_ready, b2_done, b2_added = (c.sem(f"{tag}_{n}") for n in ("b2_in", "wT_done", "wT_ready", "b2_done", "b2_added"))
        routed = c.sem(f"{tag}_routed")
        MM = 2 if gated else 1

        def steps(eng, make, use, bias=lambda i: None):
            def run(q, us, after, bias=lambda i: None):
                at = [(q, u, b) for u in us for b in range(BATCH)]
                for i, (now, then) in enumerate(zip(at, at[1:] + [after])):
                    if then is not None:
                        make(*then)
                    use(*now)
                    bias(i)

            with eng.Fori(0, PAIRS - 1) as q:
                run(q, range(HALVES), (q + 1, 0, 0))
            run(PAIRS - 1, range(HALVES), (PAIRS, 0, 0) if tail_expert else None, bias)
            if tail_expert:
                run(PAIRS, range(1), None)

        with nc.Block() as block:
            @block.sync
            def _(sp):
                def load(e, u):
                    sp.dma_start(w1[:, u, :], c.dram[f"{tag}_{'gu' if gated else 'w1'}"][bass.ds(e, 1)].rearrange(
                        "e d g f -> (e d) (g f)" if gated else "e d f -> (e d) f")).then_inc(w_in[u], 16)
                    sp.dma_start(w2[:, u], c.dram[f"{tag}_{'dn' if gated else 'w2'}"][bass.ds(e, 1)].rearrange(
                        "e r f d -> (e r) f d")).then_inc(w_in[u], 16)

                route.sync(sp)
                if not gated:
                    sp.dma_start(b2[:], c.dram[f"{tag}_b2"]).then_inc(b2_in, 16)
                for u in range(HALVES):
                    load(u, u)
                with sp.Fori(1, PAIRS) as q:
                    for u in range(HALVES):
                        sp.wait_ge(out_done, (q * HALVES + u - 1) * BATCH)
                        load(q * HALVES + u, u)
                if tail_expert:
                    sp.wait_ge(out_done, (E - 2) * BATCH)
                    load(E - 1, 0)

            if folded:
                @block.gpsimd
                def _(pool):
                    with pool.Fori(0, PAIRS) as q:
                        for u in range(HALVES):
                            pool.wait_ge(w_in[u], q * 32 + 32)
                            pool.tensor_tensor(w1g[:, u, :], w1[:, u, 0:W1], w1[:, u, GAIN:GAIN + 1].broadcast_to([P, W1]), ALU.mult).then_inc(scaled, 1)

            @block.tensor
            def _(pe):
                norm.tensor(pe)

                def hidden(q, u, b):
                    e = q * HALVES + u
                    s = e * BATCH + b
                    if b == 0:
                        pe.wait_ge(w_in[u], q * 32 + 32)
                        if folded:
                            pe.wait_ge(scaled, e + 1)
                            if not isinstance(e, int) or e > 0:
                                pe.wait_ge(shift_ready, e)
                            for f in range(F):
                                last = pe.matmul(ps[:, 6, f:f + 1], w1[:, u, f * R:(f + 1) * R],
                                                 w1[:, u, SHIFT:SHIFT + 1], start=True, stop=True)
                            last.then_inc(shift_done, 1)
                    if not isinstance(s, int) or s > 0:
                        pe.wait_ge(hid_ready, s * F)
                    for f in range(F):
                        slot = (b * F + f) % SLOTS
                        for m in range(MM):
                            pe.matmul(ps[0:R, m * SLOTS + slot, :], w1g[:, u, (m * F + f) * R:(m * F + f + 1) * R],
                                      c.normT[:, b * SEQ:(b + 1) * SEQ], start=True, stop=True).then_inc(hid_done, 1)

                def result(q, u, b):
                    s = (q * HALVES + u) * BATCH + b
                    pe.wait_ge(hid_ready, s * F + F)
                    pe.wait_ge(out_added[b % 2], (q * HALVES + u) * (BATCH // 2) + b // 2 + 1)
                    for t in range(TPB):
                        for f in range(F):
                            last = pe.matmul(ps[:, YBANK + b % 2, t * P:(t + 1) * P], hid[:, b % 2, f, t * P:(t + 1) * P],
                                             w2[:, u, f, :], start=(f == 0), stop=(f == F - 1))
                    last.then_inc(out_done, 1)

                def bias(i):
                    b = i // 2
                    if i == 0:
                        pe.wait_ge(b2_in, 16)
                        pe.wait_ge(routed, 1)
                    if i % 2 == 0:
                        if b > 0:
                            pe.wait_ge(b2_added, b)
                        for t in range(TPB):
                            last = pe.transpose(ps[0:E, 7, t * P:(t + 1) * P], route.weight[:, b * TPB + t, :], c.ident[:])
                        last.then_inc(wT_done, 1)
                    else:
                        pe.wait_ge(wT_ready, b + 1)
                        for t in range(TPB):
                            last = pe.matmul(ps[:, 7, t * P:(t + 1) * P], weightT[:, t * P:(t + 1) * P], b2[:], start=True, stop=True)
                        last.then_inc(b2_done, 1)

                norm.wait(pe, BATCH - 1 if folded else 0)
                hidden(0, 0, 0)
                norm.wait(pe)
                if gated:
                    pe.wait_ge(hid_ready, F)
                route.tensor(pe)
                if gated:
                    steps(pe, hidden, result)
                else:
                    steps(pe, hidden, result, bias)

            @block.scalar
            def _(act):
                norm.scalar(act)

                def activate(q, u, b):
                    e = q * HALVES + u
                    s = e * BATCH + b
                    if folded and b == 0:
                        act.wait_ge(shift_ready, e + 1)
                    for f in range(F):
                        slot = (b * F + f) % SLOTS
                        act.wait_ge(hid_done, (s * F + f) * MM + 1)
                        if gated:
                            act.activation(gate[:, f, :], ps[0:R, slot, :], func).then_inc(gate_ready, 1)
                        else:
                            bias = b1[:, u, f:f + 1] if folded else w1[:, u, W1 + f:W1 + f + 1]
                            act.activation(hid[:, b % 2, f, :], ps[0:R, slot, :], func, bias=bias).then_inc(hid_ready, 1)

                def bias(i):
                    if i % 2 == 0:
                        act.wait_ge(wT_done, i // 2 + 1)
                        act.activation(weightT[:], ps[0:E, 7, :], ACT.Copy).then_inc(wT_ready, 1)

                activate(0, 0, 0)
                route.scalar(act)
                if gated:
                    steps(act, activate, lambda q, u, b: None)
                else:
                    steps(act, activate, lambda q, u, b: None, bias)

            @block.vector
            def _(dve):
                norm.vector(dve)
                flat = route.weight[:].rearrange("p n e -> p (n e)")

                def add(q, u, b):
                    e = q * HALVES + u
                    s = e * BATCH + b
                    dve.wait_ge(out_done, s + 1)
                    dve.wait_ge(out_added[b % 2], e * (BATCH // 2) + b // 2 + 1)
                    if biased[0]:
                        dve.wait_ge(b2_added, biased[0])
                    for t in range(TPB):
                        n = b * TPB + t
                        last = dve.scalar_tensor_tensor(out=c.resid[:, n, :], in0=ps[:, YBANK + b % 2, t * P:(t + 1) * P],
                                                        scalar=flat[:, bass.ds(n * E + e, 1)], in1=c.resid[:, n, :],
                                                        op0=ALU.mult, op1=ALU.add)
                    last.then_inc(out_added[b % 2], 1)

                def finish_hidden(q, u, b):
                    e = q * HALVES + u
                    s = e * BATCH + b
                    if folded and b == 0:
                        dve.wait_ge(shift_done, e + 1)
                        dve.tensor_tensor(b1[:, u, :], ps[:, 6, 0:F], w1[:, u, W1:W1 + F], ALU.add).then_inc(shift_ready, 1)
                    for f in range(F if gated else 0):
                        dve.wait_ge(gate_ready, s * F + f + 1)
                        dve.wait_ge(hid_done, (s * F + f) * MM + 2)
                        dve.tensor_tensor(hid[:, b % 2, f, :], gate[:, f, :], ps[0:R, SLOTS + f, :], ALU.mult).then_inc(hid_ready, 1)

                biased = [0]

                def bias(i):
                    if i % 2 == 1:
                        b = i // 2
                        x = c.resid[:, b * TPB:(b + 1) * TPB, :]
                        dve.wait_ge(b2_done, b + 1)
                        dve.wait_ge(out_added[b % 2], (PAIRS - 1) * HALVES * 2 + (i - b % 2) // 2 + 2)
                        dve.tensor_tensor(x, ps[:, 7, :].rearrange("p (t d) -> p t d", t=TPB), x, ALU.add).then_inc(b2_added, 1)
                        biased[0] += 1

                def results_may_come():
                    for h in range(2):
                        dve.engine_nop().then_inc(out_added[h], 1)

                finish_hidden(0, 0, 0)
                if not gated:
                    results_may_come()
                route.vector(dve)
                dve.engine_nop().then_inc(routed, 1)
                if gated:
                    results_may_come()
                if gated:
                    steps(dve, finish_hidden, add)
                else:
                    steps(dve, finish_hidden, add, bias)
                for h in range(2):
                    dve.wait_ge(out_added[h], E * 2 + 1)
                if not gated:
                    dve.wait_ge(b2_added, BATCH)


def latent_attention(c):
    nc, ps = c.nc, c.ps
    PAIRS, D = 8, 64
    NK = SEQ + KEYS
    KB = 5
    BK = (NK + KB - 1) // KB
    STEPS = 2 * TPB
    TURNS = PAIRS * BATCH
    RING = 4
    AHEAD = 3
    Q, V4, NORMS, Y, V1, KL, KC, NKL = range(STEPS)
    FOR = {Q: 1, V4: 1, NORMS: 1, Y: -1, V1: 1, KL: 2, KC: 2, NKL: 2}
    PROLOGUE = [(KL, 0), (KC, 0), (NKL, 0), (Q, 0), (V4, 0), (NORMS, 0), (V1, 0), (KL, 1), (KC, 1), (NKL, 1)]
    with ExitStack() as ctx:
        norm = Norm(c, ctx, "L1", inner_eps=1e-5, gain=c.vec("L1_lg"), shift=c.vec("L1_lb"))
        keysT = c.sb(ctx, "L1_keysT", [P, BATCH, KB * BK])
        w_all = c.sb(ctx, "L1_w_all", [P, PAIRS + 1, 3, P])
        wq, wk = c.sb(ctx, "L1_wq", [P, P]), c.sb(ctx, "L1_wk", [P, P])
        wo = c.sb(ctx, "L1_wo", [P, PAIRS + 1, P])
        keep, barred = c.sb(ctx, "L1_keep", [P, BATCH, KEYS], U8), c.sb(ctx, "L1_barred", [P, BATCH, KEYS])
        cx, cstage = c.sb(ctx, "L1_cx", [KEYS, BATCH, P]), c.sb(ctx, "L1_cstage", [KEYS, BATCH, P])
        cstats, cwork = c.sb(ctx, "L1_cstats", [KEYS, BATCH, 6]), c.sb(ctx, "L1_cwork", [KEYS, 6, BATCH])
        gains = c.sb(ctx, "L1_gains", [P, 1])
        q2, kT = c.sb(ctx, "L1_q2", [P, 2, 2, SEQ]), c.sb(ctx, "L1_kT", [P, 2, NK])
        v, qinv = c.sb(ctx, "L1_v", [BK, 2, KB, P]), c.sb(ctx, "L1_qinv", [P, 2, STEPS])
        ksq, qsq = c.sb(ctx, "L1_ksq", [P, NK]), c.sb(ctx, "L1_qsq", [P, SEQ])
        kinv, qms = c.sb(ctx, "L1_kinv", [P, NK]), c.sb(ctx, "L1_qms", [P, STEPS])
        top, low, sums, rsums = (c.sb(ctx, f"L1_{n}", [P, RING]) for n in ("top", "low", "sums", "rsums"))
        prob, probT = c.sb(ctx, "L1_prob", [P, RING, KB * BK]), c.sb(ctx, "L1_probT", [BK, RING, KB, P])
        mixedT = c.sb(ctx, "L1_mixedT", [P, SEQ])
        w_in, ctx_in, keep_in, filled, tokens_in = (c.sem(f"L1_{n}") for n in ("w_in", "ctx_in", "keep_in", "filled", "tokens_in"))
        corder, cvar_ready, cstd_ready, cstaged, cturned, ctx_ready = (c.sem(f"L1_{n}") for n in (
            "corder", "cvar_ready", "cstd_ready", "cstaged", "cturned", "ctx_ready"))
        order, act_order, prepared, bias_added = (c.sem(f"L1_{n}") for n in ("order", "act_order", "prepared", "bias_added"))
        w_ready, side_done, side_read, squared = (c.sem(f"L1_{n}") for n in ("w_ready", "side_done", "side_read", "squared"))
        kinv_ready, qinv_ready, k_ready = (c.sem(f"L1_{n}") for n in ("kinv_ready", "qinv_ready", "k_ready"))
        scored, bounded, exped, summed, normed, turned, turn_read, mix_done, mixed_ready = (c.sem(f"L1_{n}") for n in (
            "scored", "bounded", "exped", "summed", "normed", "turned", "turn_read", "mix_done", "mixed_ready"))
        S = [ps[:, 2 * i:2 * i + 2, :].rearrange("p b n -> p (b n)") for i in range(2)]
        PT = ps[0:BK, 4:6, :].rearrange("p b n -> p (b n)")
        O, side = ps[:, 6, :], ps[:, 7, :]

        def use_of(turn, s):
            return len(PROLOGUE) + turn * STEPS + s

        def squares(turn, kind):
            return turn * 3 + {KL: 1, KC: 2, Q: 3}[kind]

        def scalings(turn, kind):
            return turn * 2 + {NKL: 1, NORMS: 2}[kind]

        def turns(eng, body):
            with eng.Fori(0, PAIRS) as p:
                for b in range(BATCH):
                    body(p, b, p * BATCH + b)

        def batch_of(b, kind):
            return (b + FOR[kind]) % BATCH

        with nc.Block() as block:
            @block.sync
            def _(sp):
                sp.dma_start(cx[:], c.dram["ctx"]).then_inc(ctx_in, 16)
                sp.dma_start(keep[:], c.dram["keep_L1"]).then_inc(keep_in, 16)
                weights = c.dram["L1_w"].rearrange("j p w f -> p j w f")
                sp.dma_start(w_all[:, 0:PAIRS], weights).then_inc(w_in, 16)
                sp.dma_start(w_all[:, PAIRS:PAIRS + 1], weights[:, 0:1]).then_inc(w_in, 16)
                out_rows = c.dram["L1_wo"].rearrange("j p d -> p j d")
                sp.dma_start(wo[:, 1:PAIRS + 1], out_rows).then_inc(w_in, 16)
                sp.dma_start(wo[:, 0:1], out_rows[:, 0:1]).then_inc(w_in, 16)

            @block.gpsimd
            def _(pool):
                pool.memset(q2[:], 0.0)
                pool.memset(prob[:], 0.0)
                pool.memset(v[:, 1], 0.0)
                pool.memset(keysT[:, :, NK:KB * BK], 0.0).then_inc(filled, 1)
                pool.memset(probT[:], 0.0).then_inc(turn_read, 1)

                def take_weights(to, p, kind):
                    pool.tensor_copy(to[:], w_all[:, bass.ds(p, 1), kind].rearrange("p j f -> p (j f)")).then_inc(w_ready, 1)

                pool.wait_ge(w_in, 64)
                take_weights(wk, 0, 1)
                take_weights(wq, 0, 0)

                def scale_keys(turn, w, kind):
                    a, e = (0, SEQ) if kind == NKL else (SEQ, NK)
                    pool.wait_ge(kinv_ready, scalings(turn, kind))
                    pool.tensor_tensor(kT[:, w, a:e], kT[:, w, a:e], kinv[:, a:e], ALU.mult).then_inc(k_ready, 1)

                def divide(now, s):
                    pool.wait_ge(summed, now + 1)
                    x = prob[:, s % RING, 0:NK]
                    pool.tensor_tensor(x, x, rsums[:, s % RING:s % RING + 1].broadcast_to([P, NK]), ALU.mult).then_inc(normed, 1)

                scale_keys(0, 0, NKL)
                scale_keys(0, 0, NORMS)
                norm.wait(pool)
                pool.tensor_tensor(c.resid[:], c.resid[:], bcast(c.row("L1_bout"), [TILES, None]), ALU.add).then_inc(bias_added, 1)
                for s in range(AHEAD - 1):
                    divide(s, s)

                def body(p, b, turn):
                    for s in range(STEPS):
                        if b == 2 and s == 0:
                            pool.wait_ge(side_done, use_of(turn, KC) - STEPS + 1)
                            take_weights(wk, p + 1, 1)
                        if b == 2 and s == 2:
                            pool.wait_ge(side_done, use_of(turn, Q) + 1)
                            take_weights(wq, p + 1, 0)
                        divide(turn * STEPS + s + AHEAD - 1, s + AHEAD - 1)
                        if s == 1:
                            scale_keys(turn + 1, (b + 1) % 2, NKL)
                        if s == 4:
                            scale_keys(turn + 1, (b + 1) % 2, NORMS)

                turns(pool, body)

            @block.tensor
            def _(pe):
                pe.wait_ge(cstaged, 1)
                for b in range(BATCH):
                    last = pe.transpose(ps[:, 2, b * KEYS:(b + 1) * KEYS], cstage[:, b, :], c.ident[0:KEYS, 0:KEYS])
                last.then_inc(cturned, 1)
                norm.tensor(pe)
                pe.wait_ge(tokens_in, BATCH)
                pe.wait_ge(ctx_ready, 1)
                pe.wait_ge(filled, 1)

                def use_side(kind, at, turn, b, p):
                    if not isinstance(at, int) or at > 0:
                        pe.wait_ge(side_read, at)
                    tokens, context = keysT[:, b, 0:SEQ], keysT[:, b, SEQ:NK]
                    if kind == KL:
                        last = pe.matmul(side, wk[:], tokens, start=True, stop=True)
                    elif kind == KC:
                        last = pe.matmul(side[:, 0:KEYS], wk[:], context, start=True, stop=True)
                    elif kind == Q:
                        last = pe.matmul(side, wq[:], tokens, start=True, stop=True)
                    elif kind == NKL:
                        pe.wait_ge(squared, squares(turn, KL))
                        last = pe.matmul(side, c.pairsum[:], ksq[:, 0:SEQ], start=True, stop=True)
                    elif kind == NORMS:
                        pe.wait_ge(squared, squares(turn, Q))
                        pe.matmul(side[:, 0:KEYS], c.pairsum[:], ksq[:, SEQ:NK], start=True, stop=True)
                        for t in range(TPB):
                            last = pe.matmul(side[:, P + 2 * t:P + 2 * t + 2], qsq[:, t * P:(t + 1) * P], c.pairsum[:, 0:P:D], start=True, stop=True)
                    elif kind == Y:
                        pe.wait_ge(mixed_ready, turn + 2)
                        for t in range(TPB):
                            last = pe.matmul(side[:, t * P:(t + 1) * P], mixedT[:, t * P:(t + 1) * P], wo[:, bass.ds(p, 1)].rearrange("p j d -> p (j d)"),
                                             start=True, stop=True)
                    else:
                        wv = w_all[:, bass.ds(p, 1), 2].rearrange("p j f -> p (j f)")
                        for k in range(KB - 1) if kind == V4 else [KB - 1]:
                            last = pe.matmul(side[0:BK, k % 4 * P:(k % 4 + 1) * P], keysT[:, b, k * BK:(k + 1) * BK], wv, start=True, stop=True)
                    last.then_inc(side_done, 1)

                def scores(turn, s, w):
                    if s == 0:
                        pe.wait_ge(k_ready, scalings(turn, NORMS))
                    q = q2[:, w, s % 2, s // 2 * P:(s // 2 + 1) * P]
                    pe.matmul(S[s % 2][:, 0:SEQ], q, kT[:, w, 0:SEQ], start=True, stop=True)
                    pe.matmul(S[s % 2][:, SEQ:NK], q, kT[:, w, SEQ:NK], start=True, stop=True).then_inc(scored, 1)

                def turn_step(now, s):
                    pe.wait_ge(normed, now + 1)
                    pe.wait_ge(turn_read, now + 1)
                    for k in range(KB):
                        last = pe.transpose(PT[:, k * P:(k + 1) * P], prob[:, s % RING, k * BK:(k + 1) * BK], c.ident[:])
                    last.then_inc(turned, 1)

                def product(now, t, w):
                    pe.wait_ge(turn_read, now + 1)
                    for k in range(KB):
                        for h in range(2):
                            last = pe.matmul(O[h * D:(h + 1) * D, t * P:(t + 1) * P], v[:, w, k, h * D:(h + 1) * D], probT[:, (2 * t + h) % RING, k, :],
                                             start=(k == 0), stop=(k == KB - 1))
                    if t == TPB - 1:
                        last.then_inc(mix_done, 1)

                pe.wait_ge(w_ready, 2)
                for at, (kind, turn) in enumerate(PROLOGUE):
                    use_side(kind, at, turn, turn, 0)
                for s in range(AHEAD):
                    if s == 2:
                        pe.wait_ge(exped, 1)
                    scores(0, s, 0)
                pe.wait_ge(turn_read, 1)
                pe.matmul(O, probT[:, 0, 0, :], probT[:, 0, 0:4].rearrange("k b t -> k (b t)"), start=True, stop=True)

                def body(p, b, turn):
                    w = b % 2
                    for s in range(STEPS):
                        now = turn * STEPS + s
                        turn_step(now, s)
                        to = s + AHEAD
                        pe.wait_ge(exped, now + AHEAD - 1)
                        scores(turn + to // STEPS, to % STEPS, (b + to // STEPS) % 2)
                        if s == 0:
                            product(now, TPB - 1, 1 - w)
                        elif s % 2 == 0:
                            if s == 2:
                                pe.wait_ge(mixed_ready, turn + 1)
                                pe.wait_ge(side_read, use_of(turn, V1) - STEPS + 1)
                            product(now, s // 2 - 1, w)
                        kind = s
                        if kind == KL and b == 2:
                            pe.wait_ge(w_ready, p * 2 + 3)
                        if kind == Q and b == 3:
                            pe.wait_ge(w_ready, p * 2 + 4)
                        pair = p + (b + FOR[kind]) // BATCH
                        use_side(kind, use_of(turn, s), turn + FOR[kind], batch_of(b, kind), pair + 1 if kind == Y else pair)

                turns(pe, body)
                product(TURNS * STEPS, TPB - 1, 1)
                use_side(Y, use_of(TURNS, 0), TURNS - 1, BATCH - 1, PAIRS)

            @block.scalar
            def _(act):
                act.wait_ge(cvar_ready, 1)
                act.activation(cwork[:, 4, :], cwork[:, 3, :], ACT.Sqrt).then_inc(cstd_ready, 1)
                act.wait_ge(cturned, 1)
                act.activation(keysT[:, :, SEQ:NK], ps[:, 2, 0:BATCH * KEYS].rearrange("p (b k) -> p b k", b=BATCH), ACT.Identity,
                               bias=c.vec("L1_xb"), scale=c.vec("L1_xg")).then_inc(ctx_ready, 1)
                norm.scalar(act)
                norm.wait(act)
                for b in range(BATCH):
                    act.activation(keysT[:, b, 0:SEQ], c.normT[:, b * SEQ:(b + 1) * SEQ], ACT.Copy).then_inc(tokens_in, 1)
                act.preload_act_table_set("natural_log_exp_and_others")
                step = InOrder(act, act_order)

                def square(kind, at, turn, w):
                    if kind == Q:
                        act.wait_ge(side_done, at + 1)
                        act.activation(qsq[:], side, ACT.Square).then_inc(squared, 1)
                    else:
                        act.wait_ge(side_read, at + 1)
                        a, e = (0, SEQ) if kind == KL else (SEQ, NK)
                        act.activation(ksq[:, a:e], kT[:, w, a:e], ACT.Square).then_inc(squared, 1)

                def invert(kind, at, w, base):
                    act.wait_ge(side_read, at + 1)
                    if kind == NKL:
                        step(act.activation(kinv[:, 0:SEQ], kinv[:, 0:SEQ], ACT.Ln), base)
                        act.activation(kinv[:, 0:SEQ], kinv[:, 0:SEQ], ACT.Exp, scale=-0.5).then_inc(kinv_ready, 1)
                    else:
                        act.activation(kinv[:, SEQ:NK], kinv[:, SEQ:NK], ACT.Ln)
                        step(act.activation(qms[:], qms[:], ACT.Ln), base)
                        act.activation(kinv[:, SEQ:NK], kinv[:, SEQ:NK], ACT.Exp, scale=-0.5).then_inc(kinv_ready, 1)
                        act.activation(qinv[:, w, :], qms[:], ACT.Exp, scale=-0.5).then_inc(qinv_ready, 1)

                def exps(now, s, w):
                    i = s % RING
                    act.wait_ge(bounded, now + 1)
                    act.activation(prob[:, i, 0:NK], S[s % 2][:, 0:NK], ACT.Exp, bias=low[:, i:i + 1], scale=qinv[:, w, s:s + 1],
                                   accum_out=sums[:, i:i + 1]).then_inc(exped, 1)

                def mixed(turn):
                    act.wait_ge(mix_done, turn + 1)
                    act.activation(mixedT[:], O, ACT.Copy).then_inc(mixed_ready, 1)

                act.wait_ge(filled, 1)
                for at, (kind, turn) in enumerate(PROLOGUE[:-1]):
                    if kind in (KL, KC, Q):
                        square(kind, at, turn, turn)
                    if kind in (NKL, NORMS):
                        invert(kind, at, turn, 0)
                for s in range(AHEAD - 1):
                    exps(s, s, 0)
                first, LINKS = step.n, 2

                def body(p, b, turn):
                    step.n = first
                    for s in range(STEPS):
                        at = use_of(turn, s) - 1
                        if s == Q + 1:
                            square(Q, at, turn + 1, None)
                        act.wait_ge(turned, turn * STEPS + s + 1)
                        act.activation(probT[:, s % RING].rearrange("k b t -> k (b t)"), PT[:, 0:KB * P], ACT.Copy).then_inc(turn_read, 1)
                        to = s + AHEAD - 1
                        exps(turn * STEPS + to, to % STEPS, (b + to // STEPS) % 2)
                        if s == 1:
                            mixed(turn)
                        if s == (NKL + 1) % STEPS:
                            invert(NKL, at, None, turn * LINKS)
                        if s == NORMS + 1:
                            invert(NORMS, at, (b + 1) % 2, turn * LINKS)
                        if s in (KL + 1, KC + 1):
                            square(s - 1, at, turn + 2, b % 2)

                turns(act, body)
                mixed(TURNS)

            @block.vector
            def _(dve):
                cstep = InOrder(dve, corder)
                dve.wait_ge(ctx_in, 16)
                for b in range(BATCH):
                    last = dve.bn_stats(cstats[:, b, :], cx[:, b, :])
                cstep(last)
                half, gap, spread, var, std, mean = (cwork[:, i, :] for i in range(6))
                dve.tensor_tensor(half, cstats[:, :, 1], cstats[:, :, 4], ALU.add)
                dve.tensor_tensor(spread, cstats[:, :, 2], cstats[:, :, 5], ALU.add)
                cstep(dve.tensor_tensor(gap, cstats[:, :, 1], cstats[:, :, 4], ALU.subtract))
                dve.tensor_scalar(mean, half, 0.5, None, ALU.mult)
                cstep(dve.tensor_tensor(gap, gap, gap, ALU.mult))
                cstep(dve.tensor_scalar(spread, spread, 1.0 / P, NORM_EPS, ALU.mult, ALU.add))
                dve.scalar_tensor_tensor(out=var, in0=gap, scalar=0.25, in1=spread, op0=ALU.mult, op1=ALU.add).then_inc(cvar_ready, 1)
                dve.wait_ge(cstd_ready, 1)
                cstep(dve.reciprocal(half, std))
                for b in range(BATCH):
                    last = dve.tensor_scalar(cstage[:, b, :], cx[:, b, :], mean[:, b:b + 1], half[:, b:b + 1], ALU.subtract, ALU.mult)
                last.then_inc(cstaged, 1)
                norm.vector(dve)
                dve.wait_ge(keep_in, 16)
                dve.tensor_scalar(barred[:], keep[:], -1.0, 1e30, ALU.add, ALU.mult).then_inc(prepared, 1)
                dve.tensor_tensor(gains[:], c.vec("L1_qg"), c.vec("L1_kg"), ALU.mult).then_inc(prepared, 1)
                dve.wait_ge(prepared, 2)
                dve.tensor_scalar(gains[:], gains[:], D ** -0.5, None, ALU.mult).then_inc(prepared, 1)
                dve.wait_ge(prepared, 3)
                dve.wait_ge(filled, 1)
                step = InOrder(dve, order)

                def bound(turn, s, b, base):
                    w, i = b % 2, s % RING
                    dve.wait_ge(scored, turn * STEPS + s + 1)
                    if s == 0:
                        dve.wait_ge(qinv_ready, turn + 1)
                    masked = S[s % 2][:, SEQ:NK]
                    step(dve.tensor_tensor(masked, masked, barred[:, b, :], ALU.add), base)
                    step(dve.tensor_reduce(top[:, i:i + 1], S[s % 2][:, 0:NK], AX.X, ALU.max), base)
                    dve.tensor_scalar(low[:, i:i + 1], top[:, i:i + 1], qinv[:, w, s:s + 1], -1.0, ALU.mult, ALU.mult).then_inc(bounded, 1)

                def invert_sum(now, s):
                    i = s % RING
                    dve.wait_ge(exped, now + 1)
                    dve.reciprocal(rsums[:, i:i + 1], sums[:, i:i + 1]).then_inc(summed, 1)

                def read_side(kind, at, turn, b):
                    w = b % 2
                    dve.wait_ge(side_done, at + 1)
                    if kind == Y:
                        x = c.resid[:, b * TPB:(b + 1) * TPB, :]
                        last = dve.tensor_tensor(x, side.rearrange("p (t d) -> p t d", t=TPB), x, ALU.add)
                    elif kind == KL:
                        last = dve.tensor_copy(kT[:, w, 0:SEQ], side)
                    elif kind == KC:
                        last = dve.tensor_copy(kT[:, w, SEQ:NK], side[:, 0:KEYS])
                    elif kind == Q:
                        dve.wait_ge(squared, squares(turn, Q))
                        dve.tensor_scalar(q2[0:D, w, 0, :], side[0:D, :], gains[0:D], None, ALU.mult)
                        last = dve.tensor_scalar(q2[D:P, w, 1, :], side[D:P, :], gains[D:P], None, ALU.mult)
                    elif kind == V4:
                        last = dve.tensor_copy(v[:, w, 0:KB - 1, :].rearrange("k b d -> k (b d)"), side[0:BK, :])
                    elif kind == V1:
                        last = dve.tensor_copy(v[:, w, KB - 1, :], side[0:BK, 0:P])
                    elif kind == NKL:
                        last = dve.tensor_scalar(kinv[:, 0:SEQ], side, 1.0 / D, 1e-16, ALU.mult, ALU.max)
                    else:
                        dve.tensor_scalar(kinv[:, SEQ:NK], side[:, 0:KEYS], 1.0 / D, 1e-16, ALU.mult, ALU.max)
                        last = dve.tensor_scalar(qms[:], side[:, P:P + STEPS], 1.0 / D, 1e-16, ALU.mult, ALU.max)
                    last.then_inc(side_read, 1)

                for at, (kind, turn) in enumerate(PROLOGUE[:-1]):
                    read_side(kind, at, turn, turn)
                for s in range(AHEAD):
                    if s > 0:
                        invert_sum(s - 1, s - 1)
                    bound(0, s, 0, 0)
                first, LINKS = step.n, 2 * STEPS
                dve.wait_ge(bias_added, 1)

                def body(p, b, turn):
                    step.n = first
                    for s in range(STEPS):
                        kind = (s - 1) % STEPS
                        ahead = FOR[kind] - (s == 0)
                        read_side(kind, use_of(turn, s) - 1, turn + ahead, (b + ahead) % BATCH)
                        to = s + AHEAD - 1
                        invert_sum(turn * STEPS + to, to)
                        to = s + AHEAD
                        bound(turn + to // STEPS, to % STEPS, (b + to // STEPS) % BATCH, turn * LINKS)

                turns(dve, body)
                read_side(NKL, use_of(TURNS, 0) - 1, TURNS + 1, 1)
                read_side(Y, use_of(TURNS, 0), TURNS - 1, BATCH - 1)
                dve.wait_ge(side_read, use_of(TURNS, 0) + 1)


def mixture_addressed(c):
    nc, ps, tag = c.nc, c.ps, "L2f"
    L, HID, ADDR, K = 12, 512, 64, 3
    FB = HID // P
    BANKS = 4
    TURN = 4
    with ExitStack() as ctx:
        norm = Norm(c, ctx, tag, banks=6)
        pw, um = c.sb(ctx, "L2f_pw", [P, ADDR]), c.sb(ctx, "L2f_u", [ADDR, 3 * L])
        addr = c.sb(ctx, "L2f_addr", [ADDR, TILES * P])
        rows = c.sb(ctx, "L2f_rows", [P, 3, TILES, L])
        weight = c.sb(ctx, "L2f_weight", [P, 3, TILES, L])
        top = [TopK(c, ctx, f"L2f{r}", L, K) for r in range(3)]
        soft = [Softmax(c, ctx, f"L2f{r}", K) for r in range(3)]
        w1, w2 = c.sb(ctx, "L2f_w1", [P, HALVES, HID]), c.sb(ctx, "L2f_w2", [P, HALVES, FB, 2 * P])
        hid = c.sb(ctx, "L2f_hid", [P, TILES, HID])
        act_hid = c.sb(ctx, "L2f_act_hid", [P, HALVES, HID])
        hidT = c.sb(ctx, "L2f_hidT", [P, FB, TILES * P])
        b2, weightT = c.sb(ctx, "L2f_b2", [L, P]), c.sb(ctx, "L2f_weightT", [L, TILES * P])
        small_in, w1_in, w2_in = c.sem("L2f_small_in"), c.pair("L2f_w1_in"), c.pair("L2f_w2_in")
        addr_done, addr_ready, scored, order = (c.sem(f"L2f_{n}") for n in ("addr_done", "addr_ready", "scored", "order"))
        cleared, first_done, second_done = c.sem("L2f_cleared"), c.sem("L2f_first_done"), c.sem("L2f_second_done")
        first_added = [c.sem(f"L2f_first_added{i}") for i in range(BANKS)]
        second_added = [c.sem(f"L2f_second_added{i}") for i in range(BANKS)]
        gelu_ready, turned, turn_read = (c.sem(f"L2f_{n}") for n in ("gelu_ready", "hid_turned", "turn_read"))
        third_ready, wT_done, wT_ready, b2_done, b2_added = (c.sem(f"L2f_{n}") for n in ("third_ready", "wT_done", "wT_ready", "b2_done", "b2_added"))
        LAG = 3
        turn_weights = {n: n // TPB for n in range(0, TILES, TPB)}
        multiply_biases = {n + 2: n // TPB for n in range(0, TILES, TPB)}
        SIDE = 6

        with nc.Block() as block:
            @block.sync
            def _(sp):
                for sb, name in ((pw, "L2f_pw"), (um, "L2f_u"), (b2, "L2f_b2")):
                    sp.dma_start(sb[:], c.dram[name]).then_inc(small_in, 16)

                def load1(e, u):
                    sp.dma_start(w1[:, u, :], c.dram["L2f_w1"][bass.ds(e, 1)].rearrange("e d f -> (e d) f")).then_inc(w1_in[u], 16)

                def load2(g, u):
                    sp.dma_start(w2[:, u], c.dram["L2f_w2"][bass.ds(g, 1)].rearrange("g p f e d -> (g p) f (e d)")).then_inc(w2_in[u], 16)

                for u in range(HALVES):
                    load1(u, u)
                    load2(u, u)
                with sp.Fori(1, L // HALVES) as q:
                    for u in range(HALVES):
                        sp.wait_ge(first_done, (q * HALVES + u - 1) * TILES)
                        load1(q * HALVES + u, u)
                with sp.Fori(1, L // 2 // HALVES) as q:
                    for u in range(HALVES):
                        sp.wait_ge(second_done, (q * HALVES + u - 1) * TILES)
                        load2(q * HALVES + u, u)

            @block.gpsimd
            def _(pool):
                pool.memset(hid[:], 0.0).then_inc(cleared, 1)

            @block.tensor
            def _(pe):
                norm.tensor(pe)
                pe.wait_ge(small_in, 48)
                for b in range(BATCH):
                    norm.wait(pe, b)
                    pe.matmul(ps[0:ADDR, 2 + b, :], pw[:], c.normT[:, b * SEQ:(b + 1) * SEQ], start=True, stop=True).then_inc(addr_done, 1)
                for n in range(TILES):
                    pe.wait_ge(addr_ready, n // TPB + 1)
                    last = pe.matmul(ps[:, 6 + n // 8, n % 8 * 64:n % 8 * 64 + 3 * L], addr[:, n * P:(n + 1) * P], um[:], start=True, stop=True)
                last.then_inc(scored, 1)
                def first(e, u, n):
                    pe.wait_ge(first_added[n % BANKS], e * (TILES // BANKS) + n // BANKS + 1)
                    pe.matmul(ps[:, n % BANKS, :], c.normT[:, n * P:(n + 1) * P], w1[:, u, :], start=True, stop=True).then_inc(first_done, 1)

                def turn(n):
                    pe.wait_ge(gelu_ready, n + 1)
                    if n >= 2:
                        pe.wait_ge(turn_read, n - 1)
                    for f in range(FB):
                        last = pe.transpose(ps[:, TURN + n % 2, f * P:(f + 1) * P], act_hid[:, n % 2, f * P:(f + 1) * P], c.ident[:])
                    last.then_inc(turned, 1)

                with pe.Fori(0, L // HALVES - 1) as q:
                    for u in range(HALVES):
                        pe.wait_ge(w1_in[u], q * 16 + 16)
                        for n in range(TILES):
                            first(q * HALVES + u, u, n)
                pe.wait_ge(third_ready, 1)
                pe.wait_ge(w1_in[0], L // HALVES * 16)
                for n in range(TILES):
                    if n in turn_weights:
                        b = turn_weights[n]
                        if b >= 2:
                            pe.wait_ge(wT_ready, b - 1)
                        for t in range(TPB):
                            last = pe.transpose(ps[0:L, SIDE + b % 2, t * P:(t + 1) * P], weight[:, 2, b * TPB + t, :], c.ident[:])
                        last.then_inc(wT_done, 1)
                    first(L - 2, 0, n)
                pe.wait_ge(w1_in[1], L // HALVES * 16)
                for n in range(TILES):
                    if n in multiply_biases:
                        b = multiply_biases[n]
                        pe.wait_ge(wT_ready, BATCH)
                        if b >= 2:
                            pe.wait_ge(b2_added, b - 1)
                        for t in range(TPB):
                            last = pe.matmul(ps[:, SIDE + b % 2, t * P:(t + 1) * P], weightT[:, (b * TPB + t) * P:(b * TPB + t + 1) * P], b2[:], start=True, stop=True)
                        last.then_inc(b2_done, 1)
                    first(L - 1, 1, n)
                    if n >= LAG:
                        turn(n - LAG)
                for n in range(TILES - LAG, TILES):
                    turn(n)
                pe.wait_ge(turn_read, TILES)
                with pe.Fori(0, L // 2 // HALVES) as q:
                    for u in range(HALVES):
                        pe.wait_ge(w2_in[u], q * 16 + 16)
                        for n in range(TILES):
                            pe.wait_ge(second_added[n % BANKS], (q * HALVES + u) * (TILES // BANKS) + n // BANKS + 1)
                            for f in range(FB):
                                last = pe.matmul(ps[:, n % BANKS, 0:2 * P], hidT[:, f, n * P:(n + 1) * P], w2[:, u, f, :], start=(f == 0), stop=(f == FB - 1))
                            last.then_inc(second_done, 1)

            @block.scalar
            def _(act):
                norm.scalar(act)
                for b in range(BATCH):
                    act.wait_ge(addr_done, b + 1)
                    act.activation(addr[:, b * SEQ:(b + 1) * SEQ], ps[0:ADDR, 2 + b, :], ACT.Copy).then_inc(addr_ready, 1)
                for r in range(3):
                    soft[r].scalar(act)
                for b in range(BATCH):
                    act.wait_ge(wT_done, b + 1)
                    act.activation(weightT[:, b * SEQ:(b + 1) * SEQ], ps[0:L, SIDE + b % 2, :], ACT.Copy).then_inc(wT_ready, 1)
                for n in range(TILES):
                    act.wait_ge(first_added[n % BANKS], (L - 1) * (TILES // BANKS) + n // BANKS + 2)
                    if n >= 2:
                        act.wait_ge(turned, n - 1)
                    act.activation(act_hid[:, n % 2, :], hid[:, n, :], ACT.Gelu).then_inc(gelu_ready, 1)

            @block.vector
            def _(dve):
                norm.vector(dve)
                step = InOrder(dve, order)
                for i in range(BANKS):
                    dve.engine_nop().then_inc(first_added[i], 1)
                dve.wait_ge(scored, 1)
                for r in range(3):
                    last = dve.tensor_copy(rows[:, r].rearrange("p (a n) e -> p a n e", a=2),
                                           ps[:, 6:8, :].rearrange("p a (n w) -> p a n w", n=8)[:, :, :, r * L:(r + 1) * L])
                step(last)

                def routed(r):
                    top[r].find(dve, step, rows[:, r])
                    soft[r].vector(dve, step, top[r].top[:, :, 0:K], top[r].top[:, :, 0])
                    top[r].spread(dve, step, soft[r].exps[:], weight[:, r])

                def add_first(e, n):
                    dve.wait_ge(first_done, e * TILES + n + 1)
                    dve.wait_ge(first_added[n % BANKS], e * (TILES // BANKS) + n // BANKS + 1)
                    dve.scalar_tensor_tensor(out=hid[:, n, :], in0=ps[:, n % BANKS, :], scalar=flat[:, bass.ds(n * L + e, 1)], in1=hid[:, n, :],
                                             op0=ALU.mult, op1=ALU.add).then_inc(first_added[n % BANKS], 1)

                def take_turned(n):
                    dve.wait_ge(turned, n + 1)
                    dve.tensor_copy(hidT[:, :, n * P:(n + 1) * P], ps[:, TURN + n % 2, :].rearrange("p (f t) -> p f t", f=FB)).then_inc(turn_read, 1)

                flat = weight[:].rearrange("p r n e -> p (r n e)")
                routed(0)
                dve.wait_ge(cleared, 1)
                for e in range(HALVES):
                    for n in range(TILES):
                        add_first(e, n)
                    routed(1 + e)
                dve.engine_nop().then_inc(third_ready, 1)
                with dve.Fori(1, L // HALVES - 1) as q:
                    for u in range(HALVES):
                        for n in range(TILES):
                            add_first(q * HALVES + u, n)
                for n in range(TILES):
                    add_first(L - 2, n)
                for n in range(TILES):
                    if n in multiply_biases:
                        b = multiply_biases[n]
                        dve.wait_ge(b2_done, b + 1)
                        x = c.resid[:, b * TPB:(b + 1) * TPB, :]
                        dve.tensor_tensor(x, ps[:, SIDE + b % 2, :].rearrange("p (t d) -> p t d", t=TPB), x, ALU.add).then_inc(b2_added, 1)
                    add_first(L - 1, n)
                    if n >= LAG:
                        take_turned(n - LAG)
                for n in range(TILES - LAG, TILES):
                    take_turned(n)
                for i in range(BANKS):
                    dve.engine_nop().then_inc(second_added[i], 1)
                dve.wait_ge(b2_added, BATCH)
                with dve.Fori(0, L // 2 // HALVES) as q:
                    for u in range(HALVES):
                        g = q * HALVES + u
                        for n in range(TILES):
                            dve.wait_ge(second_done, g * TILES + n + 1)
                            dve.wait_ge(second_added[n % BANKS], g * (TILES // BANKS) + n // BANKS + 1)
                            for i in range(2):
                                ins = dve.scalar_tensor_tensor(out=c.resid[:, n, :], in0=ps[:, n % BANKS, i * P:(i + 1) * P],
                                                               scalar=flat[:, bass.ds(TILES * L + n * L + g * 2 + i, 1)], in1=c.resid[:, n, :],
                                                               op0=ALU.mult, op1=ALU.add)
                                if i == 0:
                                    ins.then_inc(order, 1)
                                    dve.wait_ge(order, step.n + g * TILES + n + 1)
                            ins.then_inc(second_added[n % BANKS], 1)
                for i in range(BANKS):
                    dve.wait_ge(second_added[i], L // 2 * (TILES // BANKS) + 1)


def program(nc, dram, out, layers=(0, 8)):
    with ExitStack() as ctx:
        c = Core(nc, ctx, dram, layers)
        constants(c)
        steps = [
            lambda: cross_attention(c, "L0", 16, 8, 8 ** -0.5, None),
            lambda: experts(c, "L0f", TopTwo, "relu", P, 4, inner_eps=1e-6),
            lambda: latent_attention(c),
            lambda: experts(c, "L1f", Sampled, "swiglu", 112, 3),
            lambda: cross_attention(c, "L2", 16, 8, 8 ** -0.5, "scaled"),
            lambda: mixture_addressed(c),
            lambda: cross_attention(c, "L3", 8, 64, 64 ** -0.5, "barred", inner_eps=1e-5, gain=c.vec("L3_g"), shift=c.vec("L3_b")),
            lambda: experts(c, "L3f", TopProbs, "gelu", P, 2),
        ]
        for step in steps[layers[0]:layers[1]]:
            taken = nc.snapshot_sems()
            step()
            c.retire(taken)
        stored = c.sem("stored")
        with nc.Block() as block:
            @block.sync
            def _(sp):
                sp.dma_start(out, c.resid[:]).then_inc(stored, 16)
                sp.wait_ge(stored, 16)


def laid_out(i):
    import numpy as np
    a = {k: np.asarray(v) for k, v in i.items()}
    cols = lambda v: v.reshape(-1, P).T
    twice = lambda v: np.tile(v, 2)[:, None]
    b1 = np.zeros((P, 1), np.float32)
    b1[:50, 0] = a["L1_ffn_actor_b1"]
    vecs = {
        "L0_bq": cols(a["L0_xattn_bq"]), "L0_bk": cols(a["L0_xattn_bk"]), "L2_bq": cols(a["L2_xattn_bq"]), "L2_bk": cols(a["L2_xattn_bk"]),
        "L1_xg": cols(a["L1_xattn_ln_x_g"]), "L1_xb": cols(a["L1_xattn_ln_x_b"]), "L1_lg": cols(a["L1_xattn_ln_l_g"]), "L1_lb": cols(a["L1_xattn_ln_l_b"]),
        "L1_qg": twice(a["L1_xattn_qn_g"]), "L1_kg": twice(a["L1_xattn_kn_g"]), "L1f_b1": b1,
        "L3_g": cols(a["L3_xattn_ln_gamma"]), "L3_b": cols(a["L3_xattn_ln_beta"]),
    }
    rows = np.zeros((len(ROWS), P), np.float32)
    for n, k in enumerate(["L0_xattn_bv", "L0_xattn_bo", "L1_xattn_bout", "L2_xattn_bv", "L2_xattn_bo", "L3_ffn_router_b", "L1_ffn_actor_b2"]):
        rows[n, :a[k].size] = a[k]
    E = 8
    packed = lambda w, b, *more: np.concatenate([w, b.reshape(len(b), -1, P).transpose(0, 2, 1), *(m[:, :, None] for m in more)], 2)
    both = lambda n: np.concatenate([a[f"L3_ffn_s{n}"][None], a[f"L3_ffn_r{n}"]])
    ctx = a["ctx_1024"]
    got = {
        "x": a["x"].reshape(TILES, P, P).transpose(1, 0, 2),
        "vecs": np.concatenate([vecs[k] for k in VECS], 1),
        "rows": np.broadcast_to(rows, (P, *rows.shape)),
        "ctxT": ctx.transpose(2, 0, 1),
        "ctx": ctx.transpose(1, 0, 2),
        **{f"L0_w{n}": a[f"L0_xattn_W{n}"].T for n in "qkv"}, "L0_wo": a["L0_xattn_Wo"].T[:, None],
        **{f"L2_w{n}": a[f"L2_xattn_w{n}"].T for n in "qkv"}, "L2_wo": a["L2_xattn_wo"].T[:, None],
        "L2_mask": a["mask_Bx1xSxS2_fk1"].reshape(TILES, P, KEYS).transpose(1, 0, 2),
        "keep_L1": np.broadcast_to(a["mask_BxS2_bf1"], (P, BATCH, KEYS)),
        "L3_mask": np.broadcast_to(a["mask_BxS2_bk0"], (P, BATCH, KEYS)),
        "L0f_wg": a["L0_ffn_Wg"], "L0f_w1": packed(a["L0_ffn_W1"], a["L0_ffn_b1"], a["L0_ffn_gamma"], a["L0_ffn_beta"]), "L0f_b2": a["L0_ffn_b2"],
        "L0f_w2": a["L0_ffn_W2"].reshape(E, 4, P, P).transpose(0, 2, 1, 3),
        "L1_w": np.stack([a["L1_xattn_Wq"].reshape(P, 8, P), a["L1_xattn_Wkv"][:, :1024].reshape(P, 8, P), a["L1_xattn_Wkv"][:, 1024:].reshape(P, 8, P)], 2).transpose(1, 0, 2, 3),
        "L1_wo": a["L1_xattn_Wout"].reshape(8, P, P),
        "L1f_wr": a["L1_ffn_router_w"].T, "L1f_a1": a["L1_ffn_actor_w1"].T, "L1f_a2": a["L1_ffn_actor_w2"].T,
        "L1f_gu": np.stack([a["L1_ffn_gate_w"].transpose(0, 2, 1), a["L1_ffn_up_w"].transpose(0, 2, 1)], 2),
        "L1f_dn": a["L1_ffn_down_w"].transpose(0, 2, 1).reshape(E, 3, 112, P).transpose(0, 2, 1, 3),
        "L2f_pw": a["L2_ffn_P_w"].T, "L2f_u": np.concatenate([a[f"L2_ffn_U{n}"] for n in (1, 2, 3)]).T,
        "L2f_w1": a["L2_ffn_W1"].transpose(0, 2, 1),
        "L2f_w2": a["L2_ffn_W2"].reshape(6, 2, P, 4, P).transpose(0, 4, 3, 1, 2),
        "L2f_b2": a["L2_ffn_b2"],
        "L3_wq": a["L3_xattn_Wq"], "L3_wk": a["L3_xattn_Wkv"][:, :512], "L3_wv": a["L3_xattn_Wkv"][:, 512:], "L3_wo": a["L3_xattn_Wout"].reshape(4, P, P).transpose(1, 0, 2),
        "L3f_wr": a["L3_ffn_router_w"], "L3f_b2": both("b2"), "L3f_w1": packed(both("w1"), both("b1")),
        "L3f_w2": both("w2").reshape(9, 2, P, P).transpose(0, 2, 1, 3),
    }
    return {k: np.ascontiguousarray(v) for k, v in got.items()}


def kernel(**inputs):
    import concourse.bacc as bacc
    from concourse.bass_utils import run_bass_kernel_spmd

    arrays = laid_out(inputs)
    nc = bacc.Bacc("TRN2", target_bir_lowering=False, num_devices=1)
    dram = {k: nc.dram_tensor(k, v.shape, mybir.dt.from_np(v.dtype), kind="ExternalInput").ap() for k, v in arrays.items()}
    out = nc.dram_tensor("out", (P, TILES, P), F32, kind="ExternalOutput").ap()
    program(nc, dram, out)
    done = run_bass_kernel_spmd(nc, [arrays], core_ids=[0])
    return done.results[0]["out"].transpose(1, 0, 2).reshape(BATCH, SEQ, P)
```

```python
from contextlib import ExitStack

import concourse.bass as bass
from concourse import mybir

F32 = mybir.dt.float32
F32R = mybir.dt.float32r
U8 = mybir.dt.uint8
U32 = mybir.dt.uint32
ALU = mybir.AluOpType
ACT = mybir.ActivationFunctionType
AX = mybir.AxisListType

P = 128
BATCH, SEQ, KEYS = 4, 512, 77
TILES = BATCH * SEQ // P
TPB = SEQ // P
HALVES = 2
NORM_EPS = 1e-5

VECS = {}
for _name, _n in (("L0_bq", 1), ("L0_bk", 1), ("L2_bq", 1), ("L2_bk", 1), ("L1_xg", 1), ("L1_xb", 1), ("L1_lg", 1), ("L1_lb", 1), ("L1_qg", 1),
                  ("L1_kg", 1), ("L1f_b1", 1), ("L3_g", 1), ("L3_b", 1)):
    VECS[_name] = (sum(n for _, n in VECS.values()), _n)
NVEC = sum(n for _, n in VECS.values())
ROWS = ["L0_bv", "L0_bo", "L1_bout", "L2_bv", "L2_bo", "L3f_rb", "L1f_b2"]


class Core:

    def __init__(self, nc, ctx, dram, layers):
        self.nc, self.ctx, self.dram, self.layers = nc, ctx, dram, layers
        self.ps = ctx.enter_context(nc.psum_tensor("banks", [P, 8, 512], F32))
        self.resid = self.sb(ctx, "resid", [P, TILES, P])
        self.normT = self.sb(ctx, "normT", [P, TILES * P])
        self.ident = self.sb(ctx, "ident", [P, P])
        self.vecs = self.sb(ctx, "vecs", [P, NVEC])
        self.rows = self.sb(ctx, "rows", [P, len(ROWS), P])
        self.ctxT = self.sb(ctx, "ctxT", [P, BATCH, KEYS])
        self.head16 = self.sb(ctx, "head16", [P, 16])
        self.pairsum = self.sb(ctx, "pairsum", [P, P])
        self.one = self.sb(ctx, "one", [P, 1])
        self.count12 = self.sb(ctx, "count12", [P, 12])

    def sb(self, ctx, name, shape, dt=F32):
        return ctx.enter_context(self.nc.sbuf_tensor(f"sb_{name}", shape, dt))

    def sem(self, name):
        return self.nc.alloc_semaphore(name)

    def retire(self, before):
        self.nc.clear_and_free_semaphores(self.nc.allocated_since(before))
        self.nc.all_engine_barrier()

    def pair(self, name):
        return [self.sem(f"{name}{u}") for u in range(HALVES)]

    def vec(self, name, i=0):
        at = VECS[name][0] + i
        return self.vecs[:, at:at + 1]

    def row(self, name):
        return self.rows[:, ROWS.index(name), :]


def split_product(pe, out, stationary, moving, start=True, stop=True):
    (sh, sl), (mh, ml) = stationary, moving
    pe.matmul(out, sl, mh, start=start, stop=False)
    pe.matmul(out, sh, ml, start=False, stop=False)
    return pe.matmul(out, sh, mh, start=False, stop=stop)


class InOrder:

    def __init__(self, eng, sem):
        self.eng, self.sem, self.n = eng, sem, 0

    def __call__(self, ins, base=0):
        self.n += 1
        ins.then_inc(self.sem, 1)
        self.eng.wait_ge(self.sem, base + self.n)


def bcast(ap, dims):
    for i, d in enumerate(dims):
        if d is not None:
            ap = ap.unsqueeze(i + 1)
    shape = [ap.shape[0]] + [s if d is None else d for d, s in zip(dims, ap.shape[1:])]
    return ap.broadcast_to(shape)


def constants(c):
    nc, d = c.nc, c.dram
    loaded, built = c.sem("loaded"), c.sem("built")
    counts = c.ctx.enter_context(nc.sbuf_tensor("counts", [P, 12], mybir.dt.int32))
    with nc.Block() as block:
        @block.sync
        def _(sp):
            sp.dma_start(c.resid[:], d["x"]).then_inc(loaded, 16)
            sp.dma_start(c.vecs[:], d["vecs"]).then_inc(loaded, 16)
            sp.dma_start(c.rows[:], d["rows"]).then_inc(loaded, 16)
            sp.dma_start(c.ctxT[:], d["ctxT"]).then_inc(loaded, 16)
            sp.wait_ge(loaded, 64)

        @block.gpsimd
        def _(pool):
            step = InOrder(pool, built)
            pool.memset(c.ident[:], 0.0)
            pool.memset(c.head16[:], 1.0)
            pool.memset(c.one[:], 1.0)
            pool.memset(c.pairsum[:], 0.0)
            step(pool.iota(counts[:], pattern=[[1, 12]], base=0, channel_multiplier=0))
            pool.tensor_copy(c.count12[:], counts[:])
            pool.affine_select(out=c.ident[:], in_=c.ident[:], compare_op=ALU.not_equal, fill=1.0, base=0,
                               pattern=[[-1, P]], channel_multiplier=1)
            step(pool.affine_select(out=c.head16[:], in_=c.head16[:], compare_op=ALU.is_ge, fill=0.0, base=0,
                                    pattern=[[-8, 16]], channel_multiplier=1))
            step(pool.affine_select(out=c.head16[:], in_=c.head16[:], compare_op=ALU.is_ge, fill=0.0, base=7,
                                    pattern=[[8, 16]], channel_multiplier=-1))
            step(pool.memset(c.pairsum[0:64, 0:64], 1.0))
            step(pool.memset(c.pairsum[64:128, 64:128], 1.0))


class Norm:

    def __init__(self, c, ctx, tag, inner_eps=None, gain=None, shift=None, banks=0, split=False):
        self.c, self.split, self.inner_eps, self.gain, self.shift = c, split, inner_eps, gain, shift
        self.banks = c.ps[:, banks:banks + HALVES, :]
        self.stats = c.sb(ctx, f"{tag}_stats", [P, TILES, 6])
        self.mean = c.sb(ctx, f"{tag}_mean", [P, TILES])
        self.var = c.sb(ctx, f"{tag}_var", [P, TILES])
        self.std = c.sb(ctx, f"{tag}_std", [P, TILES])
        self.std2 = c.sb(ctx, f"{tag}_std2", [P, TILES])
        self.rstd = c.sb(ctx, f"{tag}_rstd", [P, TILES])
        self.scale = c.sb(ctx, f"{tag}_scale", [P, TILES])
        self.bias = c.sb(ctx, f"{tag}_bias", [P, TILES])
        self.work = c.sb(ctx, f"{tag}_work", [P, 3, TILES])
        self.stage = c.sb(ctx, f"{tag}_stage", [P, HALVES, TPB, P])
        self.order = c.sem(f"{tag}_norm_order")
        self.var_ready, self.std_ready = c.sem(f"{tag}_var_ready"), c.sem(f"{tag}_std_ready")
        self.scaled, self.turned, self.ready = (c.sem(f"{tag}_{n}") for n in ("norm_scaled", "norm_turned", "norm_ready"))
        self.staged = c.pair(f"{tag}_norm_staged")
        if split:
            self.high, self.low = (c.sb(ctx, f"{tag}_norm_{n}", [P, TILES * P], F32R) for n in ("high", "low"))
            self.parted = c.sem(f"{tag}_norm_parted")

    def vector(self, dve):
        c, step = self.c, InOrder(dve, self.order)
        for n in range(TILES):
            last = dve.bn_stats(self.stats[:, n, :], c.resid[:, n, :])
        step(last)
        me, mo = self.stats[:, :, 1], self.stats[:, :, 4]
        half, gap, spread = (self.work[:, i, :] for i in range(3))
        dve.tensor_tensor(half, me, mo, ALU.add)
        dve.tensor_tensor(spread, self.stats[:, :, 2], self.stats[:, :, 5], ALU.add)
        step(dve.tensor_tensor(gap, me, mo, ALU.subtract))
        dve.tensor_scalar(self.mean[:], half, 0.5, None, ALU.mult)
        step(dve.tensor_tensor(gap, gap, gap, ALU.mult))
        step(dve.tensor_scalar(spread, spread, 1.0 / P, None, ALU.mult))
        step(dve.scalar_tensor_tensor(out=self.var[:], in0=gap, scalar=0.25, in1=spread, op0=ALU.mult, op1=ALU.add))
        dve.tensor_scalar(gap, self.var[:], NORM_EPS, None, ALU.add).then_inc(self.var_ready, 1)
        dve.wait_ge(self.std_ready, 1)
        step(dve.reciprocal(self.rstd[:], self.std[:]))
        if self.inner_eps is not None:
            step(dve.tensor_tensor(half, self.var[:], self.rstd[:], ALU.mult))
            step(dve.tensor_tensor(half, half, self.rstd[:], ALU.mult))
            dve.tensor_scalar(spread, half, self.inner_eps, None, ALU.add).then_inc(self.var_ready, 1)
            dve.wait_ge(self.std_ready, 2)
            step(dve.reciprocal(half, self.std2[:]))
            step(dve.tensor_tensor(self.scale[:], half, self.rstd[:], ALU.mult))
        scale = self.rstd if self.inner_eps is None else self.scale
        dve.scalar_tensor_tensor(out=self.bias[:], in0=self.mean[:], scalar=-1.0, in1=scale[:], op0=ALU.mult, op1=ALU.mult).then_inc(self.scaled, 1)
        for b in range(0, BATCH, HALVES):
            if b >= HALVES:
                dve.wait_ge(self.turned, b - HALVES + 1)
            for t in range(TPB):
                n = b * TPB + t
                last = dve.tensor_scalar(self.stage[:, 0, t, :], c.resid[:, n, :], self.mean[:, n:n + 1], scale[:, n:n + 1], ALU.subtract, ALU.mult)
            last.then_inc(self.staged[0], 1)
        for b in range(BATCH if self.split else 0):
            self.wait(dve, b)
            at = slice(b * SEQ, (b + 1) * SEQ)
            step(dve.tensor_copy(self.high[:, at], c.normT[:, at]))
            dve.tensor_tensor(self.low[:, at], c.normT[:, at], self.high[:, at], ALU.subtract).then_inc(self.parted, 1)

    def tensor(self, pe):
        for b in range(BATCH):
            pe.wait_ge(self.staged[b % HALVES], b // HALVES + 1)
            if b >= HALVES:
                pe.wait_ge(self.ready, b - HALVES + 1)
            for t in range(TPB):
                last = pe.transpose(self.banks[:, b % HALVES, t * P:(t + 1) * P], self.stage[:, b % HALVES, t, :], self.c.ident[:])
            last.then_inc(self.turned, 1)

    def scalar(self, act):
        act.wait_ge(self.var_ready, 1)
        act.activation(self.std[:], self.work[:, 1, :], ACT.Sqrt).then_inc(self.std_ready, 1)
        if self.inner_eps is not None:
            act.wait_ge(self.var_ready, 2)
            act.activation(self.std2[:], self.work[:, 2, :], ACT.Sqrt).then_inc(self.std_ready, 1)
        scale = self.rstd if self.inner_eps is None else self.scale
        act.wait_ge(self.scaled, 1)
        for b in range(BATCH):
            if b % HALVES == 0:
                for t in range(TPB):
                    n = (b + 1) * TPB + t
                    last = act.activation(self.stage[:, 1, t, :], self.c.resid[:, n, :], ACT.Identity, bias=self.bias[:, n:n + 1], scale=scale[:, n:n + 1])
                last.then_inc(self.staged[1], 1)
            act.wait_ge(self.turned, b + 1)
            out = self.c.normT[:, b * SEQ:(b + 1) * SEQ]
            if self.gain is None:
                ins = act.activation(out, self.banks[:, b % HALVES, :], ACT.Copy)
            else:
                ins = act.activation(out, self.banks[:, b % HALVES, :], ACT.Identity, bias=self.shift, scale=self.gain)
            ins.then_inc(self.ready, 1)

    def wait(self, eng, b=BATCH - 1):
        eng.wait_ge(self.ready, b + 1)

    def wait_parts(self, eng, b=BATCH - 1):
        eng.wait_ge(self.parted, b + 1)

    def parts(self, a, e):
        return self.high[:, a:e], self.low[:, a:e]


def cross_attention(c, tag, H, D, score_scale, mask, **norm_args):
    nc, ps = c.nc, c.ps
    FB = H * D // P
    HB = H // FB
    GROUP = 4
    COLS = P // GROUP if FB == 1 else D
    GROUPS = H // GROUP
    PROBS = TPB
    biased = FB == 1
    with ExitStack() as ctx:
        wq, wk, wv = (c.sb(ctx, f"{tag}_w{n}", [P, FB * P]) for n in "qkv")
        wo = c.sb(ctx, f"{tag}_wo", [P, FB, P])
        bq = c.sb(ctx, f"{tag}_bq", [P, 1])
        kT = c.sb(ctx, f"{tag}_kT", [P, FB, BATCH * KEYS])
        kdiag = c.sb(ctx, f"{tag}_kdiag", [P, BATCH, FB, HB, KEYS])
        v_all, v_now = c.sb(ctx, f"{tag}_v_all", [KEYS, BATCH, H, COLS]), c.sb(ctx, f"{tag}_v_now", [KEYS, H, COLS])
        qT = c.sb(ctx, f"{tag}_qT", [P, FB, SEQ])
        prob, top = c.sb(ctx, f"{tag}_prob", [P, PROBS, H * KEYS]), c.sb(ctx, f"{tag}_top", [P, HALVES, H])
        probT = c.sb(ctx, f"{tag}_probT", [KEYS, H, P])
        rsum = c.sb(ctx, f"{tag}_rsum", [P, PROBS, H])
        mixedT = c.sb(ctx, f"{tag}_mixedT", [P, FB * P])
        masks = c.sb(ctx, f"{tag}_masks", [P, TILES, KEYS]) if mask == "scaled" else None
        keep = c.sb(ctx, f"{tag}_keep", [P, BATCH, KEYS], U8) if mask == "barred" else None
        barred = c.sb(ctx, f"{tag}_barred", [P, BATCH, KEYS]) if mask == "barred" else None
        norm = Norm(c, ctx, tag, banks=3 if FB == 1 else 2, **norm_args)
        w_in, mask_in, order, prepared, bias_added = (c.sem(f"{tag}_{n}") for n in ("w_in", "mask_in", "order", "prepared", "bias_added"))
        k_done, kT_ready, kdiag_ready, v_done, v_clear, v_ready, v_placed = (c.sem(f"{tag}_{n}") for n in (
            "k_done", "kT_ready", "kdiag_ready", "v_done", "v_clear", "v_ready", "v_placed"))
        q_done, q_ready, scored, masked, shifted, exped = (c.sem(f"{tag}_{n}") for n in (
            "q_done", "q_ready", "scored", "masked", "shifted", "exped"))
        summed, normed, turned, turn_read, pv_done, mixed_ready, y_done, y_added = (c.sem(f"{tag}_{n}") for n in (
            "summed", "normed", "turned", "turn_read", "pv_done", "mixed_ready", "y_done", "y_added"))
        score_read = shifted if mask is None else masked
        PV, Y, Q = 5, 6, (7, 4)
        if FB == 1:
            K_AT, V_AT, TURN = (0,), Y, 3
            flat = ps[:, 0:3, :].rearrange("p b n -> p (b n)")[:, 0:H * KEYS]
            cuts = [(a, min(a + 512, H * KEYS)) for a in range(0, H * KEYS, 512)]
            heads = flat.rearrange("p (g h k) -> p g h k", g=1, h=H)
        else:
            K_AT, V_AT, TURN = (0, 1, 4, 5), (0, 1, 4, 5), 2
            heads = ps[:, 0:2, 0:H // 2 * KEYS].rearrange("p g (h k) -> p g h k", h=H // 2)
        G = heads.shape[1]
        HALF = H // 2

        def later(n, k):
            return not isinstance(n, int) or 0 <= n + k < TILES

        with nc.Block() as block:
            @block.sync
            def _(sp):
                for sb, name in ((wk, "wk"), (wv, "wv"), (wq, "wq"), (wo, "wo")):
                    sp.dma_start(sb[:], c.dram[f"{tag}_{name}"]).then_inc(w_in, 16)
                if mask is not None:
                    sp.dma_start((masks if keep is None else keep)[:], c.dram[f"{tag}_mask"]).then_inc(mask_in, 16)

            @block.gpsimd
            def _(pool):
                if biased:
                    pool.memset(v_all[:], 0.0).then_inc(v_clear, 1)
                member = c.head16[:].rearrange("p (a g) -> p g a", g=GROUP) if FB == 1 else c.pairsum[:, 0:P:D].unsqueeze(1)
                for j in range(FB):
                    pool.wait_ge(kT_ready, j + 1)
                    for b in range(BATCH):
                        pool.tensor_tensor(kdiag[:, b, j].rearrange("p (g a) k -> p g a k", g=member.shape[1]),
                                           bcast(kT[:, j, b * KEYS:(b + 1) * KEYS], list(member.shape[1:]) + [None]),
                                           bcast(member, [None, None, KEYS]), ALU.mult).then_inc(kdiag_ready, 1)
                if biased:
                    norm.wait(pool)
                    pool.tensor_tensor(c.resid[:], c.resid[:], bcast(c.row(f"{tag}_bo"), [TILES, None]), ALU.add).then_inc(bias_added, 1)

                def divide(n, i):
                    for x in range(2):
                        pool.wait_ge(summed, n * 2 + x + 1)
                        half = slice(x * HALF, (x + 1) * HALF)
                        grid = prob[:, i % PROBS, :].rearrange("p (h k) -> p h k", h=H)[:, half]
                        pool.tensor_tensor(grid, grid, bcast(rsum[:, i % PROBS, half], [None, KEYS]), ALU.mult).then_inc(normed, 1)

                for n in range(2):
                    divide(n, n)
                with pool.Fori(0, BATCH - 1) as b:
                    for i in range(TPB):
                        divide(b * TPB + i + 2, i + 2)
                for n in range(TILES - TPB + 2, TILES):
                    divide(n, n)

            @block.tensor
            def _(pe):
                pe.wait_ge(w_in, 64)
                for j in range(FB):
                    pe.matmul(ps[:, K_AT[j], 0:BATCH * KEYS], wk[:, j * P:(j + 1) * P], c.ctxT[:].rearrange("p b k -> p (b k)"),
                              start=True, stop=True).then_inc(k_done, 1)
                for b in range(BATCH):
                    if FB > 1:
                        pe.wait_ge(kT_ready, b + 1)
                    at = ps[0:KEYS, V_AT, b * P:(b + 1) * P] if FB == 1 else ps[0:KEYS, V_AT[b], :]
                    pe.matmul(at, c.ctxT[:, b, :], wv[:], start=True, stop=True).then_inc(v_done, 1)
                norm.tensor(pe)

                def queries(b, j):
                    if j >= 2:
                        pe.wait_ge(q_ready, b * FB + j - 1)
                    pe.matmul(ps[:, Q[j % 2], :], wq[:, j * P:(j + 1) * P], c.normT[:, bass.ds(b * SEQ, SEQ)], start=True, stop=True).then_inc(q_done, 1)

                def scores(n, b, i):
                    if i == 0:
                        pe.wait_ge(q_ready, b * FB + FB)
                    if later(n, -1):
                        pe.wait_ge(score_read, n)
                    t = i * P
                    keys = kdiag[:, bass.ds(b, 1)]
                    if FB == 1:
                        for a, e in cuts:
                            last = pe.matmul(flat[:, a:e], qT[:, 0, t:t + P], keys.rearrange("p b j h k -> p (b j h k)")[:, a:e], start=True, stop=True)
                    else:
                        for j in range(FB):
                            last = pe.matmul(ps[:, j // 2, j % 2 * HB * KEYS:(j % 2 + 1) * HB * KEYS], qT[:, j, t:t + P],
                                             keys[:, :, j].rearrange("p b h k -> p (b h k)"), start=True, stop=True)
                    last.then_inc(scored, 1)

                def turn(n, i, g):
                    pe.wait_ge(normed, n * 2 + g * 2 // GROUPS + 1)
                    if g >= 2:
                        pe.wait_ge(turn_read, n * GROUPS + g - 1)
                    for a in range(GROUP):
                        h = g * GROUP + a
                        last = pe.transpose(ps[0:KEYS, TURN + g % 2, a * P:(a + 1) * P], prob[:, i, h * KEYS:(h + 1) * KEYS], c.ident[:])
                    last.then_inc(turned, 1)

                def product(n, b, i, g):
                    if g == 0 and i == 0:
                        pe.wait_ge(v_placed, b + 1)
                    pe.wait_ge(turn_read, n * GROUPS + g + 1)
                    for a in range(GROUP):
                        h = g * GROUP + a
                        if FB == 1:
                            last = pe.matmul(ps[a * COLS:(a + 1) * COLS, PV, 0:P], v_now[:, h, :], probT[:, h, :], start=(g == 0), stop=(g == GROUPS - 1))
                        else:
                            last = pe.matmul(ps[h % 2 * D:(h % 2 + 1) * D, PV, h // 2 * P:(h // 2 + 1) * P], v_now[:, h, :], probT[:, h, :], start=True, stop=True)
                    if g == GROUPS - 1:
                        last.then_inc(pv_done, 1)

                def output(n):
                    pe.wait_ge(mixed_ready, n + 1)
                    pe.wait_ge(y_added, n + 1)
                    for j in range(FB):
                        last = pe.matmul(ps[:, Y, 0:P], mixedT[:, j * P:(j + 1) * P], wo[:, j, :], start=(j == 0), stop=(j == FB - 1))
                    last.then_inc(y_done, 1)

                def tile(n, b, i):
                    more = later(n, TPB)
                    project = list(range(FB)) if i == 0 and more else []

                    def next_queries():
                        if project:
                            queries(b + 1, project.pop(0))

                    next_queries()
                    turn(n, i, 0)
                    next_queries()
                    turn(n, i, 1)
                    next_queries()
                    product(n, b, i, 0)
                    next_queries()
                    for g in range(1, GROUPS):
                        if g + 1 < GROUPS:
                            turn(n, i, g + 1)
                        product(n, b, i, g)
                    if more:
                        scores(n + TPB, b + 1, i)
                    output(n)

                pe.wait_ge(kdiag_ready, BATCH * FB)
                if not biased:
                    pe.wait_ge(v_ready, BATCH)
                norm.wait(pe, 0)
                for j in range(FB):
                    queries(0, j)
                for n in range(TPB):
                    scores(n, 0, n)
                norm.wait(pe)
                with pe.Fori(0, BATCH - 1) as b:
                    for i in range(TPB):
                        tile(b * TPB + i, b, i)
                for i in range(TPB):
                    tile((BATCH - 1) * TPB + i, BATCH - 1, i)

            @block.scalar
            def _(act):
                if biased:
                    act.wait_ge(k_done, 1)
                    act.activation(kT[:, 0, :], ps[:, K_AT[0], 0:BATCH * KEYS], ACT.Identity, bias=c.vec(f"{tag}_bk")).then_inc(kT_ready, 1)
                else:
                    for j in range(FB):
                        act.wait_ge(k_done, j + 1)
                        act.activation(kT[:, j, :], ps[:, K_AT[j], 0:BATCH * KEYS], ACT.Copy).then_inc(kT_ready, 1)
                    for b in range(BATCH):
                        act.wait_ge(v_done, b + 1)
                        act.activation(v_all[:, b].rearrange("k h v -> k (h v)"), ps[0:KEYS, V_AT[b], :], ACT.Copy).then_inc(v_ready, 1)
                norm.scalar(act)

                def queries(b, j):
                    act.wait_ge(q_done, b * FB + j + 1)
                    if biased:
                        act.activation(qT[:, j, :], ps[:, Q[j % 2], :], ACT.Identity, bias=bq[:], scale=score_scale).then_inc(q_ready, 1)
                    else:
                        act.activation(qT[:, j, :], ps[:, Q[j % 2], :], ACT.Copy, scale=score_scale).then_inc(q_ready, 1)

                def exps(n, i):
                    act.wait_ge(shifted, n + 1)
                    act.activation(prob[:, i % PROBS, :], prob[:, i % PROBS, :], ACT.Exp).then_inc(exped, 1)

                def group_turned(n, g):
                    act.wait_ge(turned, n * GROUPS + g + 1)
                    act.activation(probT[:, g * GROUP:(g + 1) * GROUP, :].rearrange("k h t -> k (h t)"), ps[0:KEYS, TURN + g % 2, :], ACT.Copy).then_inc(turn_read, 1)

                def mixed(n):
                    act.wait_ge(pv_done, n + 1)
                    act.activation(mixedT[:], ps[:, PV, 0:FB * P], ACT.Copy).then_inc(mixed_ready, 1)

                def tile(n, b, i):
                    project = list(range(FB)) if i == 0 and later(n, TPB) else []
                    for g in range(GROUPS):
                        if project:
                            queries(b + 1, project.pop(0))
                        group_turned(n, g)
                    for j in project:
                        queries(b + 1, j)
                    mixed(n)
                    if later(n, 3):
                        exps(n + 3, i + 3)

                if biased:
                    act.wait_ge(prepared, 1)
                for j in range(FB):
                    queries(0, j)
                for n in range(3):
                    exps(n, n)
                with act.Fori(0, BATCH - 1) as b:
                    for i in range(TPB):
                        tile(b * TPB + i, b, i)
                for i in range(TPB):
                    tile((BATCH - 1) * TPB + i, BATCH - 1, i)

            @block.vector
            def _(dve):
                if biased:
                    dve.tensor_scalar(bq[:], c.vec(f"{tag}_bq"), score_scale, None, ALU.mult).then_inc(prepared, 1)
                if mask is not None:
                    dve.wait_ge(mask_in, 16)
                if mask == "barred":
                    dve.tensor_scalar(barred[:], keep[:], -1.0, 1e38, ALU.add, ALU.mult).then_inc(prepared, 1)
                norm.vector(dve)
                if biased:
                    dve.wait_ge(v_clear, 1)
                    dve.wait_ge(v_done, BATCH)
                    for g in range(GROUP):
                        dve.tensor_tensor(v_all[:].rearrange("k b (g a) v -> k b g a v", g=GROUP)[:, :, g, :, g * D:(g + 1) * D],
                                          ps[0:KEYS, V_AT, :].rearrange("k (b a g v) -> k b g a v", b=BATCH, a=GROUP, g=GROUP)[:, :, g],
                                          bcast(c.row(f"{tag}_bv")[0:KEYS].rearrange("k (a g v) -> k g a v", a=GROUP, g=GROUP)[:, g], [BATCH, None, None]),
                                          ALU.add).then_inc(v_ready, 1)
                step = InOrder(dve, order)

                def shift(n, b, i, base):
                    grid = prob[:, i % PROBS, :].rearrange("p (g h k) -> p g h k", g=G, k=KEYS)
                    best = top[:, i % 2, :].rearrange("p (g h) -> p g h", g=G)
                    dve.wait_ge(scored, n + 1)
                    source = heads
                    if mask == "scaled":
                        dve.scalar_tensor_tensor(out=grid.rearrange("p g h k -> p (g h) k"), in0=bcast(masks[:, bass.ds(n, 1), :].rearrange("p a k -> p (a k)"), [H, None]),
                                                 scalar=-1e9, in1=heads.rearrange("p g h k -> p (g h) k"), op0=ALU.mult, op1=ALU.add).then_inc(masked, 1)
                    if mask == "barred":
                        dve.tensor_tensor(grid, heads, bcast(barred[:, bass.ds(b, 1), :].rearrange("p b k -> p (b k)"), [G, H // G, None]),
                                          ALU.add).then_inc(masked, 1)
                    if mask is not None:
                        dve.wait_ge(masked, n + 1)
                        source = grid
                    step(dve.tensor_reduce(best, source, AX.X, ALU.max), base)
                    dve.tensor_tensor(grid, source, bcast(best, [None, None, KEYS]), ALU.subtract).then_inc(shifted, 1)

                def add_up(n, i, base):
                    dve.wait_ge(exped, n + 1)
                    for x in range(2):
                        half = slice(x * HALF, (x + 1) * HALF)
                        sums = rsum[:, i % PROBS, half]
                        step(dve.tensor_reduce(sums, prob[:, i % PROBS, :].rearrange("p (h k) -> p h k", h=H)[:, half], AX.X, ALU.add), base)
                        dve.reciprocal(sums, sums).then_inc(summed, 1)

                def add(n):
                    dve.wait_ge(y_done, n + 1)
                    x = c.resid[:, bass.ds(n, 1), :].rearrange("p t d -> p (t d)")
                    dve.tensor_tensor(x, ps[:, Y, 0:P], x, ALU.add).then_inc(y_added, 1)

                def place_v(b):
                    dve.tensor_copy(v_now[:].rearrange("k h v -> k (h v)"), v_all[:, bass.ds(b, 1)].rearrange("k b h v -> k (b h v)")).then_inc(v_placed, 1)

                def tile(n, b, i, base):
                    if later(n, 3):
                        shift(n + 3, b + (i + 3) // TPB, i + 3, base)
                    if later(n, 2):
                        add_up(n + 2, i + 2, base)
                    add(n)
                    if i == TPB - 1 and later(n, 1):
                        place_v(b + 1)

                dve.wait_ge(v_ready, BATCH if not biased else GROUP)
                place_v(0)
                dve.engine_nop().then_inc(y_added, 1)
                if mask == "barred":
                    dve.wait_ge(prepared, 1)
                for n in range(3):
                    shift(n, 0, n, 0)
                    if n > 0:
                        add_up(n - 1, n - 1, 0)
                if biased:
                    dve.wait_ge(bias_added, 1)
                first, PER = step.n, 3 * TPB
                with dve.Fori(0, BATCH - 1) as b:
                    step.n = first
                    for i in range(TPB):
                        tile(b * TPB + i, b, i, b * PER)
                for i in range(TPB):
                    tile((BATCH - 1) * TPB + i, BATCH - 1, i, (BATCH - 2) * PER)
                dve.wait_ge(y_added, TILES + 1)


class TopK:

    def __init__(self, c, ctx, tag, width, k, tiles=TILES):
        self.c, self.width, self.k, self.tiles = c, width, k, tiles
        self.top = c.sb(ctx, f"{tag}_top", [P, tiles, 8])
        self.place = c.sb(ctx, f"{tag}_place", [P, tiles, 8], U32)
        self.placef = c.sb(ctx, f"{tag}_placef", [P, tiles, 8])
        self.hit = c.sb(ctx, f"{tag}_hit", [P, tiles, width, k])

    def find(self, dve, step, rows):
        for n in range(self.tiles):
            last = self.lead(dve, rows, n)
        step(last)
        for n in range(self.tiles):
            last = self.locate(dve, rows, n)
        step(last)
        self.number(dve, step)

    def lead(self, dve, rows, n):
        return dve.max(self.top[:, n, :], rows[:, n, :])

    def locate(self, dve, rows, n):
        return dve.max_index(self.place[:, n, :], self.top[:, n, :], rows[:, n, :])

    def number(self, dve, step):
        step(dve.tensor_copy(self.placef[:], self.place[:]))

    def spread(self, dve, step, weights, out):
        self.mark(dve, step)
        self.weigh(dve, step, weights)
        self.collect(dve, step, out)

    def mark(self, dve, step):
        step(dve.tensor_tensor(self.hit[:], bcast(self.c.count12[:, 0:self.width], [self.tiles, None, self.k]),
                               bcast(self.placef[:, :, 0:self.k], [None, self.width, None]), ALU.is_equal))

    def weigh(self, dve, step, weights):
        step(dve.tensor_tensor(self.hit[:], self.hit[:], bcast(weights, [None, self.width, None]), ALU.mult))

    def collect(self, dve, step, out):
        step(dve.tensor_reduce(out, self.hit[:], AX.X, ALU.add))


class Softmax:

    def __init__(self, c, ctx, tag, n, tiles=TILES):
        self.c, self.n = c, n
        self.lead = c.sb(ctx, f"{tag}_lead", [P, tiles])
        self.exps = c.sb(ctx, f"{tag}_exps", [P, tiles, n])
        self.shifted, self.exped = c.sem(f"{tag}_rows_shifted"), c.sem(f"{tag}_rows_exped")

    def vector(self, dve, step, rows, lead=None):
        if lead is None:
            step(dve.tensor_reduce(self.lead[:], rows, AX.X, ALU.max))
            lead = self.lead[:]
        self.shift(dve, rows, lead)
        self.divide(dve, step)

    def shift(self, dve, rows, lead):
        dve.tensor_tensor(self.exps[:], rows, bcast(lead, [None, self.n]), ALU.subtract).then_inc(self.shifted, 1)

    def divide(self, dve, step):
        dve.wait_ge(self.exped, 1)
        step(dve.tensor_reduce(self.lead[:], self.exps[:], AX.X, ALU.add))
        step(dve.reciprocal(self.lead[:], self.lead[:]))
        step(dve.tensor_tensor(self.exps[:], self.exps[:], bcast(self.lead[:], [None, self.n]), ALU.mult))

    def scalar(self, act):
        act.wait_ge(self.shifted, 1)
        act.activation(self.exps[:], self.exps[:], ACT.Exp).then_inc(self.exped, 1)


class TopTwo:
    E, FIRST = 8, 0

    def __init__(self, c, ctx, norm):
        self.c, self.norm = c, norm
        self.wg = c.sb(ctx, "L0f_wg", [P, self.E])
        self.rows = c.sb(ctx, "L0f_rows", [P, TILES, self.E])
        self.weight = c.sb(ctx, "L0f_weight", [P, TILES, self.E])
        self.total = c.sb(ctx, "L0f_total", [P, TILES])
        self.own = c.sb(ctx, "L0f_own", [P, TILES, P])
        self.top = TopK(c, ctx, "L0f", self.E, 2)
        self.soft = Softmax(c, ctx, "L0f", 2)
        self.w_in, self.scored, self.order = c.sem("L0f_wg_in"), c.sem("L0f_scored"), c.sem("L0f_route_order")

    def sync(self, sp):
        sp.dma_start(self.wg[:], self.c.dram["L0f_wg"]).then_inc(self.w_in, 16)

    def tensor(self, pe):
        pe.wait_ge(self.w_in, 16)
        for n in range(TILES):
            last = pe.matmul(self.c.ps[:, 7, n * self.E:(n + 1) * self.E], self.c.normT[:, n * P:(n + 1) * P], self.wg[:], start=True, stop=True)
        last.then_inc(self.scored, 1)

    def scalar(self, act):
        self.soft.scalar(act)

    def vector(self, dve):
        c, norm, step = self.c, self.norm, InOrder(dve, self.order)
        dve.wait_ge(self.scored, 1)
        step(dve.tensor_tensor(self.rows[:], c.ps[:, 7, 0:TILES * self.E].rearrange("p (n e) -> p n e", n=TILES),
                               bcast(norm.std2[:], [None, self.E]), ALU.mult))
        self.top.find(dve, step, self.rows)
        self.soft.vector(dve, step, self.top.top[:, :, 0:2], self.top.top[:, :, 0])
        self.top.spread(dve, step, self.soft.exps[:], self.weight[:])
        step(dve.tensor_reduce(self.total[:], self.weight[:], AX.X, ALU.add))
        step(dve.tensor_tensor(self.total[:], self.total[:], norm.rstd[:], ALU.mult))
        for n in range(TILES):
            last = dve.tensor_scalar(self.own[:, n, :], c.resid[:, n, :], norm.mean[:, n:n + 1], self.total[:, n:n + 1], ALU.subtract, ALU.mult)
        step(last)
        step(dve.tensor_tensor(c.resid[:], c.resid[:], self.own[:], ALU.add))


class Sampled:
    E, FIRST = 8, 0
    HID, KMAX = 50, 6

    def __init__(self, c, ctx, norm):
        self.c = c
        self.wr = c.sb(ctx, "L1f_wr", [P, self.E])
        self.a1 = c.sb(ctx, "L1f_a1", [P, self.HID])
        self.a2 = c.sb(ctx, "L1f_a2", [self.HID, self.KMAX])
        self.hid = c.sb(ctx, "L1f_hid", [self.HID, TILES * P])
        self.rows = c.sb(ctx, "L1f_rows", [P, TILES, self.E])
        self.choice = c.sb(ctx, "L1f_choice", [P, TILES, 8])
        self.keep = c.sb(ctx, "L1f_keep", [P, TILES, self.E])
        self.weight = c.sb(ctx, "L1f_weight", [P, TILES, self.E])
        self.top = TopK(c, ctx, "L1f", self.E, self.E)
        self.pick = TopK(c, ctx, "L1f_pick", 8, 1)
        self.soft = Softmax(c, ctx, "L1f", self.E)
        self.w_in, self.scored, self.order = c.sem("L1f_wr_in"), c.sem("L1f_scored"), c.sem("L1f_route_order")
        self.hid_done, self.hid_ready = c.sem("L1f_actor_done"), c.sem("L1f_actor_ready")

    def sync(self, sp):
        for sb, name in ((self.wr, "L1f_wr"), (self.a1, "L1f_a1"), (self.a2, "L1f_a2")):
            sp.dma_start(sb[:], self.c.dram[name]).then_inc(self.w_in, 16)

    def tensor(self, pe):
        c = self.c
        pe.wait_ge(self.w_in, 48)
        for n in range(TILES):
            last = pe.matmul(c.ps[:, 7, n * self.E:(n + 1) * self.E], c.normT[:, n * P:(n + 1) * P], self.wr[:], start=True, stop=True)
        last.then_inc(self.scored, 1)
        for b in range(BATCH):
            pe.matmul(c.ps[0:self.HID, b, :], self.a1[:], c.normT[:, b * SEQ:(b + 1) * SEQ], start=True, stop=True).then_inc(self.hid_done, 1)
        pe.wait_ge(self.hid_ready, BATCH)
        for n in range(TILES):
            last = pe.matmul(c.ps[:, 6, n * 8:n * 8 + self.KMAX], self.hid[:, n * P:(n + 1) * P], self.a2[:], start=True, stop=True)
        last.then_inc(self.scored, 1)

    def scalar(self, act):
        for b in range(BATCH):
            act.wait_ge(self.hid_done, b + 1)
            act.activation(self.hid[:, b * SEQ:(b + 1) * SEQ], self.c.ps[0:self.HID, b, :], ACT.Gelu_apprx_tanh,
                           bias=self.c.vec("L1f_b1")[0:self.HID]).then_inc(self.hid_ready, 1)
        self.soft.scalar(act)

    def vector(self, dve):
        c, step = self.c, InOrder(dve, self.order)
        step(dve.memset(self.choice[:], -1e30))
        dve.wait_ge(self.scored, 1)
        step(dve.tensor_copy(self.rows[:], c.ps[:, 7, 0:TILES * self.E].rearrange("p (n e) -> p n e", n=TILES)))
        self.soft.vector(dve, step, self.rows[:])
        self.top.find(dve, step, self.soft.exps)
        dve.wait_ge(self.scored, 2)
        logits = self.choice[:, :, 0:self.KMAX]
        step(dve.tensor_tensor(logits, c.ps[:, 6, 0:TILES * 8].rearrange("p (n k) -> p n k", n=TILES)[:, :, 0:self.KMAX],
                               bcast(c.row("L1f_b2")[:, 0:self.KMAX], [TILES, None]), ALU.add))
        step(dve.tensor_scalar(logits, logits, -30.0, 30.0, ALU.max, ALU.min))
        self.pick.find(dve, step, self.choice)
        step(dve.tensor_tensor(self.keep[:], bcast(c.count12[:, 0:self.E], [TILES, None]),
                               bcast(self.pick.placef[:, :, 0], [None, self.E]), ALU.is_le))
        step(dve.tensor_tensor(self.keep[:], self.keep[:], self.top.top[:], ALU.mult))
        self.top.spread(dve, step, self.keep[:], self.weight[:])


class TopProbs:
    E, FIRST = 9, 1

    def __init__(self, c, ctx, norm):
        self.c = c
        self.wr = c.sb(ctx, "L3f_wr", [P, 8])
        self.rows = c.sb(ctx, "L3f_rows", [P, TILES, 8])
        self.weight = c.sb(ctx, "L3f_weight", [P, TILES, 9])
        self.top = TopK(c, ctx, "L3f", 8, 2)
        self.soft = Softmax(c, ctx, "L3f", 8)
        self.w_in, self.scored, self.order = c.sem("L3f_wr_in"), c.sem("L3f_scored"), c.sem("L3f_route_order")

    def sync(self, sp):
        sp.dma_start(self.wr[:], self.c.dram["L3f_wr"]).then_inc(self.w_in, 16)

    def tensor(self, pe):
        pe.wait_ge(self.w_in, 16)
        for n in range(TILES):
            last = pe.matmul(self.c.ps[:, 7, n * 8:(n + 1) * 8], self.c.normT[:, n * P:(n + 1) * P], self.wr[:], start=True, stop=True)
        last.then_inc(self.scored, 1)

    def scalar(self, act):
        self.soft.scalar(act)

    def vector(self, dve):
        c, step = self.c, InOrder(dve, self.order)
        step(dve.memset(self.weight[:], 1.0))
        dve.wait_ge(self.scored, 1)
        step(dve.tensor_tensor(self.rows[:], c.ps[:, 7, 0:TILES * 8].rearrange("p (n e) -> p n e", n=TILES),
                               bcast(c.row("L3f_rb")[:, 0:8], [TILES, None]), ALU.add))
        self.soft.vector(dve, step, self.rows[:])
        self.top.find(dve, step, self.soft.exps)
        self.top.spread(dve, step, self.top.top[:, :, 0:2], self.weight[:, :, 1:9])


def experts(c, tag, router_kind, kind, R, F, inner_eps=None):
    nc, ps = c.nc, c.ps
    gated, folded = kind == "swiglu", kind == "relu"
    W1 = 2 * R * F if gated else R * F
    GAIN, SHIFT = W1 + F, W1 + F + 1
    PACKED = {"relu": SHIFT + 1, "gelu": W1 + F, "swiglu": W1}[kind]
    SLOTS = F if gated else 4
    YBANK = 6 if gated else 4
    func = {"relu": ACT.Relu, "gelu": ACT.Gelu, "swiglu": ACT.Silu}[kind]
    with ExitStack() as ctx:
        norm = Norm(c, ctx, tag, inner_eps, banks=6, split=True)
        route = router_kind(c, ctx, norm)
        E = route.E
        PAIRS = E // HALVES
        tail_expert = E % HALVES
        w1 = c.sb(ctx, f"{tag}_w1", [P, HALVES, PACKED])
        w2 = c.sb(ctx, f"{tag}_w2", [R, HALVES, F, P])
        hid = c.sb(ctx, f"{tag}_hidden", [R, HALVES, F, SEQ])
        w1g = c.sb(ctx, f"{tag}_w1g", [P, HALVES, W1]) if folded else w1
        high, low = (c.sb(ctx, f"{tag}_w1_{n}", [P, HALVES, W1], F32R) for n in ("high", "low"))
        b1 = c.sb(ctx, f"{tag}_b1", [P, HALVES, F]) if folded else None
        gate = c.sb(ctx, f"{tag}_gate", [R, F, SEQ]) if gated else None
        w_in = c.pair(f"{tag}_w_in")
        hid_done, gate_ready, hid_ready = (c.sem(f"{tag}_{n}") for n in ("hid_done", "gate_ready", "hid_ready"))
        out_done, out_added = c.sem(f"{tag}_out_done"), c.pair(f"{tag}_out_added")
        parted, part_order, shift_done, shift_ready = (c.sem(f"{tag}_{n}") for n in ("w1_parted", "w1_part_order", "shift_done", "shift_ready"))
        if not gated:
            b2 = c.sb(ctx, f"{tag}_b2", [E, P])
            weightT = c.sb(ctx, f"{tag}_weightT", [E, SEQ])
            b2_in, wT_done, wT_ready, b2_done, b2_added = (c.sem(f"{tag}_{n}") for n in ("b2_in", "wT_done", "wT_ready", "b2_done", "b2_added"))
        routed = c.sem(f"{tag}_routed")
        MM = 2 if gated else 1

        def steps(eng, make, use, bias=lambda i: None):
            def run(q, us, after, bias=lambda i: None):
                at = [(q, u, b) for u in us for b in range(BATCH)]
                for i, (now, then) in enumerate(zip(at, at[1:] + [after])):
                    if then is not None:
                        make(*then)
                    use(*now)
                    bias(i)

            with eng.Fori(0, PAIRS - 1) as q:
                run(q, range(HALVES), (q + 1, 0, 0))
            run(PAIRS - 1, range(HALVES), (PAIRS, 0, 0) if tail_expert else None, bias)
            if tail_expert:
                run(PAIRS, range(1), None)

        with nc.Block() as block:
            @block.sync
            def _(sp):
                def load(e, u):
                    sp.dma_start(w1[:, u, :], c.dram[f"{tag}_{'gu' if gated else 'w1'}"][bass.ds(e, 1)].rearrange(
                        "e d g f -> (e d) (g f)" if gated else "e d f -> (e d) f")).then_inc(w_in[u], 16)
                    sp.dma_start(w2[:, u], c.dram[f"{tag}_{'dn' if gated else 'w2'}"][bass.ds(e, 1)].rearrange(
                        "e r f d -> (e r) f d")).then_inc(w_in[u], 16)

                route.sync(sp)
                if not gated:
                    sp.dma_start(b2[:], c.dram[f"{tag}_b2"]).then_inc(b2_in, 16)
                for u in range(HALVES):
                    load(u, u)
                with sp.Fori(1, PAIRS) as q:
                    for u in range(HALVES):
                        sp.wait_ge(out_done, (q * HALVES + u - 1) * BATCH)
                        load(q * HALVES + u, u)
                if tail_expert:
                    sp.wait_ge(out_done, (E - 2) * BATCH)
                    load(E - 1, 0)

            @block.gpsimd
            def _(pool):
                def part(q, u):
                    e, x = q * HALVES + u, w1[:, u, 0:W1]
                    pool.wait_ge(w_in[u], q * 32 + 32)
                    gain = (w1[:, u, GAIN:GAIN + 1] if folded else c.one[:]).broadcast_to([P, W1])
                    if folded:
                        pool.tensor_tensor(w1g[:, u, :], x, gain, ALU.mult)
                    pool.tensor_tensor(high[:, u, :], x, gain, ALU.mult).then_inc(part_order, 1)
                    pool.wait_ge(part_order, e + 1)
                    pool.tensor_tensor(low[:, u, :], w1g[:, u, 0:W1], high[:, u, :], ALU.subtract).then_inc(parted, 1)

                with pool.Fori(0, PAIRS) as q:
                    for u in range(HALVES):
                        part(q, u)
                if tail_expert:
                    part(PAIRS, 0)

            @block.tensor
            def _(pe):
                norm.tensor(pe)

                def hidden(q, u, b):
                    e = q * HALVES + u
                    s = e * BATCH + b
                    if b == 0:
                        pe.wait_ge(w_in[u], q * 32 + 32)
                        pe.wait_ge(parted, e + 1)
                        if folded:
                            if not isinstance(e, int) or e > 0:
                                pe.wait_ge(shift_ready, e)
                            for f in range(F):
                                last = pe.matmul(ps[:, 6, f:f + 1], w1[:, u, f * R:(f + 1) * R],
                                                 w1[:, u, SHIFT:SHIFT + 1], start=True, stop=True)
                            last.then_inc(shift_done, 1)
                    if not isinstance(s, int) or s > 0:
                        pe.wait_ge(hid_ready, s * F)
                    for f in range(F):
                        slot = (b * F + f) % SLOTS
                        for m in range(MM):
                            at = slice((m * F + f) * R, (m * F + f + 1) * R)
                            split_product(pe, ps[0:R, m * SLOTS + slot, :], (high[:, u, at], low[:, u, at]),
                                          norm.parts(b * SEQ, (b + 1) * SEQ)).then_inc(hid_done, 1)

                def result(q, u, b):
                    s = (q * HALVES + u) * BATCH + b
                    pe.wait_ge(hid_ready, s * F + F)
                    pe.wait_ge(out_added[b % 2], (q * HALVES + u) * (BATCH // 2) + b // 2 + 1)
                    for t in range(TPB):
                        for f in range(F):
                            last = pe.matmul(ps[:, YBANK + b % 2, t * P:(t + 1) * P], hid[:, b % 2, f, t * P:(t + 1) * P],
                                             w2[:, u, f, :], start=(f == 0), stop=(f == F - 1))
                    last.then_inc(out_done, 1)

                def bias(i):
                    b = i // 2
                    if i == 0:
                        pe.wait_ge(b2_in, 16)
                        pe.wait_ge(routed, 1)
                    if i % 2 == 0:
                        if b > 0:
                            pe.wait_ge(b2_added, b)
                        for t in range(TPB):
                            last = pe.transpose(ps[0:E, 7, t * P:(t + 1) * P], route.weight[:, b * TPB + t, :], c.ident[:])
                        last.then_inc(wT_done, 1)
                    else:
                        pe.wait_ge(wT_ready, b + 1)
                        for t in range(TPB):
                            last = pe.matmul(ps[:, 7, t * P:(t + 1) * P], weightT[:, t * P:(t + 1) * P], b2[:], start=True, stop=True)
                        last.then_inc(b2_done, 1)

                norm.wait(pe, BATCH - 1 if folded else 0)
                norm.wait_parts(pe, 0)
                hidden(0, 0, 0)
                norm.wait(pe)
                if gated:
                    pe.wait_ge(hid_ready, F)
                route.tensor(pe)
                norm.wait_parts(pe)
                if gated:
                    steps(pe, hidden, result)
                else:
                    steps(pe, hidden, result, bias)

            @block.scalar
            def _(act):
                norm.scalar(act)

                def activate(q, u, b):
                    e = q * HALVES + u
                    s = e * BATCH + b
                    if folded and b == 0:
                        act.wait_ge(shift_ready, e + 1)
                    for f in range(F):
                        slot = (b * F + f) % SLOTS
                        act.wait_ge(hid_done, (s * F + f) * MM + 1)
                        if gated:
                            act.activation(gate[:, f, :], ps[0:R, slot, :], func).then_inc(gate_ready, 1)
                        else:
                            bias = b1[:, u, f:f + 1] if folded else w1[:, u, W1 + f:W1 + f + 1]
                            act.activation(hid[:, b % 2, f, :], ps[0:R, slot, :], func, bias=bias).then_inc(hid_ready, 1)

                def bias(i):
                    if i % 2 == 0:
                        act.wait_ge(wT_done, i // 2 + 1)
                        act.activation(weightT[:], ps[0:E, 7, :], ACT.Copy).then_inc(wT_ready, 1)

                activate(0, 0, 0)
                route.scalar(act)
                if gated:
                    steps(act, activate, lambda q, u, b: None)
                else:
                    steps(act, activate, lambda q, u, b: None, bias)

            @block.vector
            def _(dve):
                norm.vector(dve)
                flat = route.weight[:].rearrange("p n e -> p (n e)")

                def add(q, u, b):
                    e = q * HALVES + u
                    s = e * BATCH + b
                    dve.wait_ge(out_done, s + 1)
                    dve.wait_ge(out_added[b % 2], e * (BATCH // 2) + b // 2 + 1)
                    if biased[0]:
                        dve.wait_ge(b2_added, biased[0])
                    for t in range(TPB):
                        n = b * TPB + t
                        last = dve.scalar_tensor_tensor(out=c.resid[:, n, :], in0=ps[:, YBANK + b % 2, t * P:(t + 1) * P],
                                                        scalar=flat[:, bass.ds(n * E + e, 1)], in1=c.resid[:, n, :],
                                                        op0=ALU.mult, op1=ALU.add)
                    last.then_inc(out_added[b % 2], 1)

                def finish_hidden(q, u, b):
                    e = q * HALVES + u
                    s = e * BATCH + b
                    if folded and b == 0:
                        dve.wait_ge(shift_done, e + 1)
                        dve.tensor_tensor(b1[:, u, :], ps[:, 6, 0:F], w1[:, u, W1:W1 + F], ALU.add).then_inc(shift_ready, 1)
                    for f in range(F if gated else 0):
                        dve.wait_ge(gate_ready, s * F + f + 1)
                        dve.wait_ge(hid_done, (s * F + f) * MM + 2)
                        dve.tensor_tensor(hid[:, b % 2, f, :], gate[:, f, :], ps[0:R, SLOTS + f, :], ALU.mult).then_inc(hid_ready, 1)

                biased = [0]

                def bias(i):
                    if i % 2 == 1:
                        b = i // 2
                        x = c.resid[:, b * TPB:(b + 1) * TPB, :]
                        dve.wait_ge(b2_done, b + 1)
                        dve.wait_ge(out_added[b % 2], (PAIRS - 1) * HALVES * 2 + (i - b % 2) // 2 + 2)
                        dve.tensor_tensor(x, ps[:, 7, :].rearrange("p (t d) -> p t d", t=TPB), x, ALU.add).then_inc(b2_added, 1)
                        biased[0] += 1

                def results_may_come():
                    for h in range(2):
                        dve.engine_nop().then_inc(out_added[h], 1)

                finish_hidden(0, 0, 0)
                if not gated:
                    results_may_come()
                route.vector(dve)
                dve.engine_nop().then_inc(routed, 1)
                if gated:
                    results_may_come()
                if gated:
                    steps(dve, finish_hidden, add)
                else:
                    steps(dve, finish_hidden, add, bias)
                for h in range(2):
                    dve.wait_ge(out_added[h], E * 2 + 1)
                if not gated:
                    dve.wait_ge(b2_added, BATCH)


def latent_attention(c):
    nc, ps = c.nc, c.ps
    PAIRS, D = 8, 64
    NK = SEQ + KEYS
    KB = 5
    BK = (NK + KB - 1) // KB
    KH = (NK + 3) // 4 * 2
    KW = 2 * KH
    STEPS = 2 * TPB
    TURNS = PAIRS * BATCH
    RING = 4
    AHEAD = 3
    Q, V4, NORMS, Y, V1, KL, KC, NKL = range(STEPS)
    FOR = {Q: 1, V4: 1, NORMS: 1, Y: -1, V1: 1, KL: 2, KC: 2, NKL: 2}
    PROLOGUE = [(KL, 0), (KC, 0), (Q, 0), (NKL, 0), (V4, 0), (NORMS, 0), (V1, 0), (KL, 1), (KC, 1), (NKL, 1)]
    with ExitStack() as ctx:
        norm = Norm(c, ctx, "L1", inner_eps=1e-5, gain=c.vec("L1_lg"), shift=c.vec("L1_lb"), split=True)
        keysT = c.sb(ctx, "L1_keysT", [P, BATCH, KB * BK])
        w_all = c.sb(ctx, "L1_w_all", [P, PAIRS + 1, 3, P])
        wq, wk = c.sb(ctx, "L1_wq", [P, P]), c.sb(ctx, "L1_wk", [P, P])
        wk_high, wk_low, wq_high, wq_low = (c.sb(ctx, f"L1_{n}", [P, P], F32R) for n in ("wk_high", "wk_low", "wq_high", "wq_low"))
        wo = c.sb(ctx, "L1_wo", [P, PAIRS + 1, P])
        keep, barred = c.sb(ctx, "L1_keep", [P, BATCH, KEYS], U8), c.sb(ctx, "L1_barred", [P, BATCH, KW - SEQ])
        cx, cstage = c.sb(ctx, "L1_cx", [KEYS, BATCH, P]), c.sb(ctx, "L1_cstage", [KEYS, BATCH, P])
        cstats, cwork = c.sb(ctx, "L1_cstats", [KEYS, BATCH, 6]), c.sb(ctx, "L1_cwork", [KEYS, 6, BATCH])
        gains = c.sb(ctx, "L1_gains", [P, 1])
        kT = c.sb(ctx, "L1_kT", [P, 2, NK])
        q2_high, q2_low = (c.sb(ctx, f"L1_q2_{n}", [P, 2, 2, SEQ], F32R) for n in ("high", "low"))
        kT_high, kT_low = (c.sb(ctx, f"L1_kT_{n}", [P, 2, KW], F32R) for n in ("high", "low"))
        v, qinv = c.sb(ctx, "L1_v", [BK, 2, KB, P]), c.sb(ctx, "L1_qinv", [P, 2, STEPS])
        q_raw = c.sb(ctx, "L1_q_raw", [P, SEQ])
        ksq, qsq = c.sb(ctx, "L1_ksq", [P, NK]), c.sb(ctx, "L1_qsq", [P, SEQ])
        kinv, qms = c.sb(ctx, "L1_kinv", [P, NK]), c.sb(ctx, "L1_qms", [P, STEPS])
        top, low, sums, rsums = (c.sb(ctx, f"L1_{n}", [P, RING]) for n in ("top", "low", "sums", "rsums"))
        prob, probT = c.sb(ctx, "L1_prob", [P, RING, KW]), c.sb(ctx, "L1_probT", [BK, RING, KB, P])
        mixedT = c.sb(ctx, "L1_mixedT", [P, SEQ])
        w_in, ctx_in, keep_in, filled, tokens_in = (c.sem(f"L1_{n}") for n in ("w_in", "ctx_in", "keep_in", "filled", "tokens_in"))
        corder, cvar_ready, cstd_ready, cstaged, cturned, ctx_ready = (c.sem(f"L1_{n}") for n in (
            "corder", "cvar_ready", "cstd_ready", "cstaged", "cturned", "ctx_ready"))
        order, act_order, prepared, bias_added = (c.sem(f"L1_{n}") for n in ("order", "act_order", "prepared", "bias_added"))
        w_high_ready, w_ready, side_done, side_read, squared = (c.sem(f"L1_{n}") for n in ("w_high_ready", "w_ready", "side_done", "side_read", "squared"))
        kinv_ready, qinv_ready, k_ready = (c.sem(f"L1_{n}") for n in ("kinv_ready", "qinv_ready", "k_ready"))
        q_high_ready, q_parted, k_high_ready, k_parted, ctx_high_ready = (c.sem(f"L1_{n}") for n in ("q_high_ready", "q_parted", "k_high_ready", "k_parted", "ctx_high_ready"))
        scored, bounded, exped, summed, normed, turned, turn_read, mix_done, mixed_ready = (c.sem(f"L1_{n}") for n in (
            "scored", "bounded", "exped", "summed", "normed", "turned", "turn_read", "mix_done", "mixed_ready"))
        S = [ps[:, 2 * i:2 * i + 2, 0:KH] for i in range(2)]
        PT = ps[0:BK, 4:6, :].rearrange("p b n -> p (b n)")
        O = ps[:, 6, :]

        def use_of(turn, s):
            return len(PROLOGUE) + turn * STEPS + s

        def side_of(at):
            if isinstance(at, int) and at < len(PROLOGUE):
                return ps[:, 7 if at % 2 else 5, :], 2
            return ps[:, 7, :], 1

        def squares(turn, kind):
            return turn * 3 + {KL: 1, KC: 2, Q: 3}[kind]

        def scalings(turn, kind):
            return turn * 2 + {NKL: 1, NORMS: 2}[kind]

        def turns(eng, body):
            with eng.Fori(0, PAIRS) as p:
                for b in range(BATCH):
                    body(p, b, p * BATCH + b)

        def batch_of(b, kind):
            return (b + FOR[kind]) % BATCH

        with nc.Block() as block:
            @block.sync
            def _(sp):
                sp.dma_start(cx[:], c.dram["ctx"]).then_inc(ctx_in, 16)
                sp.dma_start(keep[:], c.dram["keep_L1"]).then_inc(keep_in, 16)
                weights = c.dram["L1_w"].rearrange("j p w f -> p j w f")
                sp.dma_start(w_all[:, 0:PAIRS], weights).then_inc(w_in, 16)
                sp.dma_start(w_all[:, PAIRS:PAIRS + 1], weights[:, 0:1]).then_inc(w_in, 16)
                out_rows = c.dram["L1_wo"].rearrange("j p d -> p j d")
                sp.dma_start(wo[:, 1:PAIRS + 1], out_rows).then_inc(w_in, 16)
                sp.dma_start(wo[:, 0:1], out_rows[:, 0:1]).then_inc(w_in, 16)

            @block.gpsimd
            def _(pool):
                pool.memset(q2_high[:].bitcast(F32), 0.0)
                pool.memset(q2_low[:].bitcast(F32), 0.0)
                pool.memset(kT_high[:, :, NK:KW].bitcast(F32), 0.0)
                pool.memset(kT_low[:, :, NK:KW].bitcast(F32), 0.0)
                pool.memset(barred[:, :, KEYS:KW - SEQ], -1e30)
                pool.memset(prob[:], 0.0)
                pool.memset(v[:, 1], 0.0)
                pool.memset(keysT[:, :, NK:KB * BK], 0.0).then_inc(filled, 1)
                pool.memset(probT[:], 0.0).then_inc(turn_read, 1)

                def take_weights(w, high, low, p, kind, n):
                    x = w_all[:, bass.ds(p, 1), kind].rearrange("p j f -> p (j f)")
                    pool.tensor_copy(w[:], x)
                    pool.tensor_tensor(high[:], x, c.one[:].broadcast_to([P, P]), ALU.mult).then_inc(w_high_ready, 1)
                    pool.wait_ge(w_high_ready, n + 1)
                    pool.tensor_tensor(low[:], w[:], high[:], ALU.subtract).then_inc(w_ready, 1)

                pool.wait_ge(w_in, 64)
                take_weights(wk, wk_high, wk_low, 0, 1, 0)
                take_weights(wq, wq_high, wq_low, 0, 0, 1)

                for b in range(BATCH):
                    norm.wait(pool, b)
                    pool.tensor_copy(keysT[:, b, 0:SEQ], c.normT[:, b * SEQ:(b + 1) * SEQ]).then_inc(tokens_in, 1)

                def scale_keys(turn, w, kind):
                    pool.wait_ge(kinv_ready, scalings(turn, kind))
                    if kind == NKL:
                        pool.tensor_tensor(kT[:, w, 0:SEQ], kT[:, w, 0:SEQ], kinv[:, 0:SEQ], ALU.mult).then_inc(k_ready, 1)
                    else:
                        x = kT[:, w, SEQ:NK]
                        pool.tensor_tensor(kT_high[:, w, SEQ:NK], x, kinv[:, SEQ:NK], ALU.mult)
                        pool.tensor_tensor(x, x, kinv[:, SEQ:NK], ALU.mult).then_inc(ctx_high_ready, 1)
                        pool.wait_ge(ctx_high_ready, turn + 1)
                        pool.tensor_tensor(kT_low[:, w, SEQ:NK], x, kT_high[:, w, SEQ:NK], ALU.subtract).then_inc(k_ready, 1)

                def low_keys(turn, w):
                    pool.wait_ge(k_high_ready, turn + 1)
                    pool.tensor_tensor(kT_low[:, w, 0:SEQ], kT[:, w, 0:SEQ], kT_high[:, w, 0:SEQ], ALU.subtract).then_inc(k_parted, 1)

                def divide(now, s):
                    pool.wait_ge(summed, now + 1)
                    x = prob[:, s % RING, 0:NK]
                    pool.tensor_tensor(x, x, rsums[:, s % RING:s % RING + 1].broadcast_to([P, NK]), ALU.mult).then_inc(normed, 1)

                scale_keys(0, 0, NKL)
                scale_keys(0, 0, NORMS)
                low_keys(0, 0)
                pool.tensor_tensor(c.resid[:], c.resid[:], bcast(c.row("L1_bout"), [TILES, None]), ALU.add).then_inc(bias_added, 1)
                for s in range(AHEAD - 1):
                    divide(s, s)

                def body(p, b, turn):
                    for s in range(STEPS):
                        if b == 2 and s == 0:
                            pool.wait_ge(side_done, use_of(turn, KC) - STEPS + 1)
                            take_weights(wk, wk_high, wk_low, p + 1, 1, p * 2 + 2)
                        if b == 2 and s == 2:
                            pool.wait_ge(side_done, use_of(turn, Q) + 1)
                            take_weights(wq, wq_high, wq_low, p + 1, 0, p * 2 + 3)
                        if s == 4:
                            scale_keys(turn + 1, (b + 1) % 2, NORMS)
                        divide(turn * STEPS + s + AHEAD - 1, s + AHEAD - 1)
                        if s == 1:
                            scale_keys(turn + 1, (b + 1) % 2, NKL)
                        if s == 2:
                            low_keys(turn + 1, (b + 1) % 2)

                turns(pool, body)

            @block.tensor
            def _(pe):
                pe.wait_ge(cstaged, 1)
                for b in range(BATCH):
                    last = pe.transpose(ps[:, 2, b * KEYS:(b + 1) * KEYS], cstage[:, b, :], c.ident[0:KEYS, 0:KEYS])
                last.then_inc(cturned, 1)
                norm.tensor(pe)
                norm.wait_parts(pe, 1)
                pe.wait_ge(ctx_ready, 1)
                pe.wait_ge(filled, 1)

                def use_side(kind, at, turn, b, p):
                    side, uses = side_of(at)
                    if not isinstance(at, int) or at >= uses:
                        pe.wait_ge(side_read, at - uses + 1)
                    tokens, context = norm.parts(b * SEQ, (b + 1) * SEQ), keysT[:, b, SEQ:NK]
                    if kind == KL:
                        last = split_product(pe, side, (wk_high[:], wk_low[:]), tokens)
                    elif kind == KC:
                        last = pe.matmul(side[:, 0:KEYS], wk[:], context, start=True, stop=True)
                    elif kind == Q:
                        last = split_product(pe, side, (wq_high[:], wq_low[:]), tokens)
                    elif kind == NKL:
                        pe.wait_ge(squared, squares(turn, KL))
                        last = pe.matmul(side, c.pairsum[:], ksq[:, 0:SEQ], start=True, stop=True)
                    elif kind == NORMS:
                        pe.wait_ge(squared, squares(turn, Q))
                        pe.matmul(side[:, 0:KEYS], c.pairsum[:], ksq[:, SEQ:NK], start=True, stop=True)
                        for t in range(TPB):
                            last = pe.matmul(side[:, P + 2 * t:P + 2 * t + 2], qsq[:, t * P:(t + 1) * P], c.pairsum[:, 0:P:D], start=True, stop=True)
                    elif kind == Y:
                        pe.wait_ge(mixed_ready, turn + 2)
                        for t in range(TPB):
                            last = pe.matmul(side[:, t * P:(t + 1) * P], mixedT[:, t * P:(t + 1) * P], wo[:, bass.ds(p, 1)].rearrange("p j d -> p (j d)"),
                                             start=True, stop=True)
                    else:
                        wv = w_all[:, bass.ds(p, 1), 2].rearrange("p j f -> p (j f)")
                        for k in range(KB - 1) if kind == V4 else [KB - 1]:
                            last = pe.matmul(side[0:BK, k % 4 * P:(k % 4 + 1) * P], keysT[:, b, k * BK:(k + 1) * BK], wv, start=True, stop=True)
                    last.then_inc(side_done, 1)

                def scores(turn, s, w):
                    if s == 0:
                        pe.wait_ge(k_ready, scalings(turn, NORMS))
                        pe.wait_ge(k_parted, turn + 1)
                    if s < 2:
                        pe.wait_ge(q_parted, turn * 2 + s + 1)
                    at = slice(s // 2 * P, (s // 2 + 1) * P)
                    for i in range(2):
                        half = slice(i * KH, (i + 1) * KH)
                        last = split_product(pe, S[s % 2][:, i], (q2_high[:, w, s % 2, at], q2_low[:, w, s % 2, at]), (kT_high[:, w, half], kT_low[:, w, half]))
                    last.then_inc(scored, 1)

                def turn_step(now, s):
                    pe.wait_ge(normed, now + 1)
                    pe.wait_ge(turn_read, now + 1)
                    for k in range(KB):
                        last = pe.transpose(PT[:, k * P:(k + 1) * P], prob[:, s % RING, k * BK:(k + 1) * BK], c.ident[:])
                    last.then_inc(turned, 1)

                def product(now, t, w):
                    pe.wait_ge(turn_read, now + 1)
                    for k in range(KB):
                        for h in range(2):
                            last = pe.matmul(O[h * D:(h + 1) * D, t * P:(t + 1) * P], v[:, w, k, h * D:(h + 1) * D], probT[:, (2 * t + h) % RING, k, :],
                                             start=(k == 0), stop=(k == KB - 1))
                    if t == TPB - 1:
                        last.then_inc(mix_done, 1)

                pe.wait_ge(w_ready, 2)
                for at, (kind, turn) in enumerate(PROLOGUE):
                    if kind == V4:
                        pe.wait_ge(tokens_in, 1)
                    use_side(kind, at, turn, turn, 0)
                norm.wait_parts(pe)
                pe.wait_ge(tokens_in, BATCH)
                for s in range(AHEAD):
                    if s == 2:
                        pe.wait_ge(exped, 1)
                    scores(0, s, 0)
                pe.wait_ge(turn_read, 1)
                pe.matmul(O, probT[:, 0, 0, :], probT[:, 0, 0:4].rearrange("k b t -> k (b t)"), start=True, stop=True)

                def body(p, b, turn):
                    w = b % 2
                    for s in range(STEPS):
                        now = turn * STEPS + s
                        turn_step(now, s)
                        to = s + AHEAD
                        pe.wait_ge(exped, now + AHEAD - 1)
                        scores(turn + to // STEPS, to % STEPS, (b + to // STEPS) % 2)
                        if s == 0:
                            product(now, TPB - 1, 1 - w)
                        elif s % 2 == 0:
                            if s == 2:
                                pe.wait_ge(mixed_ready, turn + 1)
                                pe.wait_ge(side_read, use_of(turn, V1) - STEPS + 1)
                            product(now, s // 2 - 1, w)
                        kind = s
                        if kind == KL and b == 2:
                            pe.wait_ge(w_ready, p * 2 + 3)
                        if kind == Q and b == 3:
                            pe.wait_ge(w_ready, p * 2 + 4)
                        pair = p + (b + FOR[kind]) // BATCH
                        use_side(kind, use_of(turn, s), turn + FOR[kind], batch_of(b, kind), pair + 1 if kind == Y else pair)

                turns(pe, body)
                product(TURNS * STEPS, TPB - 1, 1)
                use_side(Y, use_of(TURNS, 0), TURNS - 1, BATCH - 1, PAIRS)

            @block.scalar
            def _(act):
                act.wait_ge(cvar_ready, 1)
                act.activation(cwork[:, 4, :], cwork[:, 3, :], ACT.Sqrt).then_inc(cstd_ready, 1)
                act.wait_ge(cturned, 1)
                act.activation(keysT[:, :, SEQ:NK], ps[:, 2, 0:BATCH * KEYS].rearrange("p (b k) -> p b k", b=BATCH), ACT.Identity,
                               bias=c.vec("L1_xb"), scale=c.vec("L1_xg")).then_inc(ctx_ready, 1)
                norm.scalar(act)
                act.preload_act_table_set("natural_log_exp_and_others")
                step = InOrder(act, act_order)

                def square(kind, at, turn, w):
                    if kind == Q:
                        act.wait_ge(side_done, at + 1)
                        act.activation(qsq[:], side_of(at)[0], ACT.Square).then_inc(squared, 1)
                    else:
                        act.wait_ge(side_read, at + 1)
                        a, e = (0, SEQ) if kind == KL else (SEQ, NK)
                        act.activation(ksq[:, a:e], kT[:, w, a:e], ACT.Square).then_inc(squared, 1)

                def high_queries(turn, w, h, use):
                    act.wait_ge(side_read, use + 1)
                    rows = slice(h * D, (h + 1) * D)
                    act.activation(q2_high[rows, w, h], q_raw[rows], ACT.Copy).then_inc(q_high_ready, 1)

                def invert(kind, at, w, base):
                    act.wait_ge(side_read, at + 1)
                    if kind == NKL:
                        step(act.activation(kinv[:, 0:SEQ], kinv[:, 0:SEQ], ACT.Ln), base)
                        act.activation(kinv[:, 0:SEQ], kinv[:, 0:SEQ], ACT.Exp, scale=-0.5).then_inc(kinv_ready, 1)
                    else:
                        act.activation(kinv[:, SEQ:NK], kinv[:, SEQ:NK], ACT.Ln)
                        step(act.activation(qms[:], qms[:], ACT.Ln), base)
                        act.activation(kinv[:, SEQ:NK], kinv[:, SEQ:NK], ACT.Exp, scale=-0.5).then_inc(kinv_ready, 1)
                        act.activation(qinv[:, w, :], qms[:], ACT.Exp, scale=-0.5).then_inc(qinv_ready, 1)

                def exps(now, s, w):
                    i = s % RING
                    act.wait_ge(bounded, now + 1)
                    act.activation(prob[:, i].rearrange("p (a k) -> p a k", a=2), S[s % 2], ACT.Exp, bias=low[:, i:i + 1], scale=qinv[:, w, s:s + 1],
                                   accum_out=sums[:, i:i + 1]).then_inc(exped, 1)

                def mixed(turn):
                    act.wait_ge(mix_done, turn + 1)
                    act.activation(mixedT[:], O, ACT.Copy).then_inc(mixed_ready, 1)

                act.wait_ge(filled, 1)
                for at, (kind, turn) in enumerate(PROLOGUE[:-1]):
                    if kind in (KL, KC, Q):
                        square(kind, at, turn, turn)
                    if kind in (NKL, NORMS):
                        invert(kind, at, turn, 0)
                    if kind == Q:
                        for h in range(2):
                            high_queries(turn, turn, h, at)
                for s in range(AHEAD - 1):
                    exps(s, s, 0)
                first, LINKS = step.n, 2

                def body(p, b, turn):
                    step.n = first
                    for s in range(STEPS):
                        at = use_of(turn, s) - 1
                        if s == Q + 1:
                            square(Q, at, turn + 1, None)
                        act.wait_ge(turned, turn * STEPS + s + 1)
                        act.activation(probT[:, s % RING].rearrange("k b t -> k (b t)"), PT[:, 0:KB * P], ACT.Copy).then_inc(turn_read, 1)
                        to = s + AHEAD - 1
                        exps(turn * STEPS + to, to % STEPS, (b + to // STEPS) % 2)
                        if s in (1, 2):
                            high_queries(turn + 1, (b + 1) % 2, s - 1, use_of(turn, Q))
                        if s == 1:
                            mixed(turn)
                        if s == (NKL + 1) % STEPS:
                            invert(NKL, at, None, turn * LINKS)
                        if s == NORMS + 1:
                            invert(NORMS, at, (b + 1) % 2, turn * LINKS)
                        if s in (KL + 1, KC + 1):
                            square(s - 1, at, turn + 2, b % 2)

                turns(act, body)
                mixed(TURNS)

            @block.vector
            def _(dve):
                cstep = InOrder(dve, corder)
                dve.wait_ge(ctx_in, 16)
                for b in range(BATCH):
                    last = dve.bn_stats(cstats[:, b, :], cx[:, b, :])
                cstep(last)
                half, gap, spread, var, std, mean = (cwork[:, i, :] for i in range(6))
                dve.tensor_tensor(half, cstats[:, :, 1], cstats[:, :, 4], ALU.add)
                dve.tensor_tensor(spread, cstats[:, :, 2], cstats[:, :, 5], ALU.add)
                cstep(dve.tensor_tensor(gap, cstats[:, :, 1], cstats[:, :, 4], ALU.subtract))
                dve.tensor_scalar(mean, half, 0.5, None, ALU.mult)
                cstep(dve.tensor_tensor(gap, gap, gap, ALU.mult))
                cstep(dve.tensor_scalar(spread, spread, 1.0 / P, NORM_EPS, ALU.mult, ALU.add))
                dve.scalar_tensor_tensor(out=var, in0=gap, scalar=0.25, in1=spread, op0=ALU.mult, op1=ALU.add).then_inc(cvar_ready, 1)
                dve.wait_ge(cstd_ready, 1)
                cstep(dve.reciprocal(half, std))
                for b in range(BATCH):
                    last = dve.tensor_scalar(cstage[:, b, :], cx[:, b, :], mean[:, b:b + 1], half[:, b:b + 1], ALU.subtract, ALU.mult)
                last.then_inc(cstaged, 1)
                norm.vector(dve)
                dve.wait_ge(keep_in, 16)
                dve.tensor_scalar(barred[:, :, 0:KEYS], keep[:], -1.0, 1e30, ALU.add, ALU.mult).then_inc(prepared, 1)
                dve.tensor_tensor(gains[:], c.vec("L1_qg"), c.vec("L1_kg"), ALU.mult).then_inc(prepared, 1)
                dve.wait_ge(prepared, 2)
                dve.tensor_scalar(gains[:], gains[:], D ** -0.5, None, ALU.mult).then_inc(prepared, 1)
                dve.wait_ge(prepared, 3)
                dve.wait_ge(filled, 1)
                step = InOrder(dve, order)

                def bound(turn, s, b, base):
                    w, i = b % 2, s % RING
                    dve.wait_ge(scored, turn * STEPS + s + 1)
                    if s == 0:
                        dve.wait_ge(qinv_ready, turn + 1)
                    masked = S[s % 2][:, 1, SEQ - KH:KH]
                    step(dve.tensor_tensor(masked, masked, barred[:, b, :], ALU.add), base)
                    step(dve.tensor_reduce(top[:, i:i + 1], S[s % 2], AX.XY, ALU.max), base)
                    dve.tensor_scalar(low[:, i:i + 1], top[:, i:i + 1], qinv[:, w, s:s + 1], -1.0, ALU.mult, ALU.mult).then_inc(bounded, 1)

                def invert_sum(now, s):
                    i = s % RING
                    dve.wait_ge(exped, now + 1)
                    dve.reciprocal(rsums[:, i:i + 1], sums[:, i:i + 1]).then_inc(summed, 1)

                def read_side(kind, at, turn, b):
                    w, side = b % 2, side_of(at)[0]
                    dve.wait_ge(side_done, at + 1)
                    if kind == Y:
                        x = c.resid[:, b * TPB:(b + 1) * TPB, :]
                        last = dve.tensor_tensor(x, side.rearrange("p (t d) -> p t d", t=TPB), x, ALU.add)
                    elif kind == KL:
                        last = dve.tensor_copy(kT[:, w, 0:SEQ], side)
                    elif kind == KC:
                        last = dve.tensor_copy(kT[:, w, SEQ:NK], side[:, 0:KEYS])
                    elif kind == Q:
                        dve.wait_ge(squared, squares(turn, Q))
                        last = dve.tensor_scalar(q_raw[:], side, gains[:], None, ALU.mult)
                    elif kind == V4:
                        last = dve.tensor_copy(v[:, w, 0:KB - 1, :].rearrange("k b d -> k (b d)"), side[0:BK, :])
                    elif kind == V1:
                        last = dve.tensor_copy(v[:, w, KB - 1, :], side[0:BK, 0:P])
                    elif kind == NKL:
                        last = dve.tensor_scalar(kinv[:, 0:SEQ], side, 1.0 / D, 1e-16, ALU.mult, ALU.max)
                    else:
                        dve.tensor_scalar(kinv[:, SEQ:NK], side[:, 0:KEYS], 1.0 / D, 1e-16, ALU.mult, ALU.max)
                        last = dve.tensor_scalar(qms[:], side[:, P:P + STEPS], 1.0 / D, 1e-16, ALU.mult, ALU.max)
                    last.then_inc(side_read, 1)

                def high_keys(turn, w):
                    dve.wait_ge(k_ready, scalings(turn, NKL))
                    dve.tensor_copy(kT_high[:, w, 0:SEQ], kT[:, w, 0:SEQ]).then_inc(k_high_ready, 1)

                def low_queries(turn, w, h):
                    rows = slice(h * D, (h + 1) * D)
                    dve.wait_ge(q_high_ready, turn * 2 + h + 1)
                    dve.tensor_tensor(q2_low[rows, w, h], q_raw[rows], q2_high[rows, w, h], ALU.subtract).then_inc(q_parted, 1)

                for at, (kind, turn) in enumerate(PROLOGUE[:-1]):
                    read_side(kind, at, turn, turn)
                    if kind == Q:
                        for h in range(2):
                            low_queries(0, 0, h)
                    if (kind, turn) == (NORMS, 0):
                        high_keys(0, 0)
                for s in range(AHEAD):
                    if s > 0:
                        invert_sum(s - 1, s - 1)
                    bound(0, s, 0, 0)
                first, LINKS = step.n, 2 * STEPS
                dve.wait_ge(bias_added, 1)

                def body(p, b, turn):
                    step.n = first
                    for s in range(STEPS):
                        kind = (s - 1) % STEPS
                        ahead = FOR[kind] - (s == 0)
                        read_side(kind, use_of(turn, s) - 1, turn + ahead, (b + ahead) % BATCH)
                        to = s + AHEAD - 1
                        invert_sum(turn * STEPS + to, to)
                        to = s + AHEAD
                        bound(turn + to // STEPS, to % STEPS, (b + to // STEPS) % BATCH, turn * LINKS)
                        if s == 2:
                            high_keys(turn + 1, (b + 1) % 2)
                        if s in (2, 3):
                            low_queries(turn + 1, (b + 1) % 2, s - 2)

                turns(dve, body)
                read_side(NKL, use_of(TURNS, 0) - 1, TURNS + 1, 1)
                read_side(Y, use_of(TURNS, 0), TURNS - 1, BATCH - 1)
                dve.wait_ge(side_read, use_of(TURNS, 0) + 1)


def mixture_addressed(c):
    nc, ps, tag = c.nc, c.ps, "L2f"
    L, HID, ADDR, K = 12, 512, 64, 3
    FB = HID // P
    TRIO, TRIOS = 3, L // 3
    BANKS = 4
    TURN = 4
    with ExitStack() as ctx:
        norm = Norm(c, ctx, tag, banks=6, split=True)
        pw, um = c.sb(ctx, "L2f_pw", [P, ADDR]), c.sb(ctx, "L2f_u", [ADDR, 3 * L])
        addr = c.sb(ctx, "L2f_addr", [ADDR, TILES * P])
        weightT = addr[0:L]
        rows = c.sb(ctx, "L2f_rows", [P, 3, TILES, L])
        weight = c.sb(ctx, "L2f_weight", [P, 3, TILES, L])
        LATER = 2 * TILES
        top, later_top = TopK(c, ctx, "L2f", L, K), TopK(c, ctx, "L2f_later", L, K, LATER)
        soft, later_soft = Softmax(c, ctx, "L2f", K), Softmax(c, ctx, "L2f_later", K, LATER)
        w1, w2 = c.sb(ctx, "L2f_w1", [P, HALVES, HID]), c.sb(ctx, "L2f_w2", [P, FB, TRIO * P])
        w1_high, w1_low = (c.sb(ctx, f"L2f_w1_{n}", [P, HALVES, HID], F32R) for n in ("high", "low"))
        w2_high, w2_low = (c.sb(ctx, f"L2f_w2_{n}", [P, HALVES, FB, TRIO * P], F32R) for n in ("high", "low"))
        hidT_high, hidT_low = (c.sb(ctx, f"L2f_hidT_{n}", [P, FB, TILES * P], F32R) for n in ("high", "low"))
        hid = c.sb(ctx, "L2f_hid", [P, TILES, HID])
        b2 = c.sb(ctx, "L2f_b2", [L, P])
        small_in, w1_in, w2_in = c.sem("L2f_small_in"), c.pair("L2f_w1_in"), c.sem("L2f_w2_in")
        addr_done, addr_ready, scored, order = (c.sem(f"L2f_{n}") for n in ("addr_done", "addr_ready", "scored", "order"))
        cleared, first_done, second_done = c.sem("L2f_cleared"), c.sem("L2f_first_done"), c.sem("L2f_second_done")
        first_added = [c.sem(f"L2f_first_added{i}") for i in range(BANKS)]
        second_added = [c.sem(f"L2f_second_added{i}") for i in range(BANKS)]
        gelu_ready, turned, turn_read = (c.sem(f"L2f_{n}") for n in ("gelu_ready", "hid_turned", "turn_read"))
        w1_parted, w2_parted, part_order, high_ready = (c.sem(f"L2f_{n}") for n in ("w1_parted", "w2_parted", "part_order", "high_ready"))
        third_ready, wT_done, wT_ready, b2_done, b2_added = (c.sem(f"L2f_{n}") for n in ("third_ready", "wT_done", "wT_ready", "b2_done", "b2_added"))
        LAG = 3
        turn_weights = {n: n // TPB for n in range(0, TILES, TPB)}
        multiply_biases = {n + 2: n // TPB for n in range(0, TILES, TPB)}
        SIDE = 6

        def turned_block(n):
            return ps[:, TURN + n % 2, :].rearrange("p (f t) -> p f t", f=FB)

        with nc.Block() as block:
            @block.sync
            def _(sp):
                for sb, name in ((pw, "L2f_pw"), (um, "L2f_u"), (b2, "L2f_b2")):
                    sp.dma_start(sb[:], c.dram[name]).then_inc(small_in, 16)

                def load1(e, u):
                    sp.dma_start(w1[:, u, :], c.dram["L2f_w1"][bass.ds(e, 1)].rearrange("e d f -> (e d) f")).then_inc(w1_in[u], 16)

                def load2(g):
                    sp.dma_start(w2[:], c.dram["L2f_w2"][bass.ds(g, 1)].rearrange("g p f e d -> (g p) f (e d)")).then_inc(w2_in, 16)

                for u in range(HALVES):
                    load1(u, u)
                load2(0)
                with sp.Fori(1, L // HALVES) as q:
                    for u in range(HALVES):
                        sp.wait_ge(first_done, (q * HALVES + u - 1) * TILES)
                        load1(q * HALVES + u, u)
                with sp.Fori(1, TRIOS) as g:
                    sp.wait_ge(w2_parted, g)
                    load2(g)

            @block.gpsimd
            def _(pool):
                pool.memset(hid[:], 0.0).then_inc(cleared, 1)
                with pool.Fori(0, L // HALVES) as q:
                    for u in range(HALVES):
                        pool.wait_ge(w1_in[u], q * 16 + 16)
                        pool.tensor_tensor(w1_high[:, u, :], w1[:, u, :], c.one[:].broadcast_to([P, HID]), ALU.mult).then_inc(part_order, 1)
                        pool.wait_ge(part_order, q * HALVES + u + 1)
                        pool.tensor_tensor(w1_low[:, u, :], w1[:, u, :], w1_high[:, u, :], ALU.subtract).then_inc(w1_parted, 1)
                for g in range(TRIOS):
                    u = g % HALVES
                    pool.wait_ge(w2_in, g * 16 + 16)
                    if g >= HALVES:
                        pool.wait_ge(second_done, (g - 1) * TILES)
                    pool.tensor_tensor(w2_high[:, u], w2[:], bcast(c.one[:], [FB, None]).broadcast_to([P, FB, TRIO * P]), ALU.mult).then_inc(part_order, 1)
                    pool.wait_ge(part_order, L + g + 1)
                    pool.tensor_tensor(w2_low[:, u], w2[:], w2_high[:, u], ALU.subtract).then_inc(w2_parted, 1)

            @block.tensor
            def _(pe):
                norm.tensor(pe)
                pe.wait_ge(small_in, 48)
                for b in range(BATCH):
                    norm.wait(pe, b)
                    pe.matmul(ps[0:ADDR, 2 + b, :], pw[:], c.normT[:, b * SEQ:(b + 1) * SEQ], start=True, stop=True).then_inc(addr_done, 1)
                for n in range(TILES):
                    pe.wait_ge(addr_ready, n // TPB + 1)
                    last = pe.matmul(ps[:, 6 + n // 8, n % 8 * 64:n % 8 * 64 + 3 * L], addr[:, n * P:(n + 1) * P], um[:], start=True, stop=True)
                last.then_inc(scored, 1)
                norm.wait_parts(pe)

                def first(e, u, n):
                    pe.wait_ge(first_added[n % BANKS], e * (TILES // BANKS) + n // BANKS + 1)
                    split_product(pe, ps[:, n % BANKS, :], norm.parts(n * P, (n + 1) * P), (w1_high[:, u, :], w1_low[:, u, :])).then_inc(first_done, 1)

                def turn(n):
                    pe.wait_ge(gelu_ready, n + 1)
                    if n >= 2:
                        pe.wait_ge(turn_read, n - 1)
                    for f in range(FB):
                        last = pe.transpose(ps[:, TURN + n % 2, f * P:(f + 1) * P], hid[:, n, f * P:(f + 1) * P], c.ident[:])
                    last.then_inc(turned, 1)

                with pe.Fori(0, L // HALVES - 1) as q:
                    for u in range(HALVES):
                        pe.wait_ge(w1_parted, q * HALVES + u + 1)
                        for n in range(TILES):
                            first(q * HALVES + u, u, n)
                pe.wait_ge(third_ready, 1)
                pe.wait_ge(w1_parted, L - 1)
                for n in range(TILES):
                    if n in turn_weights:
                        b = turn_weights[n]
                        if b >= 2:
                            pe.wait_ge(wT_ready, b - 1)
                        for t in range(TPB):
                            last = pe.transpose(ps[0:L, SIDE + b % 2, t * P:(t + 1) * P], weight[:, 2, b * TPB + t, :], c.ident[:])
                        last.then_inc(wT_done, 1)
                    first(L - 2, 0, n)
                pe.wait_ge(w1_parted, L)
                for n in range(TILES):
                    if n in multiply_biases:
                        b = multiply_biases[n]
                        pe.wait_ge(wT_ready, BATCH)
                        if b >= 2:
                            pe.wait_ge(b2_added, b - 1)
                        for t in range(TPB):
                            last = pe.matmul(ps[:, SIDE + b % 2, t * P:(t + 1) * P], weightT[:, (b * TPB + t) * P:(b * TPB + t + 1) * P], b2[:], start=True, stop=True)
                        last.then_inc(b2_done, 1)
                    first(L - 1, 1, n)
                    if n >= LAG:
                        turn(n - LAG)
                for n in range(TILES - LAG, TILES):
                    turn(n)
                pe.wait_ge(turn_read, TILES)
                with pe.Fori(0, TRIOS // HALVES) as q:
                    for u in range(HALVES):
                        pe.wait_ge(w2_parted, q * HALVES + u + 1)
                        for n in range(TILES):
                            pe.wait_ge(second_added[n % BANKS], (q * HALVES + u) * (TILES // BANKS) + n // BANKS + 1)
                            for f in range(FB):
                                at = slice(n * P, (n + 1) * P)
                                last = split_product(pe, ps[:, n % BANKS, 0:TRIO * P], (hidT_high[:, f, at], hidT_low[:, f, at]),
                                                     (w2_high[:, u, f, :], w2_low[:, u, f, :]), start=(f == 0), stop=(f == FB - 1))
                            last.then_inc(second_done, 1)

            @block.scalar
            def _(act):
                norm.scalar(act)
                for b in range(BATCH):
                    act.wait_ge(addr_done, b + 1)
                    act.activation(addr[:, b * SEQ:(b + 1) * SEQ], ps[0:ADDR, 2 + b, :], ACT.Copy).then_inc(addr_ready, 1)
                soft.scalar(act)
                later_soft.scalar(act)
                for b in range(BATCH):
                    act.wait_ge(wT_done, b + 1)
                    act.activation(weightT[:, b * SEQ:(b + 1) * SEQ], ps[0:L, SIDE + b % 2, :], ACT.Copy).then_inc(wT_ready, 1)

                def take_high(n):
                    act.wait_ge(turned, n + 1)
                    act.activation(hidT_high[:, :, n * P:(n + 1) * P], turned_block(n), ACT.Copy).then_inc(high_ready, 1)

                for n in range(TILES):
                    act.wait_ge(first_added[n % BANKS], (L - 1) * (TILES // BANKS) + n // BANKS + 2)
                    act.activation(hid[:, n, :], hid[:, n, :], ACT.Gelu).then_inc(gelu_ready, 1)
                    if n >= 2:
                        take_high(n - 2)
                for n in range(TILES - 2, TILES):
                    take_high(n)

            @block.vector
            def _(dve):
                norm.vector(dve)
                step = InOrder(dve, order)
                for i in range(BANKS):
                    dve.engine_nop().then_inc(first_added[i], 1)
                dve.wait_ge(scored, 1)
                for r in range(3):
                    last = dve.tensor_copy(rows[:, r].rearrange("p (a n) e -> p a n e", a=2),
                                           ps[:, 6:8, :].rearrange("p a (n w) -> p a n w", n=8)[:, :, :, r * L:(r + 1) * L])
                step(last)

                def add_first(e, n):
                    dve.wait_ge(first_done, e * TILES + n + 1)
                    dve.wait_ge(first_added[n % BANKS], e * (TILES // BANKS) + n // BANKS + 1)
                    dve.scalar_tensor_tensor(out=hid[:, n, :], in0=ps[:, n % BANKS, :], scalar=flat[:, bass.ds(n * L + e, 1)], in1=hid[:, n, :],
                                             op0=ALU.mult, op1=ALU.add).then_inc(first_added[n % BANKS], 1)

                def take_turned(n):
                    dve.wait_ge(high_ready, n + 1)
                    at = slice(n * P, (n + 1) * P)
                    dve.tensor_tensor(hidT_low[:, :, at], turned_block(n), hidT_high[:, :, at], ALU.subtract).then_inc(turn_read, 1)

                flat = weight[:].rearrange("p r n e -> p (r n e)")
                top.find(dve, step, rows[:, 0])
                soft.vector(dve, step, top.top[:, :, 0:K], top.top[:, :, 0])
                top.spread(dve, step, soft.exps[:], weight[:, 0])
                dve.wait_ge(cleared, 1)
                later_rows = rows[:, 1:3].rearrange("p r n e -> p (r n) e")

                def lead(n):
                    for i in range(2):
                        last = later_top.lead(dve, later_rows, 2 * n + i)
                    if n == TILES - 1:
                        step(last)

                def locate(n):
                    for i in range(2):
                        last = later_top.locate(dve, later_rows, 2 * n + i)
                    if n == TILES - 1:
                        step(last)

                def weights(n):
                    if n == 0:
                        later_top.number(dve, step)
                        later_soft.shift(dve, later_top.top[:, :, 0:K], later_top.top[:, :, 0])
                    if n == 3:
                        later_top.mark(dve, step)
                    if n == 6:
                        later_soft.divide(dve, step)
                    if n == 9:
                        later_top.weigh(dve, step, later_soft.exps[:])
                    if n == 12:
                        later_top.collect(dve, step, weight[:, 1:3].rearrange("p r n e -> p (r n) e"))

                for e, route in enumerate((lead, locate, weights, lambda n: None)):
                    for n in range(TILES):
                        add_first(e, n)
                        route(n)
                dve.engine_nop().then_inc(third_ready, 1)
                with dve.Fori(2, L // HALVES - 1) as q:
                    for u in range(HALVES):
                        for n in range(TILES):
                            add_first(q * HALVES + u, n)
                for n in range(TILES):
                    add_first(L - 2, n)
                for n in range(TILES):
                    if n in multiply_biases:
                        b = multiply_biases[n]
                        dve.wait_ge(b2_done, b + 1)
                        x = c.resid[:, b * TPB:(b + 1) * TPB, :]
                        dve.tensor_tensor(x, ps[:, SIDE + b % 2, :].rearrange("p (t d) -> p t d", t=TPB), x, ALU.add).then_inc(b2_added, 1)
                    add_first(L - 1, n)
                    if n >= LAG:
                        take_turned(n - LAG)
                for n in range(TILES - LAG, TILES):
                    take_turned(n)
                for i in range(BANKS):
                    dve.engine_nop().then_inc(second_added[i], 1)
                dve.wait_ge(b2_added, BATCH)
                with dve.Fori(0, TRIOS // HALVES) as q:
                    for u in range(HALVES):
                        g = q * HALVES + u
                        for n in range(TILES):
                            dve.wait_ge(second_done, g * TILES + n + 1)
                            dve.wait_ge(second_added[n % BANKS], g * (TILES // BANKS) + n // BANKS + 1)
                            for i in range(TRIO):
                                ins = dve.scalar_tensor_tensor(out=c.resid[:, n, :], in0=ps[:, n % BANKS, i * P:(i + 1) * P],
                                                               scalar=flat[:, bass.ds(TILES * L + n * L + g * TRIO + i, 1)], in1=c.resid[:, n, :],
                                                               op0=ALU.mult, op1=ALU.add)
                                if i < TRIO - 1:
                                    ins.then_inc(order, 1)
                                    dve.wait_ge(order, step.n + (g * TILES + n) * (TRIO - 1) + i + 1)
                            ins.then_inc(second_added[n % BANKS], 1)
                for i in range(BANKS):
                    dve.wait_ge(second_added[i], TRIOS * (TILES // BANKS) + 1)


def program(nc, dram, out, layers=(0, 8)):
    with ExitStack() as ctx:
        c = Core(nc, ctx, dram, layers)
        constants(c)
        steps = [
            lambda: cross_attention(c, "L0", 16, 8, 8 ** -0.5, None),
            lambda: experts(c, "L0f", TopTwo, "relu", P, 4, inner_eps=1e-6),
            lambda: latent_attention(c),
            lambda: experts(c, "L1f", Sampled, "swiglu", 112, 3),
            lambda: cross_attention(c, "L2", 16, 8, 8 ** -0.5, "scaled"),
            lambda: mixture_addressed(c),
            lambda: cross_attention(c, "L3", 8, 64, 64 ** -0.5, "barred", inner_eps=1e-5, gain=c.vec("L3_g"), shift=c.vec("L3_b")),
            lambda: experts(c, "L3f", TopProbs, "gelu", P, 2),
        ]
        for step in steps[layers[0]:layers[1]]:
            taken = nc.snapshot_sems()
            step()
            c.retire(taken)
        stored = c.sem("stored")
        with nc.Block() as block:
            @block.sync
            def _(sp):
                sp.dma_start(out, c.resid[:]).then_inc(stored, 16)
                sp.wait_ge(stored, 16)


def laid_out(i):
    import numpy as np
    a = {k: np.asarray(v) for k, v in i.items()}
    cols = lambda v: v.reshape(-1, P).T
    twice = lambda v: np.tile(v, 2)[:, None]
    b1 = np.zeros((P, 1), np.float32)
    b1[:50, 0] = a["L1_ffn_actor_b1"]
    vecs = {
        "L0_bq": cols(a["L0_xattn_bq"]), "L0_bk": cols(a["L0_xattn_bk"]), "L2_bq": cols(a["L2_xattn_bq"]), "L2_bk": cols(a["L2_xattn_bk"]),
        "L1_xg": cols(a["L1_xattn_ln_x_g"]), "L1_xb": cols(a["L1_xattn_ln_x_b"]), "L1_lg": cols(a["L1_xattn_ln_l_g"]), "L1_lb": cols(a["L1_xattn_ln_l_b"]),
        "L1_qg": twice(a["L1_xattn_qn_g"]), "L1_kg": twice(a["L1_xattn_kn_g"]), "L1f_b1": b1,
        "L3_g": cols(a["L3_xattn_ln_gamma"]), "L3_b": cols(a["L3_xattn_ln_beta"]),
    }
    rows = np.zeros((len(ROWS), P), np.float32)
    for n, k in enumerate(["L0_xattn_bv", "L0_xattn_bo", "L1_xattn_bout", "L2_xattn_bv", "L2_xattn_bo", "L3_ffn_router_b", "L1_ffn_actor_b2"]):
        rows[n, :a[k].size] = a[k]
    E = 8
    packed = lambda w, b, *more: np.concatenate([w, b.reshape(len(b), -1, P).transpose(0, 2, 1), *(m[:, :, None] for m in more)], 2)
    both = lambda n: np.concatenate([a[f"L3_ffn_s{n}"][None], a[f"L3_ffn_r{n}"]])
    ctx = a["ctx_1024"]
    got = {
        "x": a["x"].reshape(TILES, P, P).transpose(1, 0, 2),
        "vecs": np.concatenate([vecs[k] for k in VECS], 1),
        "rows": np.broadcast_to(rows, (P, *rows.shape)),
        "ctxT": ctx.transpose(2, 0, 1),
        "ctx": ctx.transpose(1, 0, 2),
        **{f"L0_w{n}": a[f"L0_xattn_W{n}"].T for n in "qkv"}, "L0_wo": a["L0_xattn_Wo"].T[:, None],
        **{f"L2_w{n}": a[f"L2_xattn_w{n}"].T for n in "qkv"}, "L2_wo": a["L2_xattn_wo"].T[:, None],
        "L2_mask": a["mask_Bx1xSxS2_fk1"].reshape(TILES, P, KEYS).transpose(1, 0, 2),
        "keep_L1": np.broadcast_to(a["mask_BxS2_bf1"], (P, BATCH, KEYS)),
        "L3_mask": np.broadcast_to(a["mask_BxS2_bk0"], (P, BATCH, KEYS)),
        "L0f_wg": a["L0_ffn_Wg"], "L0f_w1": packed(a["L0_ffn_W1"], a["L0_ffn_b1"], a["L0_ffn_gamma"], a["L0_ffn_beta"]), "L0f_b2": a["L0_ffn_b2"],
        "L0f_w2": a["L0_ffn_W2"].reshape(E, 4, P, P).transpose(0, 2, 1, 3),
        "L1_w": np.stack([a["L1_xattn_Wq"].reshape(P, 8, P), a["L1_xattn_Wkv"][:, :1024].reshape(P, 8, P), a["L1_xattn_Wkv"][:, 1024:].reshape(P, 8, P)], 2).transpose(1, 0, 2, 3),
        "L1_wo": a["L1_xattn_Wout"].reshape(8, P, P),
        "L1f_wr": a["L1_ffn_router_w"].T, "L1f_a1": a["L1_ffn_actor_w1"].T, "L1f_a2": a["L1_ffn_actor_w2"].T,
        "L1f_gu": np.stack([a["L1_ffn_gate_w"].transpose(0, 2, 1), a["L1_ffn_up_w"].transpose(0, 2, 1)], 2),
        "L1f_dn": a["L1_ffn_down_w"].transpose(0, 2, 1).reshape(E, 3, 112, P).transpose(0, 2, 1, 3),
        "L2f_pw": a["L2_ffn_P_w"].T, "L2f_u": np.concatenate([a[f"L2_ffn_U{n}"] for n in (1, 2, 3)]).T,
        "L2f_w1": a["L2_ffn_W1"].transpose(0, 2, 1),
        "L2f_w2": a["L2_ffn_W2"].reshape(4, 3, P, 4, P).transpose(0, 4, 3, 1, 2),
        "L2f_b2": a["L2_ffn_b2"],
        "L3_wq": a["L3_xattn_Wq"], "L3_wk": a["L3_xattn_Wkv"][:, :512], "L3_wv": a["L3_xattn_Wkv"][:, 512:], "L3_wo": a["L3_xattn_Wout"].reshape(4, P, P).transpose(1, 0, 2),
        "L3f_wr": a["L3_ffn_router_w"], "L3f_b2": both("b2"), "L3f_w1": packed(both("w1"), both("b1")),
        "L3f_w2": both("w2").reshape(9, 2, P, P).transpose(0, 2, 1, 3),
    }
    return {k: np.ascontiguousarray(v) for k, v in got.items()}


def kernel(**inputs):
    import concourse.bacc as bacc
    from concourse.bass_utils import run_bass_kernel_spmd

    arrays = laid_out(inputs)
    nc = bacc.Bacc("TRN2", target_bir_lowering=False, num_devices=1)
    dram = {k: nc.dram_tensor(k, v.shape, mybir.dt.from_np(v.dtype), kind="ExternalInput").ap() for k, v in arrays.items()}
    out = nc.dram_tensor("out", (P, TILES, P), F32, kind="ExternalOutput").ap()
    program(nc, dram, out)
    done = run_bass_kernel_spmd(nc, [arrays], core_ids=[0])
    return done.results[0]["out"].transpose(1, 0, 2).reshape(BATCH, SEQ, P)
```
